# Optimizing a Trainium2 kernel written in Bass

```python
import numpy as np
import jax
import jax.numpy as jnp

def _softmax(x, axis=-1):
    return jax.nn.softmax(x, axis=axis)

def _gelu(x):
    return jax.nn.gelu(x, approximate=True)

def _silu(x):
    return jax.nn.silu(x)

def _sigmoid(x):
    return jax.nn.sigmoid(x)

def _layernorm(x, axis=-1, eps=1e-05):
    m = jnp.mean(x, axis=axis, keepdims=True)
    v = jnp.var(x, axis=axis, keepdims=True)
    return (x - m) / jnp.sqrt(v + eps)

def _scatter_add(tgt, idx, src, axis=0):
    return tgt.at[idx].add(src)

def _segment_sum(src, seg, n):
    return jax.ops.segment_sum(src, seg, n)
kernel_name = 'mk_gps_d1_gnn_r64_a9009f'

def setup_inputs(seed: int=0):
    np.random.seed(seed)
    _w = jnp.asarray

    def _rec_inputs():
        import jax
        import jax.numpy as jnp
        _gk = jax.random.key(seed)
        x = -0.000125 + 0.9999 * jax.random.normal(jax.random.fold_in(_gk, 1), (1024, 512), jnp.float32)
        _s = jax.random.randint(jax.random.fold_in(_gk, 2), (8192,), 0, 1024, jnp.int32)
        _d = jax.random.randint(jax.random.fold_in(_gk, 3), (8192,), 0, 1024, jnp.int32)
        _loop = jnp.arange(1024, dtype=jnp.int32)
        src = jnp.concatenate([_s, _d, _loop])
        dst = jnp.concatenate([_d, _s, _loop])
        _o = jnp.argsort(dst, stable=True)
        src = src[_o]
        dst = dst[_o]
        return (x, src, dst)
    x, src, dst = _rec_inputs()

    def _L0_gnn_setup():
        import jax, jax.numpy as jnp
        import numpy as np
        N = 1024
        F = 512
        H = 512
        E = 8192
        key = jax.random.key(seed)
        ks = jax.random.split(key, 12)
        s = 0.02
        return {'x': jax.random.normal(ks[0], (N, F), dtype=jnp.float32), 'edge_index': jax.random.randint(ks[1], (2, E), 0, N, dtype=jnp.int64), 'W_rel1': jax.random.normal(ks[2], (H, F), dtype=jnp.float32) * s, 'b_rel1': jnp.zeros((H,), dtype=jnp.float32), 'W_root1': jax.random.normal(ks[3], (H, F), dtype=jnp.float32) * s, 'W_lin1': jax.random.normal(ks[4], (H, H), dtype=jnp.float32) * s, 'b_lin1': jnp.zeros((H,), dtype=jnp.float32), 'W_rel2': jax.random.normal(ks[5], (H, H), dtype=jnp.float32) * s, 'b_rel2': jnp.zeros((H,), dtype=jnp.float32), 'W_root2': jax.random.normal(ks[6], (H, H), dtype=jnp.float32) * s, 'W_lin2': jax.random.normal(ks[7], (H, H), dtype=jnp.float32) * s, 'b_lin2': jnp.zeros((H,), dtype=jnp.float32)}
    _L0_gnn_all = _L0_gnn_setup()
    _L0_gnn_in = {k: v for k, v in _L0_gnn_all.items() if k in ('W_rel1', 'b_rel1', 'W_root1', 'W_lin1', 'b_lin1', 'W_rel2', 'b_rel2', 'W_root2', 'W_lin2', 'b_lin2')}
    del _L0_gnn_all

    def _L0_mix_setup():
        import jax, jax.numpy as jnp
        import numpy as np
        B, N, D = (2, 128, 512)
        L, H, DH, M = (2, 8, 64, 256)
        EPS_K = 0.0001

        def _layernorm(x, s, b):
            m = x.mean(-1, keepdims=True)
            v = x.var(-1, keepdims=True)
            return (x - m) / jnp.sqrt(v + 1e-05) * s + b

        def _softmax_kernel(x, proj, is_query):
            dh = x.shape[-1]
            data_norm = dh ** (-0.25)
            ratio = proj.shape[0] ** (-0.5)
            dd = jnp.einsum('bhnd,md->bhnm', x * data_norm, proj)
            diag = 0.5 * jnp.sum(x * x, axis=-1) * data_norm ** 2
            if is_query:
                stab = jnp.max(dd, axis=-1, keepdims=True)
            else:
                stab = jnp.max(dd, axis=(-1, -2), keepdims=True)
            return ratio * (jnp.exp(dd - diag[..., None] - stab) + EPS_K)

        def _linear_attention(qp, kp, v):
            k_sum = kp.sum(axis=2)
            d_inv = 1.0 / jnp.einsum('bhnm,bhm->bhn', qp, k_sum)
            ctx = jnp.einsum('bhnm,bhnd->bhmd', kp, v)
            return jnp.einsum('bhnm,bhmd,bhn->bhnd', qp, ctx, d_inv)

        def _performer_forward(x, ln1_s, ln1_b, Wq, bq, Wk, bk, Wv, bv, Wo, bo, proj, ln2_s, ln2_b, W1, b1, W2, b2):
            depth = Wq.shape[0]
            for l in range(depth):
                h = _layernorm(x, ln1_s[l], ln1_b[l])
                b, n, d = h.shape

                def heads(t):
                    return t.reshape(b, n, H, DH).transpose(0, 2, 1, 3)
                q = heads(h @ Wq[l] + bq[l])
                k = heads(h @ Wk[l] + bk[l])
                v = heads(h @ Wv[l] + bv[l])
                qp = _softmax_kernel(q, proj[l], True)
                kp = _softmax_kernel(k, proj[l], False)
                attn = _linear_attention(qp, kp, v)
                attn = attn.transpose(0, 2, 1, 3).reshape(b, n, H * DH)
                x = x + (attn @ Wo[l] + bo[l])
                h2 = _layernorm(x, ln2_s[l], ln2_b[l])
                ff = jax.nn.gelu(h2 @ W1[l] + b1[l]) @ W2[l] + b2[l]
                x = x + ff
            return x
        key = jax.random.key(seed)
        ks = jax.random.split(key, 16)
        s = 0.02
        inp = {'x': jax.random.normal(ks[0], (B, N, D), jnp.float32), 'ln1_s': jnp.ones((L, D), jnp.float32), 'ln1_b': jnp.zeros((L, D), jnp.float32), 'Wq': s * jax.random.normal(ks[1], (L, D, H * DH), jnp.float32), 'bq': jnp.zeros((L, H * DH), jnp.float32), 'Wk': s * jax.random.normal(ks[2], (L, D, H * DH), jnp.float32), 'bk': jnp.zeros((L, H * DH), jnp.float32), 'Wv': s * jax.random.normal(ks[3], (L, D, H * DH), jnp.float32), 'bv': jnp.zeros((L, H * DH), jnp.float32), 'Wo': s * jax.random.normal(ks[4], (L, H * DH, D), jnp.float32), 'bo': jnp.zeros((L, D), jnp.float32), 'proj': jax.random.normal(ks[5], (L, M, DH), jnp.float32), 'ln2_s': jnp.ones((L, D), jnp.float32), 'ln2_b': jnp.zeros((L, D), jnp.float32), 'W1': s * jax.random.normal(ks[6], (L, D, 4 * D), jnp.float32), 'b1': jnp.zeros((L, 4 * D), jnp.float32), 'W2': s * jax.random.normal(ks[7], (L, 4 * D, D), jnp.float32), 'b2': jnp.zeros((L, D), jnp.float32)}
        return inp
    _L0_mix_all = _L0_mix_setup()
    _L0_mix_in = {k: v for k, v in _L0_mix_all.items() if k in ('ln1_s', 'ln1_b', 'Wq', 'bq', 'Wk', 'bk', 'Wv', 'bv', 'Wo', 'bo', 'proj', 'ln2_s', 'ln2_b', 'W1', 'b1', 'W2', 'b2')}
    del _L0_mix_all

    def _L0_ffn_setup():
        import jax, jax.numpy as jnp
        import numpy as np
        K = 2
        EPS = 1e-06

        def _layernorm(x, gamma, beta):
            mu = jnp.mean(x, axis=-1, keepdims=True)
            var = jnp.mean(jnp.square(x - mu), axis=-1, keepdims=True)
            return (x - mu) * jax.lax.rsqrt(var + EPS) * gamma + beta
        key = jax.random.key(seed)
        ks = jax.random.split(key, 5)
        B, S, D, F, E = (8, 32, 512, 32, 8)
        x = jax.random.normal(ks[0], (B, S, D), dtype=jnp.float32)
        router_w = jax.random.normal(ks[1], (D, E), dtype=jnp.float32) * 0.02
        w1 = jax.random.normal(ks[2], (E, D, F), dtype=jnp.float32) * 0.02
        b1 = jnp.zeros((E, F), dtype=jnp.float32)
        w2 = jax.random.normal(ks[3], (E, F, D), dtype=jnp.float32) * 0.02
        b2 = jnp.zeros((E, D), dtype=jnp.float32)
        gamma = jnp.ones((E, D), dtype=jnp.float32)
        beta = jnp.zeros((E, D), dtype=jnp.float32)
        return {'x': x, 'router_w': router_w, 'w1': w1, 'b1': b1, 'w2': w2, 'b2': b2, 'gamma': gamma, 'beta': beta}
    _L0_ffn_all = _L0_ffn_setup()
    _L0_ffn_in = {k: v for k, v in _L0_ffn_all.items() if k in ('router_w', 'w1', 'b1', 'w2', 'b2', 'gamma', 'beta')}
    del _L0_ffn_all
    return {'x': x, 'src': src, 'dst': dst, 'L0_gnn_W_rel1': _L0_gnn_in['W_rel1'], 'L0_gnn_b_rel1': _L0_gnn_in['b_rel1'], 'L0_gnn_W_root1': _L0_gnn_in['W_root1'], 'L0_gnn_W_lin1': _L0_gnn_in['W_lin1'], 'L0_gnn_b_lin1': _L0_gnn_in['b_lin1'], 'L0_gnn_W_rel2': _L0_gnn_in['W_rel2'], 'L0_gnn_b_rel2': _L0_gnn_in['b_rel2'], 'L0_gnn_W_root2': _L0_gnn_in['W_root2'], 'L0_gnn_W_lin2': _L0_gnn_in['W_lin2'], 'L0_gnn_b_lin2': _L0_gnn_in['b_lin2'], 'L0_mix_ln1_s': _L0_mix_in['ln1_s'], 'L0_mix_ln1_b': _L0_mix_in['ln1_b'], 'L0_mix_Wq': _L0_mix_in['Wq'], 'L0_mix_bq': _L0_mix_in['bq'], 'L0_mix_Wk': _L0_mix_in['Wk'], 'L0_mix_bk': _L0_mix_in['bk'], 'L0_mix_Wv': _L0_mix_in['Wv'], 'L0_mix_bv': _L0_mix_in['bv'], 'L0_mix_Wo': _L0_mix_in['Wo'], 'L0_mix_bo': _L0_mix_in['bo'], 'L0_mix_proj': _L0_mix_in['proj'], 'L0_mix_ln2_s': _L0_mix_in['ln2_s'], 'L0_mix_ln2_b': _L0_mix_in['ln2_b'], 'L0_mix_W1': _L0_mix_in['W1'], 'L0_mix_b1': _L0_mix_in['b1'], 'L0_mix_W2': _L0_mix_in['W2'], 'L0_mix_b2': _L0_mix_in['b2'], 'L0_ffn_router_w': _L0_ffn_in['router_w'], 'L0_ffn_w1': _L0_ffn_in['w1'], 'L0_ffn_b1': _L0_ffn_in['b1'], 'L0_ffn_w2': _L0_ffn_in['w2'], 'L0_ffn_b2': _L0_ffn_in['b2'], 'L0_ffn_gamma': _L0_ffn_in['gamma'], 'L0_ffn_beta': _L0_ffn_in['beta']}

def reference(x, src, dst, L0_gnn_W_rel1, L0_gnn_b_rel1, L0_gnn_W_root1, L0_gnn_W_lin1, L0_gnn_b_lin1, L0_gnn_W_rel2, L0_gnn_b_rel2, L0_gnn_W_root2, L0_gnn_W_lin2, L0_gnn_b_lin2, L0_mix_ln1_s, L0_mix_ln1_b, L0_mix_Wq, L0_mix_bq, L0_mix_Wk, L0_mix_bk, L0_mix_Wv, L0_mix_bv, L0_mix_Wo, L0_mix_bo, L0_mix_proj, L0_mix_ln2_s, L0_mix_ln2_b, L0_mix_W1, L0_mix_b1, L0_mix_W2, L0_mix_b2, L0_ffn_router_w, L0_ffn_w1, L0_ffn_b1, L0_ffn_w2, L0_ffn_b2, L0_ffn_gamma, L0_ffn_beta):
    import jax
    import jax.numpy as jnp

    def _L0_gnn_ref(x, edge_index, W_rel1, b_rel1, W_root1, W_lin1, b_lin1, W_rel2, b_rel2, W_root2, W_lin2, b_lin2):
        import jax, jax.numpy as jnp
        import numpy as np
        N = 1024
        F = 512
        H = 512
        E = 8192
        src, dst = (edge_index[0], edge_index[1])

        def graph_conv(h, W_rel, b_rel, W_root):
            agg = jax.ops.segment_sum(h[src], dst, num_segments=N)
            return agg @ W_rel.T + b_rel + h @ W_root.T
        h = jax.nn.relu(graph_conv(x, W_rel1, b_rel1, W_root1) @ W_lin1.T + b_lin1)
        h = jax.nn.relu(graph_conv(h, W_rel2, b_rel2, W_root2) @ W_lin2.T + b_lin2)
        return h

    def _L0_mix_ref(x, ln1_s, ln1_b, Wq, bq, Wk, bk, Wv, bv, Wo, bo, proj, ln2_s, ln2_b, W1, b1, W2, b2):
        import jax, jax.numpy as jnp
        import numpy as np
        B, N, D = (2, 128, 512)
        L, H, DH, M = (2, 8, 64, 256)
        EPS_K = 0.0001

        def _layernorm(x, s, b):
            m = x.mean(-1, keepdims=True)
            v = x.var(-1, keepdims=True)
            return (x - m) / jnp.sqrt(v + 1e-05) * s + b

        def _softmax_kernel(x, proj, is_query):
            dh = x.shape[-1]
            data_norm = dh ** (-0.25)
            ratio = proj.shape[0] ** (-0.5)
            dd = jnp.einsum('bhnd,md->bhnm', x * data_norm, proj)
            diag = 0.5 * jnp.sum(x * x, axis=-1) * data_norm ** 2
            if is_query:
                stab = jnp.max(dd, axis=-1, keepdims=True)
            else:
                stab = jnp.max(dd, axis=(-1, -2), keepdims=True)
            return ratio * (jnp.exp(dd - diag[..., None] - stab) + EPS_K)

        def _linear_attention(qp, kp, v):
            k_sum = kp.sum(axis=2)
            d_inv = 1.0 / jnp.einsum('bhnm,bhm->bhn', qp, k_sum)
            ctx = jnp.einsum('bhnm,bhnd->bhmd', kp, v)
            return jnp.einsum('bhnm,bhmd,bhn->bhnd', qp, ctx, d_inv)

        def _performer_forward(x, ln1_s, ln1_b, Wq, bq, Wk, bk, Wv, bv, Wo, bo, proj, ln2_s, ln2_b, W1, b1, W2, b2):
            depth = Wq.shape[0]
            for l in range(depth):
                h = _layernorm(x, ln1_s[l], ln1_b[l])
                b, n, d = h.shape

                def heads(t):
                    return t.reshape(b, n, H, DH).transpose(0, 2, 1, 3)
                q = heads(h @ Wq[l] + bq[l])
                k = heads(h @ Wk[l] + bk[l])
                v = heads(h @ Wv[l] + bv[l])
                qp = _softmax_kernel(q, proj[l], True)
                kp = _softmax_kernel(k, proj[l], False)
                attn = _linear_attention(qp, kp, v)
                attn = attn.transpose(0, 2, 1, 3).reshape(b, n, H * DH)
                x = x + (attn @ Wo[l] + bo[l])
                h2 = _layernorm(x, ln2_s[l], ln2_b[l])
                ff = jax.nn.gelu(h2 @ W1[l] + b1[l]) @ W2[l] + b2[l]
                x = x + ff
            return x
        return _performer_forward(x, ln1_s, ln1_b, Wq, bq, Wk, bk, Wv, bv, Wo, bo, proj, ln2_s, ln2_b, W1, b1, W2, b2)

    def _L0_ffn_ref(x, router_w, w1, b1, w2, b2, gamma, beta):
        import jax, jax.numpy as jnp
        import numpy as np
        K = 2
        EPS = 1e-06

        def _layernorm(x, gamma, beta):
            mu = jnp.mean(x, axis=-1, keepdims=True)
            var = jnp.mean(jnp.square(x - mu), axis=-1, keepdims=True)
            return (x - mu) * jax.lax.rsqrt(var + EPS) * gamma + beta
        B, S, D = x.shape
        E = w1.shape[0]
        xf = x.reshape(-1, D)
        logits = xf @ router_w
        gate_vals, idx = jax.lax.top_k(logits, K)
        gates = jax.nn.softmax(gate_vals, axis=-1)
        out = jnp.zeros_like(xf)
        for e in range(E):
            h = jax.nn.relu(xf @ w1[e] + b1[e]) @ w2[e] + b2[e]
            y = _layernorm(xf + h, gamma[e], beta[e])
            w = jnp.sum(jnp.where(idx == e, gates, 0.0), axis=-1)
            out = out + w[:, None] * y
        return out.reshape(B, S, D)
    edge_index = jnp.stack([src, dst])
    xn = _layernorm(x, axis=-1)
    x = x + _L0_gnn_ref(xn, edge_index, L0_gnn_W_rel1, L0_gnn_b_rel1, L0_gnn_W_root1, L0_gnn_W_lin1, L0_gnn_b_lin1, L0_gnn_W_rel2, L0_gnn_b_rel2, L0_gnn_W_root2, L0_gnn_W_lin2, L0_gnn_b_lin2) + _L0_mix_ref(xn[None], L0_mix_ln1_s, L0_mix_ln1_b, L0_mix_Wq, L0_mix_bq, L0_mix_Wk, L0_mix_bk, L0_mix_Wv, L0_mix_bv, L0_mix_Wo, L0_mix_bo, L0_mix_proj, L0_mix_ln2_s, L0_mix_ln2_b, L0_mix_W1, L0_mix_b1, L0_mix_W2, L0_mix_b2)[0]
    x = x + _L0_ffn_ref(_layernorm(x, axis=-1)[None], L0_ffn_router_w, L0_ffn_w1, L0_ffn_b1, L0_ffn_w2, L0_ffn_b2, L0_ffn_gamma, L0_ffn_beta)[0]
    return x

_drawn_inputs = setup_inputs


def setup_inputs(seed=0):
    import zlib

    import numpy as np

    out = dict(_drawn_inputs(seed))
    spreads = {'L0_gnn_b_rel1': (0.0, 0.277),
     'L0_gnn_b_lin1': (0.0, 0.1),
     'L0_gnn_b_rel2': (0.0, 0.484),
     'L0_gnn_b_lin2': (0.0, 0.1),
     'L0_mix_ln1_s': (1.0, 0.6),
     'L0_mix_ln1_b': (0.0, 0.559),
     'L0_mix_bq': (0.0, 0.8),
     'L0_mix_bk': (0.0, 0.8),
     'L0_mix_bv': (0.0, 0.1),
     'L0_mix_bo': (0.0, 0.1),
     'L0_mix_ln2_s': (1.0, 0.2),
     'L0_mix_ln2_b': (0.0, 0.497),
     'L0_mix_b1': (0.0, 0.1),
     'L0_mix_b2': (0.0, 0.1),
     'L0_ffn_b1': (0.0, 0.8),
     'L0_ffn_b2': (0.0, 0.349),
     'L0_ffn_gamma': (1.0, 0.2),
     'L0_ffn_beta': (0.0, 0.367)}
    factors = {'L0_mix_Wq': 8.0,
     'L0_mix_Wk': 8.0,
     'L0_mix_proj': 8.0,
     'L0_ffn_w1': 8.0,
     'L0_ffn_w2': 6.696}
    for name, (base, spread) in spreads.items():
        noise = np.random.default_rng([zlib.crc32(name.encode()), seed]).standard_normal(out[name].shape)
        drawn = base * np.exp(spread * noise) if base else spread * noise
        out[name] = jnp.asarray(drawn.astype(out[name].dtype))
    for name, factor in factors.items():
        out[name] = (out[name] * factor).astype(out[name].dtype)
    return out
```

```python
import concourse.bass as bass
from concourse import mybir
from contextlib import ExitStack

N, D, P = 1024, 512, 128
NT, KT = N // P, D // P
H = 2
NH, DH, M = 8, 64, 256
MT = M // P
E_TOT = 2 * 8192 + 1024
EC = E_TOT // P
EP = EC // 2
EXP, EF = 8, 32
FC = 4
LAYERS = 2
EPS_LN, EPS_MOE, EPS_K = 1e-5, 1e-6, 1e-4
DN = float(DH) ** -0.25
SLOTS, PIECES = 4, 2
MIX_SLOTS = 4 + 2 * FC
GNN_SLOTS = 4
N_SLOTS = LAYERS * MIX_SLOTS + LAYERS * GNN_SLOTS
BANKS = 4

f32, f32r = mybir.dt.float32, mybir.dt.float32r
bf16, f16, i32, u32 = mybir.dt.bfloat16, mybir.dt.float16, mybir.dt.int32, mybir.dt.uint32
RMAX = bass.bass_isa.ReduceOp.max
ALU, ACT, AX = mybir.AluOpType, mybir.ActivationFunctionType, mybir.AxisListType


def numbered(names):
    return {name: i for i, name in enumerate(names)}


STEPS = NH // 2 * (NT // 2)
MIX_A = numbered(
    [("n1", h, k) for h in range(H) for k in range(KT)]
    + [("q", m, h) for m in range(KT) for h in range(H)]
    + [("k", m, h) for m in range(KT) for h in range(H)]
    + [("ddq", g, j) for g in range(STEPS) for j in range(2)]
    + [("o", h, k) for h in range(H) for k in range(KT)]
    + [("n2", h, k) for h in range(H) for k in range(KT)]
    + [("f", c, m, h) for c in range(FC) for m in range(KT) for h in range(H)]
)


def attention_order():
    for g in range(STEPS + 2):
        pair, s = divmod(g, NT // 2)
        if s == 0 and g < STEPS:
            yield "ctx", pair
            if pair + 1 < NH // 2:
                yield "ddk", pair + 1
        if g < STEPS:
            yield "ddq", g
        if 1 <= g <= STEPS:
            yield "tr", g - 1
        if g >= 2:
            yield "at", g - 2


def ring_v_attention():
    for what, g in attention_order():
        if what == "ddk":
            yield from (("ddk", g, s, j) for s in range(NT // 2) for j in range(2))
        elif what != "ddq":
            yield from ((what, g, j) for j in range(2))


FFN_ORDER = [("f", 0), ("f", 1), ("g", 0), ("f", 2), ("g", 1), ("f", 3), ("g", 2), ("g", 3)]
MIX_V = numbered(
    [("diag", w, m, h) for w in range(2) for m in range(KT) for h in range(H)]
    + [("ddk", 0, s, j) for s in range(NT // 2) for j in range(2)]
    + [("v", t) for t in range(NT)]
    + list(ring_v_attention())
    + [("wo", t) for t in range(NT)]
    + [("g", c, t) for c in range(FC) for t in range(NT)]
)
NA, NV = len(MIX_A), len(MIX_V)
assert NA % BANKS == 0 and NV % BANKS == 0
MIX_SPLIT = numbered([n for n in MIX_A if n[0] in ("n1", "o", "n2", "f")])
NS = len(MIX_SPLIT)
MIX_W = numbered(["q", "k", "v", "o"] + [w for w in FFN_ORDER])

GNN_A = numbered([(w, h, m) for w in ("g", "l") for h in range(H) for m in range(KT)])
GNN_V = numbered([("p", t) for t in range(NT)])


def build(nc, x, ends_c, wstream, cols, rows, projt, gcols, b1col, small, w2, ident_c, headmask_c,
          repl_c, iota_c, pair_c, iota8_c, out):
    ctx = ExitStack()
    with ctx:
        sem = lambda name: ctx.enter_context(nc.semaphore(name))
        sb = lambda name, shape, dt=f32: ctx.enter_context(nc.sbuf_tensor(name, shape, dt))

        ident = sb("ident", [P, P])
        iota8 = sb("iota8", [P, EXP])
        repl = sb("repl", [EXP, 2 * P])
        headmask = sb("headmask", [P, 2])
        proj_sb = sb("proj_sb", [P, M])
        col_sb = sb("col_sb", [P, 40])
        gcol_sb = sb("gcol_sb", [P, LAYERS * 8])
        b1_sb = sb("b1_sb", [P, 2])
        ctx_sb = sb("ctx_sb", [P, 2, 2, MT, DH + 1])
        ndiag = sb("ndiag", [P, 2, NT, NH])
        stats = sb("stats", [P, NT, 6])
        mv = sb("mv", [P, 2 * NT, 2])
        vare = sb("vare", [P, 2 * NT])
        rstd = sb("rstd", [P, 2 * NT])
        nhalf = sb("nhalf", [P, 2 * NT])
        kmax = sb("kmax", [P, NH // 2, 2, NT // 2])
        kmax1 = sb("kmax1", [P, NH // 2, 2])
        kall = sb("kall", [P, NH // 2, 2])
        nkall = sb("nkall", [P, NH // 2, 2])
        kbias = sb("kbias", [P, NH // 2, 2, NT])
        qmax = sb("qmax", [P, STEPS, 2, 2])
        qbias = sb("qbias", [P, STEPS, 2, 2])
        rden = sb("rden", [P, STEPS, 2, 2])
        span_p = sb("span_p", [P, 2, NT])
        span = sb("span", [P, 2, NT])
        bound = sb("bound", [P, 5, NT])
        bound_i = sb("bound_i", [P, 5, NT], i32)
        most_b = sb("most_b", [P, NT])
        most_p = sb("most_p", [P, 1])
        most = sb("most", [P, 1])
        most_i = sb("most_i", [P, 1], i32)

        KB = 1024
        offs, top = {}, (nc.sbuf_base + 31) // 32 * 32
        for name, size in [("slots", 64 * KB), ("stage", 8 * KB), ("xm", 16 * KB), ("ht", 32 * KB), ("q", 16 * KB),
                           ("k", 16 * KB), ("v", 16 * KB + 256), ("nat", 16 * KB), ("work", 8 * KB), ("rows", 6 * KB)]:
            offs[name] = top
            top += size
        assert top <= nc.sbuf_usable_end
        arena = sb("arena", [P, (top - offs["slots"]) // 4])
        at = lambda name, shape, dt, region, skip=0: nc.alloc_sbuf_tensor_at(name, shape, dt, offset=offs[region] + skip)
        Whi = at("w_hi", [P, SLOTS, KT, 512], f32r, "slots")
        Wlo = at("w_lo", [P, SLOTS, KT, 512], f32r, "slots", 32 * KB)
        stage = at("stage", [P, 2, 1024], f32, "stage")
        Xm = at("xm", [P, NT, D], f32, "xm")
        hT = at("ht_hi", [P, KT, N], f32r, "ht"), at("ht_lo", [P, KT, N], f32r, "ht", 16 * KB)
        qT = at("q_t", [P, KT, N], f32, "q")
        kT = at("k_t", [P, KT, N], f32, "k")
        V = at("v_sb", [P, NT, NH // 2, 2 * (DH + 1)], f32, "v")
        nat = at("nat", [P, NT, D], f32, "nat")
        sq = at("sq", [P, 2, 512], f32, "nat")
        expk = at("expk", [P, 2, NT, M], f32, "nat")
        work = at("work", [P, 4, 512], f32, "work")
        rows_sb = at("rows_sb", [P, 3, D], f32, "rows")
        fT = [(at("f0_hi", [P, KT, N], f32r, "q"), at("f0_lo", [P, KT, N], f32r, "k")),
              (at("f1_hi", [P, KT, N], f32r, "v"), at("f1_lo", [P, KT, N], f32r, "v", 16 * KB))]
        xg = at("xg", [P, NT, D], f32, "q")
        adj = at("adj", [P, NT, N], f32, "q")
        Pr = at("p_hi", [P, NT, D], f32r, "v"), at("p_lo", [P, NT, D], f32r, "v", 16 * KB)
        ends_i = at("ends_i", [P, 2, EC], i32, "rows")
        ends_f = at("ends_f", [P, 2, EC], f32, "rows", 2 * EC * 4)
        hot_src = at("hot_src", [P, 2, N], bf16, "v")
        hot_dst = at("hot_dst", [P, 2, P], bf16, "v", 4 * KB)
        iota = at("iota", [P, N], f16, "v", 5 * KB)
        zeros = at("zeros", [P, P], bf16, "v", 7 * KB)
        adj_nat = at("adj_nat", [P, 2, 512], f32, "v", 8 * KB)
        spans = at("spans", [P, 2, NT, EC], f32, "v", 7 * KB + 256)
        block_i = at("block_i", [P, EC], i32, "rows", 4 * EC * 4)
        block_f = at("block_f", [P, EC], f32, "rows", 5 * EC * 4)
        pair_no = at("pair_no", [P, 2, EC], f32, "rows", 6 * EC * 4)
        hsum = at("hsum", [P, KT, N], f32, "q")
        Xf = at("xf", [P, NT, D], f32, "k")
        h1 = at("h1", [P, 2, N], f32, "q")
        small_sb = at("small_sb", [EXP, 3, D], f32, "q", 8 * KB)
        hm = [at(f"hm{k}", [P, 2, N], f32, "v", 8 * KB * k) for k in range(2)]
        hotT = [at(f"hot_t{k}", [EXP, N], f32, "v", 16 * KB + 256 + 4 * KB * k) for k in range(3)]
        w2_sb = at("w2_sb", [P, 2, D], f32, "v", 28 * KB + 256)
        zz = [at(f"z{k}", [P, NT, D], f32, "ht", 16 * KB * k) for k in range(2)]
        logit = at("logit", [P, NT, EXP], f32, "work")
        best = at("best", [P, NT, 8], f32, "work", 256)
        besti = at("besti", [P, NT, 8], u32, "work", 512)
        bestf = at("bestf", [P, NT, 8], f32, "work", 768)
        hot = at("hot", [P, 3, NT, EXP], f32, "work", 1024)
        hotw = at("hotw", [P, NT, EXP], f32, "work", 1792)
        gate = at("gate", [P, 4, NT], f32, "work", 2048)
        gscale = at("gscale", [P, 2, NT], f32, "work", 3264)
        ut = at("ut", [P, 2, D], f32, "work", 4 * KB)

        psA = ctx.enter_context(nc.psum_tensor("ps_a", [P, BANKS, 512], f32))
        psV = ctx.enter_context(nc.psum_tensor("ps_v", [P, BANKS, 512], f32))

        a_full, a_empty = sem("a_full"), sem("a_empty")
        v_full, v_empty = sem("v_full"), sem("v_empty")
        consts_in, x_in, par_in, ends_in = (sem(s) for s in
            ("consts_in", "x_in", "par_in", "ends_in"))
        w_in = [sem("w_in0"), sem("w_in1")]
        w_split = sem("w_split")
        staged, split = sem("staged"), sem("split")
        sq_ready = sem("sq_ready")
        normed = sem("normed")
        var_ready, eps_added, rstd_ready = sem("var_ready"), sem("eps_added"), sem("rstd_ready")
        kmax_ready, kall_ready, kbias_ready = sem("kmax_ready"), sem("kall_ready"), sem("kbias_ready")
        expk_done, expk_eps = sem("expk_done"), sem("expk_eps")
        qbias_ready = sem("qbias_ready")
        bias_added = sem("bias_added")
        v_chain = sem("v_chain")
        p_chain = sem("p_chain")
        hot_ready, hot_used = sem("hot_ready"), sem("hot_used")
        span_ready, span_all, bounds_ready = sem("span_ready"), sem("span_all"), sem("bounds_ready")
        most_ready, most_all, most_loaded = sem("most_ready"), sem("most_all"), sem("most_loaded")
        adj_full, adj_copied, adj_turned, adj_done = (sem(s) for s in
            ("adj_full", "adj_copied", "adj_turned", "adj_done"))
        gate_in, gate_exp = sem("gate_in"), sem("gate_exp")
        hots_ready, y_ready, stored = sem("hots_ready"), sem("y_ready"), sem("stored")
        rows_in, moe_in = sem("rows_in"), sem("moe_in")
        w_high, high, p_high = sem("w_high"), sem("high"), sem("p_high")
        held = sem("held")
        stats_done, x_normed, nkall_done = sem("stats_done"), sem("x_normed"), sem("nkall_done")
        qmax_done, rden_done, ends_done = sem("qmax_done"), sem("rden_done"), sem("ends_done")

        A_BASE, V_BASE, S_BASE = LAYERS * NA, LAYERS * NV, LAYERS * NS
        GA_T = A_BASE
        GA = GA_T + H * KT
        MA_T = GA + LAYERS * 16
        MA_H = MA_T + H * KT
        GV = V_BASE
        GV_X = GV + LAYERS * NT
        MV_L = GV_X + NT
        MV_O = MV_L + 1
        MV_R = MV_O + 6
        MV_Z = MV_R + 8
        MV_G = MV_Z + 2 * NT
        SP_T = S_BASE
        SP_G = SP_T + H * KT
        SP_M = SP_G + LAYERS * 16
        NORM_X, NORM_MIX = 0, 2 * NT
        NORM_G = LAYERS * NORM_MIX
        NORM_M = NORM_G + NT
        LN_MIX, LN_G, LN_M, LN_Y = 2, 2 + 4 * LAYERS, 4 + 4 * LAYERS, 6 + 4 * LAYERS
        W_GNN = LAYERS * MIX_SLOTS

        def free(i):
            return i + 1

        def done(i):
            return i + (1 + BANKS)

        def hold(engine):
            engine.sem_inc(held, 1)

        def nodes(t):
            return slice(t * P, (t + 1) * P)

        def half(h):
            return slice(h * 512, (h + 1) * 512)

        def pair_bounds(engine, g):
            load = lambda n, least, most: engine.value_load(bound_i[0:1, n, bass.ds(g, 1)], min_val=least, max_val=most)
            return load(0, 0, EP - 1), load(1, 1, EP), load(4, 0, (NT + 1) * EP)

        block = ctx.enter_context(nc.Block())

        @block.sync
        def _(sp):
            sp.dma_start(ident[:], ident_c).then_inc(consts_in, 16)
            sp.dma_start(headmask[:], headmask_c).then_inc(consts_in, 16)
            sp.dma_start(gcol_sb[:], gcols).then_inc(consts_in, 16)
            sp.dma_start(b1_sb[:], b1col).then_inc(consts_in, 16)
            sp.dma_start(iota8[:], iota8_c).then_inc(consts_in, 16)
            sp.dma_start(repl[:], repl_c).then_inc(consts_in, 16)

            for j in range(PIECES):
                sp.dma_start(stage[:, j, :], wstream[0, j]).then_inc(w_in[j], 16)
            with sp.Fori(1, N_SLOTS) as s:
                for j in range(PIECES):
                    sp.wait_ge(w_split, s * PIECES + (j - 1))
                    sp.dma_start(stage[:, j, :], wstream[s, j]).then_inc(w_in[j], 16)
            for t in range(NT):
                sp.wait_ge(v_empty, done(MV_G + 2 * NT + t))
                sp.dma_start(out[t * P:(t + 1) * P, :], Xm[:, t, :]).then_inc(stored, 16)
            sp.wait_ge(stored, 16 * NT)

        @block.tensor
        def _(pe):
            def mm3(ps, left, right, first, last):
                nc.tensor.matmul(ps, left[0], right[0], start=first, stop=False)
                nc.tensor.matmul(ps, left[0], right[1], start=False, stop=False)
                return nc.tensor.matmul(ps, left[1], right[0], start=False, stop=last)

            def part(tensors, k, columns):
                return tensors[0][:, k, columns], tensors[1][:, k, columns]

            def weight(slot, k, columns=slice(0, 512)):
                return Whi[:, slot, k, columns], Wlo[:, slot, k, columns]

            def bank_a(i, base=0):
                pe.wait_ge(a_empty, base + free(i))
                return psA[:, i % BANKS, :]

            def bank_v(i, base=0):
                pe.wait_ge(v_empty, base + free(i))
                return psV[:, i % BANKS, :]

            def turn(ps, sources, full):
                for n, source in enumerate(sources):
                    last = nc.tensor.transpose(ps[:, nodes(n)], source, ident[:])
                last.then_inc(full, 1)

            def into_t(w, right, m, h, ps):
                for k in range(KT):
                    last = mm3(ps, w(k, nodes(m)), part(right, k, half(h)), k == 0, k == KT - 1)
                return last

            def into_nat(w, left, t, ps):
                for k in range(KT):
                    last = mm3(ps, part(left, k, nodes(t)), w(k), k == 0, k == KT - 1)
                return last

            def slot_of(n):
                return lambda k, columns=slice(0, 512): weight(n, k, columns)

            pe.wait_ge(consts_in, 96)

            def mix_layer(L):
                a0, v0, s0 = L * NA, L * NV, L * NS

                def bank(ring, name):
                    return bank_a(MIX_A[name], a0) if ring == "a" else bank_v(MIX_V[name], v0)

                def written_a(name):
                    pe.wait_ge(a_empty, a0 + done(MIX_A[name]))

                def written_v(name):
                    pe.wait_ge(v_empty, v0 + done(MIX_V[name]))

                def weight_slot(name):
                    pe.wait_ge(w_split, L * (MIX_SLOTS * PIECES) + (MIX_W[name] + 1) * PIECES)
                    return slot_of(MIX_W[name] % SLOTS)

                def need_split(name):
                    pe.wait_ge(split, s0 + done(MIX_SPLIT[name]))

                def turn_normed(which):
                    for h in range(H):
                        pe.wait_ge(normed, L * NORM_MIX + (NT * (which - 1) + 4 * (h + 1)))
                        for k in range(KT):
                            turn(bank("a", (f"n{which}", h, k)), [nat[:, 4 * h + n, nodes(k)] for n in range(4)], a_full)

                turn_normed(1)

                def diag(w, m, h):
                    i = w * 8 + m * H + h
                    ps = bank("v", ("diag", w, m, h))
                    pe.wait_ge(sq_ready, L * 16 + (i + 1))
                    for n in range(4):
                        last = nc.tensor.matmul(ps[:, 2 * n:2 * n + 2], sq[:, i % 2, nodes(n)], headmask[:],
                                                start=True, stop=True)
                    last.then_inc(v_full, 1)

                behind = None
                for w, name in enumerate(("q", "k")):
                    slot = weight_slot(name)
                    for m in range(KT):
                        for h in range(H):
                            need_split(("n1", h, KT - 1))
                            into_t(slot, hT, m, h, bank("a", (name, m, h))).then_inc(a_full, 1)
                            if behind:
                                diag(*behind)
                            behind = w, m, h
                diag(*behind)

                pe.wait_ge(par_in, L * 32 + 32)

                def scores(source, pair, s, banks, full):
                    for n in range(2):
                        for j in range(2):
                            head = slice(DH * j, DH * (j + 1))
                            last = nc.tensor.matmul(banks[j][:, M * n:M * (n + 1)],
                                                    source[head, pair, nodes(2 * s + n)], proj_sb[head, :],
                                                    start=True, stop=True)
                            if n == 1:
                                last.then_inc(full, 1)

                def ddk(pair):
                    for s in range(NT // 2):
                        scores(kT, pair, s, [bank("v", ("ddk", pair, s, j)) for j in range(2)], v_full)

                written_a(("k", KT - 1, H - 1))
                ddk(0)
                slot = weight_slot("v")
                for t in range(NT):
                    into_nat(slot, hT, t, bank("v", ("v", t))).then_inc(v_full, 1)
                written_v(("v", NT - 1))

                for what, g in attention_order():
                    pair, s = divmod(g, NT // 2)
                    if what == "ddk":
                        ddk(g)
                    elif what == "ddq":
                        scores(qT, pair, s, [bank("a", ("ddq", g, j)) for j in range(2)], a_full)
                    else:
                        for j in range(2):
                            ps = bank("v", (what, g, j))
                            if what == "ctx":
                                pe.wait_ge(expk_eps, L * NH + (2 * g + j + 1))
                                for m in range(MT):
                                    for t in range(NT):
                                        last = nc.tensor.matmul(ps[:, m * (DH + 1):(m + 1) * (DH + 1)],
                                                                expk[:, j, t, nodes(m)], V[:, t, g, (DH + 1) * j:(DH + 1) * (j + 1)],
                                                                start=t == 0, stop=t == NT - 1)
                                last.then_inc(v_full, 1)
                            elif what == "tr":
                                written_a(("ddq", g, j))
                                turn(ps, [work[:, j, M * n + m * P:M * n + (m + 1) * P]
                                          for m in range(MT) for n in range(2)], v_full)
                            else:
                                written_v(("tr", g, j))
                                for n in range(2):
                                    for m in range(MT):
                                        last = nc.tensor.matmul(ps[:, n * (DH + 1):(n + 1) * (DH + 1)],
                                                                work[:, 2 + j, nodes(2 * m + n)],
                                                                ctx_sb[:, pair % 2, j, m, :],
                                                                start=m == 0, stop=m == MT - 1)
                                last.then_inc(v_full, 1)

                written_v(("at", STEPS - 1, 1))
                for h in range(H):
                    for k in range(KT):
                        turn(bank("a", ("o", h, k)), [V[:, 4 * h + n, k, 1:1 + P] for n in range(4)], a_full)
                slot = weight_slot("o")
                for t in range(NT):
                    need_split(("o", t // 4, KT - 1))
                    into_nat(slot, hT, t, bank("v", ("wo", t))).then_inc(v_full, 1)

                turn_normed(2)
                for kind, c in FFN_ORDER:
                    slot = weight_slot((kind, c))
                    if kind == "f":
                        for m in range(KT):
                            for h in range(H):
                                need_split(("n2", h, KT - 1))
                                into_t(slot, hT, m, h, bank("a", ("f", c, m, h))).then_inc(a_full, 1)
                    else:
                        need_split(("f", c, KT - 1, H - 1))
                        for t in range(NT):
                            into_nat(slot, fT[c % 2], t, bank("v", ("g", c, t))).then_inc(v_full, 1)

            with pe.Fori(0, LAYERS) as L:
                mix_layer(L)

            for h in range(H):
                pe.wait_ge(normed, NORM_G + 4 * (h + 1))
                for k in range(KT):
                    turn(bank_a(GA_T + h * KT + k), [xg[:, 4 * h + n, nodes(k)] for n in range(4)], a_full)

            pe.wait_ge(v_empty, done(V_BASE - 1))
            pe.wait_ge(bounds_ready, 1)
            with pe.Fori(0, NT) as g:
                first, end, base = pair_bounds(pe, g)
                pe.wait_ge(adj_copied, g + 1)
                for s in range(2):
                    nc.tensor.matmul(psV[:, s, :], zeros[:], iota[:, half(s)], start=True, stop=False)
                with pe.Fori(first, end) as c:
                    for u in range(2):
                        pe.wait_ge(hot_ready, (c + base) * 2 + (u + 1))
                        for s in range(2):
                            last = nc.tensor.matmul(psV[:, s, :], hot_dst[:, u, :], hot_src[:, u, half(s)],
                                                    start=False, stop=False)
                        last.then_inc(hot_used, 1)
                for s in range(2):
                    last = nc.tensor.matmul(psV[:, s, :], zeros[:], iota[:, half(s)], start=False, stop=True)
                last.then_inc(adj_full, 1)
                pe.wait_ge(adj_copied, g + 2)
                pe.wait_ge(adj_done, g * 2 + 2)
                for s in range(2):
                    turn(psV[:, 2 + s, :], [adj_nat[:, s, nodes(n)] for n in range(4)], adj_turned)
            pe.wait_ge(adj_done, 2 * NT + 2)
            pe.wait_ge(most_loaded, 1)
            largest = pe.value_load(most_i[0:1, 0:1], min_val=0, max_val=E_TOT)

            with pe.Fori(0, LAYERS) as L:
                w0 = L * (GNN_SLOTS * PIECES)
                pe.wait_ge(w_split, w0 + (W_GNN + 1) * PIECES)
                pe.wait_ge(split, L * 16 + done(SP_G - 1))
                for t in range(NT):
                    into_nat(slot_of(0), hT, t, bank_v(GV + t, L * NT)).then_inc(v_full, 1)
                pe.wait_ge(w_split, w0 + (W_GNN + 2) * PIECES)
                for h in range(H):
                    for m in range(KT):
                        ps = bank_a(GA + h * KT + m, L * 16)
                        for k in range(KT - 1):
                            mm3(ps, weight(1, k, nodes(m)), part(hT, k, half(h)), k == 0, False)
                        pe.wait_ge(v_empty, L * NT + done(GV + NT - 1))
                        with pe.If(largest <= 4096):
                            for t in range(NT):
                                for i in range(2):
                                    nc.tensor.matmul(ps, Pr[i][:, t, nodes(m)], adj[:, t, half(h)].bitcast(f32r),
                                                     start=False, stop=False)
                        with pe.Else():
                            for t in range(NT):
                                for i in range(2):
                                    nc.tensor.matmul(ps, Pr[i][:, t, nodes(m)].bitcast(f32), adj[:, t, half(h)],
                                                     start=False, stop=False)
                        mm3(ps, weight(1, KT - 1, nodes(m)), part(hT, KT - 1, half(h)), False,
                            True).then_inc(a_full, 1)
                pe.wait_ge(w_split, w0 + (W_GNN + 3) * PIECES)
                for h in range(H):
                    pe.wait_ge(split, L * 16 + done(SP_G + KT * (h + 1) - 1))
                    for m in range(KT):
                        into_t(slot_of(2), hT, m, h, bank_a(GA + 8 + h * KT + m, L * 16)).then_inc(a_full, 1)

            pe.wait_ge(y_ready, KT)
            for t in range(NT):
                turn(bank_v(GV_X + t), [hsum[:, k, nodes(t)] for k in range(KT)], v_full)

            for h in range(H):
                pe.wait_ge(normed, NORM_M + 4 * (h + 1))
                for k in range(KT):
                    turn(bank_a(MA_T + h * KT + k), [Xf[:, 4 * h + n, nodes(k)] for n in range(4)], a_full)
            x0 = GNN_SLOTS - 1
            w1 = [w[:, x0, 0:2, :].rearrange("p a b -> p (a b)").rearrange("p (k n) -> p k n", k=KT) for w in (Whi, Wlo)]
            router = [w[:, x0, 2, 0:KT * EXP].rearrange("p (k n) -> p k n", k=KT) for w in (Whi, Wlo)]
            pe.wait_ge(w_split, N_SLOTS * PIECES)
            pe.wait_ge(split, done(SP_M + 7))
            ps = bank_v(MV_L)
            for t in range(NT):
                for k in range(KT):
                    last = mm3(ps[:, t * EXP:(t + 1) * EXP], part(hT, k, nodes(t)), (router[0][:, k, :], router[1][:, k, :]),
                               k == 0, k == KT - 1)
            last.then_inc(v_full, 1)
            for m in range(2):
                for h in range(H):
                    ps = bank_a(MA_H + 2 * m + h)
                    for k in range(KT):
                        last = mm3(ps, part(w1, k, nodes(m)), part(hT, k, half(h)), k == 0, k == KT - 1)
                    last.then_inc(a_full, 1)
            pe.wait_ge(hots_ready, 1)
            for q in range(3):
                for h in range(H):
                    ps = bank_v(MV_O + 2 * q + h)
                    for n in range(4):
                        last = nc.tensor.transpose(ps[0:EXP, nodes(n)], hot[:, q, 4 * h + n, :], ident[:])
                    last.then_inc(v_full, 1)
            pe.wait_ge(moe_in, 32)
            pe.wait_ge(v_empty, done(MV_O + 5))
            for q in range(2):
                for m in range(2):
                    for h in range(H):
                        nc.tensor.matmul(bank_v(MV_R + 4 * q + 2 * m + h), repl[:, nodes(m)], hotT[q][:, half(h)],
                                         start=True, stop=True).then_inc(v_full, 1)
            for q in range(2):
                pe.wait_ge(v_empty, done(MV_R + 4 * q + 3))
                for t in range(NT):
                    ps = bank_v(MV_Z + q * NT + t)
                    for m in range(2):
                        nc.tensor.matmul(ps, hm[q][:, m, nodes(t)], w2_sb[:, m, :], start=m == 0, stop=False)
                    nc.tensor.matmul(ps, hotT[q][:, nodes(t)], small_sb[:, 0, :], start=False,
                                     stop=True).then_inc(v_full, 1)
            for q in range(3):
                for t in range(NT):
                    nc.tensor.matmul(bank_v(MV_G + q * NT + t), hotT[q][:, nodes(t)], small_sb[:, 1 + q // 2, :],
                                     start=True, stop=True).then_inc(v_full, 1)

        @block.scalar
        def _(act):
            act.sem_inc(a_empty, BANKS)
            for t in range(NT):
                act.dma_start(nat[:, t, :], x[t * P:(t + 1) * P, :]).then_inc(x_in, 16)

            def evacuate(i, n, base_a, base_s, func, own_wait=False, **how):
                act.wait_ge(a_full, base_a + (i + 1))
                act.wait_ge(split, base_s + free(n))
                if own_wait:
                    hold(act)
                nc.scalar.activation(work[:, n % 4, :], psA[:, i % BANKS, :], func, **how).then_inc(a_empty, 1)

            def mix_layer(L):
                a0, s0, v0 = L * NA, L * NS, L * NV
                act.wait_ge(a_empty, a0 + BANKS)
                act.wait_ge(bias_added, L * 2 * NT + 1)
                act.wait_ge(v_empty, v0 + 1)
                act.dma_start(col_sb[:], cols[L]).then_inc(par_in, 16)
                act.dma_start(proj_sb[:], projt[L]).then_inc(par_in, 16)
                act.dma_start(rows_sb[:], rows[L].partition_broadcast(P)).then_inc(rows_in, 16)
                act.wait_ge(par_in, L * 32 + 32)

                def out(name, func, **how):
                    evacuate(MIX_A[name], MIX_SPLIT[name], a0, s0, func, **how)

                def column(n):
                    return col_sb[:, n:n + 1]

                for h in range(H):
                    for k in range(KT):
                        out(("n1", h, k), ACT.Identity, scale=column(k), bias=column(4 + k))
                for w, (name, dest) in enumerate((("q", qT), ("k", kT))):
                    for m in range(KT):
                        for h in range(H):
                            i, n = MIX_A[(name, m, h)], w * 8 + m * H + h
                            bias = column(8 + 4 * w + m)
                            act.wait_ge(a_full, a0 + (i + 1))
                            if n >= 2:
                                w2_, r = divmod(n - 2, 8)
                                act.wait_ge(v_full, v0 + (MIX_V[("diag", w2_, r // 2, r % 2)] + 1))
                            nc.scalar.activation(sq[:, n % 2, :], psA[:, i % BANKS, :], ACT.Square,
                                                 bias=bias).then_inc(sq_ready, 1)
                            nc.scalar.activation(dest[:, m, half(h)], psA[:, i % BANKS, :],
                                                 ACT.Identity, bias=bias).then_inc(a_empty, 1)

                def exp_k(pair, first, last):
                    act.wait_ge(kbias_ready, L * (NH // 2) + (pair + 1))
                    for n in range(first, last):
                        j, t = divmod(n, NT)
                        nc.scalar.activation(expk[:, j, t, :], expk[:, j, t, :], ACT.Exp, scale=DN,
                                             bias=kbias[:, pair, j, t:t + 1]).then_inc(expk_done, 1)

                exp_k(0, 0, 2 * NT)
                for g in range(STEPS):
                    pair, s = divmod(g, NT // 2)
                    for j in range(2):
                        i = MIX_A[("ddq", g, j)]
                        act.wait_ge(qbias_ready, L * 2 * STEPS + (2 * g + j + 1))
                        if g:
                            act.wait_ge(v_full, v0 + (MIX_V[("tr", g - 1, j)] + 1))
                        for n in range(2):
                            last = nc.scalar.activation(work[:, j, M * n:M * (n + 1)],
                                                        psA[:, i % BANKS, M * n:M * (n + 1)], ACT.Exp, scale=DN,
                                                        bias=qbias[:, g, j, n:n + 1])
                        last.then_inc(a_empty, 1)
                    if s and pair + 1 < NH // 2:
                        exp_k(pair + 1, (0, 6, 11)[s - 1], (6, 11, 16)[s - 1])
                for h in range(H):
                    for k in range(KT):
                        out(("o", h, k), ACT.Copy)
                for h in range(H):
                    for k in range(KT):
                        out(("n2", h, k), ACT.Identity, scale=column(16 + k), bias=column(20 + k))
                for c in range(FC):
                    for m in range(KT):
                        for h in range(H):
                            out(("f", c, m, h), ACT.Gelu_apprx_tanh, bias=column(24 + 4 * c + m))

            with act.Fori(0, LAYERS) as L:
                mix_layer(L)

            def gbias(L, n):
                return gcol_sb[:, bass.ds(L * 8 + n, 1)]

            act.wait_ge(v_empty, done(V_BASE - 1))
            act.wait_ge(bias_added, LAYERS * 2 * NT + 1)
            for t in range(NT):
                act.dma_start(nat[:, t, :], x[t * P:(t + 1) * P, :]).then_inc(x_in, 16)
            act.dma_start(ends_i[:], ends_c).then_inc(ends_in, 16)
            act.dma_start(iota[:], iota_c.partition_broadcast(P)).then_inc(ends_in, 16)
            act.dma_start(pair_no[:], pair_c.partition_broadcast(P)).then_inc(ends_in, 16)
            for n in range(H * KT):
                evacuate(GA_T + n, SP_T + n, 0, 0, ACT.Copy)
            with act.Fori(0, LAYERS) as L:
                for n in range(H * KT):
                    evacuate(GA + n, SP_G + n, L * 16, L * 16, ACT.Identity, True, bias=gbias(L, n % KT))
                for n in range(H * KT):
                    evacuate(GA + 8 + n, SP_G + 8 + n, L * 16, L * 16, ACT.Relu, True, bias=gbias(L, 4 + n % KT))
            act.wait_ge(v_full, MV_L)
            act.dma_start(small_sb[:], small).then_inc(moe_in, 16)
            act.dma_start(w2_sb[:], w2).then_inc(moe_in, 16)
            for n in range(H * KT):
                evacuate(MA_T + n, SP_M + n, 0, 0, ACT.Copy)
            for m in range(2):
                for h in range(H):
                    i = MA_H + 2 * m + h
                    act.wait_ge(a_full, i + 1)
                    nc.scalar.activation(h1[:, m, half(h)], psA[:, i % BANKS, :], ACT.Relu,
                                         bias=b1_sb[:, m:m + 1]).then_inc(a_empty, 1)
            act.wait_ge(gate_in, 1)
            nc.scalar.activation(gate[:, 1, :], gate[:, 0, :], ACT.Exp).then_inc(gate_exp, 1)

        @block.gpsimd
        def _(pool):
            pool.sem_inc(bias_added, 1)
            nc.gpsimd.memset(nhalf[:], -0.5).then_inc(p_chain, 1)
            pool.wait_ge(p_chain, 1)

            def split_weight(s, slot):
                for j in range(PIECES):
                    whole = slice(2 * j, 2 * j + 2)
                    hi, lo = (w[:, slot, whole, :].rearrange("p a b -> p (a b)") for w in (Whi, Wlo))
                    pool.wait_ge(w_in[j], s * 16 + 16)
                    hold(pool)
                    nc.gpsimd.tensor_copy(hi, stage[:, j, :]).then_inc(w_high, 1)
                    pool.wait_ge(w_high, s * PIECES + (j + 1))
                    nc.gpsimd.tensor_tensor(lo, stage[:, j, :], hi.bitcast(f32), ALU.subtract).then_inc(w_split, 1)

            def inverse_deviation(base, n, columns, eps=EPS_LN):
                pool.wait_ge(var_ready, base + (n + 1))
                hold(pool)
                nc.gpsimd.tensor_scalar(vare[:, columns], mv[:, columns, 1], eps, None, ALU.add).then_inc(eps_added, 1)
                pool.wait_ge(eps_added, base + (n + 1))
                nc.gpsimd.tensor_tensor(rstd[:, columns], vare[:, columns], nhalf[:, columns], ALU.pow).then_inc(rstd_ready, 1)

            def both_halves(base, n, eps=EPS_LN):
                for h in range(H):
                    inverse_deviation(base, n + h, slice(4 * h, 4 * h + 4), eps)

            split_weight(0, 0)
            both_halves(0, 0)
            for n in range(1, 4):
                split_weight(n, n)

            def mix_layer(L):
                a0, v0 = L * NA, L * NV
                w_base = L * MIX_SLOTS

                def load(n, last_user):
                    ring, name = last_user
                    if ring == "a":
                        pool.wait_ge(a_full, a0 + (MIX_A[name] + 1))
                    else:
                        pool.wait_ge(v_full, v0 + (MIX_V[name] + 1))
                    split_weight(w_base + n, n % SLOTS)

                def add_row(r, ready):
                    pool.wait_ge(rows_in, L * 16 + 16)
                    pool.wait_ge(normed, L * NORM_MIX + ready)
                    for t in range(NT):
                        nc.gpsimd.tensor_tensor(Xm[:, t, :], Xm[:, t, :], rows_sb[:, r, :], ALU.add).then_inc(bias_added, 1)

                both_halves(L * 4, LN_MIX)
                add_row(1, NT)
                for pair in range(NH // 2):
                    pool.wait_ge(kmax_ready, L * (NH // 2) + (pair + 1))
                    hold(pool)
                    nc.gpsimd.partition_all_reduce(kall[:, pair, :], kmax1[:, pair, :], P, RMAX).then_inc(kall_ready, 1)
                    for j in range(2):
                        pool.wait_ge(expk_done, L * NH * NT + (2 * pair + j + 1) * NT)
                        hold(pool)
                        e = expk[:, j, :, :].rearrange("p t m -> p (t m)")
                        nc.gpsimd.tensor_scalar(e, e, EPS_K, None, ALU.add).then_inc(expk_eps, 1)
                    if pair < 3:
                        load(4 + pair, (("a", ("q", KT - 1, H - 1)), ("a", ("k", KT - 1, H - 1)), ("v", ("v", NT - 1)))[pair])
                both_halves(L * 4, LN_MIX + 2)
                add_row(2, 2 * NT)
                load(7, ("v", ("wo", NT - 1)))
                for n in range(8, 16):
                    kind, c = FFN_ORDER[n - 8]
                    load(n, ("a", ("f", c, KT - 1, H - 1)) if kind == "f" else ("v", ("g", c, NT - 1)))

            with pool.Fori(0, LAYERS) as L:
                mix_layer(L)

            both_halves(0, LN_G)
            for t in range(NT):
                pool.wait_ge(normed, NORM_G + NT)
                nc.gpsimd.tensor_tensor(Xm[:, t, :], Xm[:, t, :], nat[:, t, :], ALU.add).then_inc(bias_added, 1)
            pool.wait_ge(span_ready, 1)
            nc.gpsimd.partition_all_reduce(span[:].rearrange("p a b -> p (a b)"), span_p[:].rearrange("p a b -> p (a b)"),
                                           P, RMAX).then_inc(span_all, 1)
            pool.wait_ge(most_ready, 1)
            nc.gpsimd.partition_all_reduce(most[:], most_p[:], P, RMAX).then_inc(most_all, 1)
            pool.wait_ge(v_full, GV + NT)
            split_weight(W_GNN + 4, 0)
            pool.wait_ge(a_full, GA + 8)
            split_weight(W_GNN + 5, 1)
            pool.wait_ge(a_full, GA + 16)
            split_weight(W_GNN + 6, 2)
            split_weight(W_GNN + 7, 3)
            both_halves(0, LN_M)
            for q in range(2):
                inverse_deviation(0, LN_Y + q, slice(NT * q, NT * (q + 1)), EPS_MOE)

        @block.vector
        def _(dve):
            dve.sem_inc(v_empty, BANKS)
            dve.sem_inc(split, BANKS)

            def statistics(source, columns):
                for t in columns:
                    last = nc.vector.bn_stats(stats[:, t % NT, :], source(t))
                last.then_inc(stats_done, 1)

            def aggregate(columns, count):
                dve.wait_ge(stats_done, count)
                hold(dve)
                for t in columns:
                    last = nc.vector.bn_aggr(mv[:, t, :], stats[:, t % NT, :])
                last.then_inc(var_ready, 1)

            def normalise(source, dest, sem_, base=0, n=0):
                for h in range(H):
                    tiles = range(4 * h, 4 * h + 4)
                    statistics(source, tiles)
                    aggregate(tiles, base + (n + h + 1))
                for h in range(H):
                    dve.wait_ge(rstd_ready, base + (n + h + 1))
                    for t in range(4 * h, 4 * h + 4):
                        last = nc.vector.tensor_scalar(dest[:, t, :], source(t), mv[:, t, 0:1], rstd[:, t:t + 1],
                                                       ALU.subtract, ALU.mult)
                        if sem_ is not None:
                            last.then_inc(sem_, 1)
                return last

            def split_block(n, base, hi, lo, after=None):
                dve.wait_ge(a_empty, after)
                nc.vector.tensor_copy(hi, work[:, n % 4, :]).then_inc(high, 1)
                dve.wait_ge(high, base + (n + 1))
                nc.vector.tensor_tensor(lo, work[:, n % 4, :], hi.bitcast(f32), ALU.subtract).then_inc(split, 1)

            dve.wait_ge(x_in, 16 * NT)
            normalise(lambda t: nat[:, t, :], Xm, None).then_inc(x_normed, 1)
            dve.wait_ge(x_normed, 1)

            def mix_layer(L):
                a0, v0, s0 = L * NA, L * NV, L * NS

                def job(*name):
                    i = MIX_V[name]
                    dve.wait_ge(v_full, v0 + (i + 1))
                    return psV[:, i % BANKS, :]

                def split_t(name, tensors, k, h):
                    split_block(MIX_SPLIT[name], s0, tensors[0][:, k, half(h)], tensors[1][:, k, half(h)],
                                after=a0 + done(MIX_A[name]))

                dve.wait_ge(v_empty, v0 + BANKS)
                normalise(lambda t: Xm[:, t, :], nat, normed, L * 4, LN_MIX)
                for h in range(H):
                    for k in range(KT):
                        split_t(("n1", h, k), hT, k, h)
                for w in range(2):
                    for m in range(KT):
                        for h in range(H):
                            ps = job("diag", w, m, h)
                            nc.vector.tensor_scalar(ndiag[:, w, 4 * h:4 * h + 4, 2 * m:2 * m + 2],
                                                    ps[:, 0:8].rearrange("p (t j) -> p t j", j=2), -0.5 * DN * DN, None,
                                                    ALU.mult).then_inc(v_empty, 1)

                def ddk(pair):
                    for s in range(NT // 2):
                        for j in range(2):
                            ps = job("ddk", pair, s, j)
                            nc.vector.tensor_scalar(expk[:, j, 2 * s:2 * s + 2, :],
                                                    ps.rearrange("p (t m) -> p t m", m=M), 1.0, -3.0e38, ALU.mult, ALU.max,
                                                    accum_out=kmax[:, pair, j, s:s + 1]).then_inc(v_empty, 1)
                    dve.wait_ge(v_empty, v0 + done(MIX_V[("ddk", pair, NT // 2 - 1, 1)]))
                    nc.vector.tensor_reduce(kmax1[:, pair, :], kmax[:, pair, :, :], axis=AX.X,
                                            op=ALU.max).then_inc(kmax_ready, 1)

                def k_bias(pair):
                    dve.wait_ge(kall_ready, L * (NH // 2) + (pair + 1))
                    nc.vector.tensor_scalar(nkall[:, pair, :], kall[:, pair, :], -DN, None, ALU.mult).then_inc(nkall_done, 1)
                    dve.wait_ge(nkall_done, L * (NH // 2) + (pair + 1))
                    for j in range(2):
                        last = nc.vector.tensor_scalar(kbias[:, pair, j, :], ndiag[:, 1, :, 2 * pair + j],
                                                       nkall[:, pair, j:j + 1], None, ALU.add)
                    last.then_inc(kbias_ready, 1)

                ddk(0)
                k_bias(0)
                dve.wait_ge(rows_in, L * 16 + 16)
                nc.vector.memset(V[:, :, :, 0:2 * DH + 2:2 * DH + 1], 1.0)
                for t in range(NT):
                    ps = job("v", t)
                    nc.vector.tensor_tensor(V[:, t, :, 1:1 + P], ps.rearrange("p (h d) -> p h d", d=P),
                                            rows_sb[:, 0, :].rearrange("p (h d) -> p h d", d=P), ALU.add).then_inc(v_empty, 1)

                for what, g in attention_order():
                    pair, s = divmod(g, NT // 2)
                    if what == "ddk":
                        ddk(g)
                        continue
                    for j in range(2):
                        if what == "ctx":
                            ps = job("ctx", g, j)
                            nc.vector.tensor_copy(ctx_sb[:, g % 2, j, :, :],
                                                  ps[:, 0:MT * (DH + 1)].rearrange("p (m d) -> p m d", m=MT)).then_inc(v_empty, 1)
                        elif what == "ddq":
                            i = MIX_A[("ddq", g, j)]
                            dve.wait_ge(a_full, a0 + (i + 1))
                            nc.vector.tensor_reduce(qmax[:, g, j, :], psA[:, i % BANKS, :].rearrange("p (t m) -> p t m", m=M),
                                                    axis=AX.X, op=ALU.max).then_inc(qmax_done, 1)
                            dve.wait_ge(qmax_done, L * 2 * STEPS + (2 * g + j + 1))
                            nc.vector.scalar_tensor_tensor(out=qbias[:, g, j, :], in0=qmax[:, g, j, :], scalar=-DN,
                                                           in1=ndiag[:, 0, 2 * s:2 * s + 2, 2 * pair + j], op0=ALU.mult,
                                                           op1=ALU.add).then_inc(qbias_ready, 1)
                        elif what == "tr":
                            ps = job("tr", g, j)
                            if g:
                                dve.wait_ge(v_full, v0 + (MIX_V[("at", g - 1, j)] + 1))
                            nc.vector.tensor_scalar(work[:, 2 + j, :], ps, EPS_K, None, ALU.add).then_inc(v_empty, 1)
                        else:
                            ps = job("at", g, j)[:, 0:2 * (DH + 1)].rearrange("p (t d) -> p t d", t=2)
                            nc.vector.reciprocal(rden[:, g, j, :], ps[:, :, DH * j]).then_inc(rden_done, 1)
                            dve.wait_ge(rden_done, L * 2 * STEPS + (2 * g + j + 1))
                            nc.vector.tensor_tensor(V[:, 2 * s:2 * s + 2, pair, 1 + DH * j:1 + DH * (j + 1)], ps[:, :, 1 - j:1 - j + DH],
                                                    rden[:, g, j, :].unsqueeze(2).to_broadcast([P, 2, DH]),
                                                    ALU.mult).then_inc(v_empty, 1)
                    if what == "ddq" and s == 0 and pair + 1 < NH // 2:
                        k_bias(pair + 1)
                for h in range(H):
                    for k in range(KT):
                        split_t(("o", h, k), hT, k, h)

                def onto_residual(name, t):
                    ps = job(*name)
                    nc.vector.tensor_tensor(Xm[:, t, :], ps, Xm[:, t, :], ALU.add).then_inc(v_empty, 1)

                dve.wait_ge(bias_added, L * 2 * NT + (NT + 1))
                for t in range(NT):
                    onto_residual(("wo", t), t)
                dve.wait_ge(v_empty, v0 + done(MIX_V[("wo", NT - 1)]))
                normalise(lambda t: Xm[:, t, :], nat, normed, L * 4, LN_MIX + 2)
                for h in range(H):
                    for k in range(KT):
                        split_t(("n2", h, k), hT, k, h)
                dve.wait_ge(bias_added, L * 2 * NT + (2 * NT + 1))
                for kind, c in FFN_ORDER:
                    if kind == "f":
                        for m in range(KT):
                            for h in range(H):
                                split_t(("f", c, m, h), fT[c % 2], m, h)
                    else:
                        if c:
                            dve.wait_ge(v_empty, v0 + done(MIX_V[("g", c - 1, NT - 1)]))
                        for t in range(NT):
                            onto_residual(("g", c, t), t)

            with dve.Fori(0, LAYERS) as L:
                mix_layer(L)

            dve.wait_ge(x_in, 2 * 16 * NT)
            dve.wait_ge(v_empty, done(V_BASE - 1))
            normalise(lambda t: nat[:, t, :], xg, normed, 0, LN_G)
            for n in range(H * KT):
                h, k = divmod(n, KT)
                split_block(SP_T + n, 0, hT[0][:, k, half(h)], hT[1][:, k, half(h)], after=done(GA_T + n))

            steps = [0]

            def then(instruction):
                steps[0] += 1
                instruction.then_inc(v_chain, 1)
                dve.wait_ge(v_chain, steps[0])

            dve.wait_ge(ends_in, 48)
            nc.vector.tensor_copy(ends_f[:], ends_i[:])
            nc.vector.memset(zeros[:], 0.0)
            then(nc.vector.tensor_scalar(block_i[:], ends_i[:, 1, :], 7, None, ALU.arith_shift_right))
            then(nc.vector.tensor_copy(block_f[:], block_i[:]))
            for r in range(2):
                for b in range(NT):
                    last = nc.vector.scalar_tensor_tensor(out=spans[:, r, b, :], in0=block_f[:], scalar=float(b),
                                                          in1=pair_no[:, r, :], op0=ALU.is_equal, op1=ALU.mult)
            then(last)
            nc.vector.tensor_reduce(span_p[:], spans[:], axis=AX.X, op=ALU.max).then_inc(span_ready, 1)
            dve.wait_ge(span_all, 1)
            first_, end_, count_, before_, base_ = (bound[:, n, :] for n in range(5))
            then(nc.vector.tensor_scalar(end_, span[:, 0, :], 1.0, None, ALU.max))
            then(nc.vector.tensor_scalar(first_, span[:, 1, :], -1.0, float(EP), ALU.mult, ALU.add))
            then(nc.vector.tensor_scalar(count_, end_, 1.0, None, ALU.subtract))
            then(nc.vector.tensor_tensor(first_, first_, count_, ALU.min))
            then(nc.vector.tensor_tensor(count_, end_, first_, ALU.subtract))
            then(nc.vector.memset(before_[:, 0:1], 0.0))
            for b in range(NT - 1):
                then(nc.vector.tensor_tensor(before_[:, b + 1:b + 2], before_[:, b:b + 1], count_[:, b:b + 1], ALU.add))
            then(nc.vector.tensor_tensor(base_, before_, first_, ALU.subtract))
            then(nc.vector.tensor_scalar(base_, base_, float(EP), None, ALU.add))
            then(nc.vector.tensor_copy(bound_i[:], bound[:]))
            nc.vector.engine_nop().then_inc(bounds_ready, 1)
            dve.sem_inc(hot_ready, 2 * EP)
            dve.sem_inc(hot_used, 2 * EP + 2)
            dve.sem_inc(adj_copied, 1)
            dve.sem_inc(adj_done, 2)
            with dve.Fori(0, NT) as g:
                first, end, base = pair_bounds(dve, g)
                with dve.Fori(first, end) as c:
                    for u in range(2):
                        dve.wait_ge(hot_used, (c + base) * 2 + (u + 1))
                        edge = c * 2 + u
                        nc.vector.tensor_scalar(hot_dst[:, u, :], iota[:, bass.ts(g, P)], ends_f[:, 1, bass.ds(edge, 1)],
                                                None, ALU.is_equal)
                        nc.vector.tensor_scalar(hot_src[:, u, :], iota[:], ends_f[:, 0, bass.ds(edge, 1)],
                                                None, ALU.is_equal).then_inc(hot_ready, 1)
                dve.wait_ge(adj_full, g + 1)
                nc.vector.tensor_scalar(adj_nat[:], psV[:, 0:2, :], 1.0, 0.0, ALU.mult, ALU.max,
                                        accum_out=most_b[:, bass.ds(g, 1)]).then_inc(adj_copied, 1)
                for s in range(2):
                    dve.wait_ge(adj_turned, g * 2 + (s + 1))
                    nc.vector.tensor_copy(adj[:, 4 * s:4 * s + 4, bass.ts(g, P)],
                                          psV[:, 2 + s, :].rearrange("p (a b) -> p a b", b=P)).then_inc(adj_done, 1)

            dve.wait_ge(adj_copied, NT + 1)
            nc.vector.tensor_reduce(most_p[:], most_b[:], axis=AX.X, op=ALU.max).then_inc(most_ready, 1)
            dve.wait_ge(most_all, 1)
            nc.vector.tensor_copy(most_i[:], most[:]).then_inc(most_loaded, 1)
            dve.wait_ge(bias_added, LAYERS * 2 * NT + NT + 1)
            with dve.Fori(0, LAYERS) as L:
                for t in range(NT):
                    i = GV + t
                    dve.wait_ge(v_full, L * NT + (i + 1))
                    nc.vector.tensor_copy(Pr[0][:, t, :], psV[:, i % BANKS, :]).then_inc(p_high, 1)
                    dve.wait_ge(p_high, L * NT + (t + 1))
                    nc.vector.tensor_tensor(Pr[1][:, t, :], psV[:, i % BANKS, :], Pr[0][:, t, :].bitcast(f32),
                                            ALU.subtract).then_inc(v_empty, 1)
                for n in range(2 * H * KT):
                    stage_, h, m = n // 8, n // KT % H, n % KT
                    dve.wait_ge(a_full, L * 16 + (GA + 8 * stage_ + KT * h + KT))
                    split_block(SP_G + n, L * 16, hT[0][:, m, half(h)], hT[1][:, m, half(h)],
                                after=L * 16 + done(GA + n))
            dve.wait_ge(split, done(SP_M - 1))
            for k in range(KT):
                nc.vector.tensor_tensor(hsum[:, k, :], hT[0][:, k, :].bitcast(f32), hT[1][:, k, :].bitcast(f32),
                                        ALU.add).then_inc(y_ready, 1)
            for t in range(NT):
                i = GV_X + t
                dve.wait_ge(v_full, i + 1)
                nc.vector.tensor_tensor(Xm[:, t, :], psV[:, i % BANKS, :], Xm[:, t, :], ALU.add).then_inc(v_empty, 1)

            dve.wait_ge(v_empty, done(MV_L - 1))
            normalise(lambda t: Xm[:, t, :], Xf, normed, 0, LN_M)
            for n in range(H * KT):
                h, k = divmod(n, KT)
                split_block(SP_M + n, 0, hT[0][:, k, half(h)], hT[1][:, k, half(h)], after=done(MA_T + n))

            dve.wait_ge(v_full, MV_L + 1)
            dve.wait_ge(split, done(SP_M + 7))
            nc.vector.tensor_copy(logit[:], psV[:, MV_L % BANKS, 0:NT * EXP].rearrange("p (t e) -> p t e", e=EXP)).then_inc(v_empty, 1)
            dve.wait_ge(v_empty, done(MV_L))
            for t in range(NT):
                last = nc.vector.max(best[:, t, :], logit[:, t, :])
            then(last)
            for t in range(NT):
                last = nc.vector.max_index(besti[:, t, :], best[:, t, :], logit[:, t, :])
            then(last)
            nc.vector.tensor_tensor(gate[:, 0, :], best[:, :, 1], best[:, :, 0], ALU.subtract).then_inc(gate_in, 1)
            then(nc.vector.tensor_copy(bestf[:], besti[:]))
            for q in range(2):
                for t in range(NT):
                    last = nc.vector.tensor_scalar(hot[:, q, t, :], iota8[:], bestf[:, t, q:q + 1], None, ALU.is_equal)
            then(last)
            dve.wait_ge(gate_exp, 1)
            then(nc.vector.tensor_scalar(gate[:, 2, :], gate[:, 1, :], 1.0, None, ALU.add))
            then(nc.vector.reciprocal(gate[:, 2, :], gate[:, 2, :]))
            then(nc.vector.tensor_tensor(gate[:, 3, :], gate[:, 1, :], gate[:, 2, :], ALU.mult))
            wide = lambda q: gate[:, 2 + q, :].unsqueeze(2).to_broadcast([P, NT, EXP])
            nc.vector.tensor_tensor(hotw[:], hot[:, 0, :, :], wide(0), ALU.mult)
            then(nc.vector.tensor_tensor(hot[:, 2, :, :], hot[:, 1, :, :], wide(1), ALU.mult))
            then(nc.vector.tensor_tensor(hot[:, 2, :, :], hot[:, 2, :, :], hotw[:], ALU.add))
            nc.vector.engine_nop().then_inc(hots_ready, 1)
            for q in range(3):
                for h in range(H):
                    i = MV_O + 2 * q + h
                    dve.wait_ge(v_full, i + 1)
                    nc.vector.tensor_copy(hotT[q][:, half(h)], psV[0:EXP, i % BANKS, :]).then_inc(v_empty, 1)
            dve.wait_ge(a_empty, done(MA_H + 3))
            for q in range(2):
                for m in range(2):
                    for h in range(H):
                        i = MV_R + 4 * q + 2 * m + h
                        dve.wait_ge(v_full, i + 1)
                        nc.vector.tensor_tensor(hm[q][:, m, half(h)], psV[:, i % BANKS, :], h1[:, m, half(h)],
                                                ALU.mult).then_inc(v_empty, 1)
            for q in range(2):
                for t in range(NT):
                    i = MV_Z + q * NT + t
                    dve.wait_ge(v_full, i + 1)
                    nc.vector.tensor_tensor(zz[q][:, t, :], psV[:, i % BANKS, :], Xf[:, t, :], ALU.add).then_inc(v_empty, 1)
                dve.wait_ge(v_empty, done(MV_Z + q * NT + NT - 1))
                columns = range(q * NT, (q + 1) * NT)
                statistics(lambda c: zz[q][:, c - q * NT, :], columns)
                aggregate(columns, LN_Y + q + 1)
            for q in range(2):
                dve.wait_ge(rstd_ready, LN_Y + q + 1)
                then(nc.vector.tensor_tensor(gscale[:, q, :], rstd[:, q * NT:(q + 1) * NT], gate[:, 2 + q, :], ALU.mult))
                for t in range(NT):
                    i, u = MV_G + q * NT + t, t % 2
                    then(nc.vector.tensor_scalar(ut[:, u, :], zz[q][:, t, :], mv[:, q * NT + t, 0:1], gscale[:, q, t:t + 1],
                                                 ALU.subtract, ALU.mult))
                    dve.wait_ge(v_full, i + 1)
                    nc.vector.tensor_tensor(ut[:, u, :], psV[:, i % BANKS, :], ut[:, u, :], ALU.mult).then_inc(v_empty, 1)
                    dve.wait_ge(v_empty, done(i))
                    then(nc.vector.tensor_tensor(Xm[:, t, :], Xm[:, t, :], ut[:, u, :], ALU.add))
            for t in range(NT):
                i = MV_G + 2 * NT + t
                dve.wait_ge(v_full, i + 1)
                nc.vector.tensor_tensor(Xm[:, t, :], psV[:, i % BANKS, :], Xm[:, t, :], ALU.add).then_inc(v_empty, 1)


def kernel(**inputs):
    import numpy as np
    import concourse.bacc as bacc
    from concourse.bass_utils import run_bass_kernel_spmd

    a = {k: np.asarray(v) for k, v in inputs.items()}
    g = lambda k: a["L0_gnn_" + k]
    m = lambda k: a["L0_mix_" + k]
    e = lambda k: a["L0_ffn_" + k]

    def slot(w):
        return w.reshape(PIECES, 2, P, 512).transpose(0, 2, 1, 3).reshape(PIECES, P, 1024)

    def columns(v):
        return v.reshape(-1, P).T

    slots = []
    for l in range(LAYERS):
        slots += [slot(m(n)[l]) for n in ("Wq", "Wk", "Wv", "Wo")]
        for kind, c in FFN_ORDER:
            piece = slice(512 * c, 512 * (c + 1))
            slots.append(slot(m("W1")[l][:, piece] if kind == "f" else m("W2")[l][piece, :]))
    w1 = e("w1").transpose(1, 0, 2).reshape(KT, P, EXP * EF).transpose(1, 0, 2).reshape(P, 1024)
    router = np.zeros((P, 1024), np.float32)
    router[:, :KT * EXP] = e("router_w").reshape(KT, P, EXP).transpose(1, 0, 2).reshape(P, KT * EXP)
    experts = np.stack([w1, router])
    for l in "12":
        slots += [slot(g(n + l).T) for n in ("W_rel", "W_root", "W_lin")] + [experts]
    hidden = np.arange(2 * P)
    data = {
        "x": a["x"],
        "ends_c": np.stack([a[n].reshape(EC, P).T for n in ("src", "dst")], axis=1),
        "wstream": np.stack(slots),
        "cols": np.stack([np.concatenate([columns(m(n)[l]) for n in ("ln1_s", "ln1_b", "bq", "bk", "ln2_s", "ln2_b", "b1")],
                                         axis=1) for l in range(LAYERS)]),
        "rows": np.stack([np.stack([m(n)[l] for n in ("bv", "bo", "b2")]) for l in range(LAYERS)]),
        "projt": np.stack([np.concatenate([m("proj")[l].T] * 2) for l in range(LAYERS)]),
        "gcols": np.concatenate([columns(g(n)) for n in ("b_rel1", "b_lin1", "b_rel2", "b_lin2")], axis=1),
        "b1col": columns(e("b1").reshape(-1)),
        "small": np.stack([e(n) for n in ("b2", "gamma", "beta")], axis=1),
        "w2": e("w2").reshape(2, P, D).transpose(1, 0, 2),
        "ident_c": np.eye(P, dtype=np.float32),
        "headmask_c": (np.arange(P)[:, None] // DH == np.arange(2)).astype(np.float32),
        "repl_c": (hidden // EF == np.arange(EXP)[:, None]).astype(np.float32),
        "iota_c": np.arange(N, dtype=np.float16),
        "pair_c": np.stack([np.arange(EC) // 2 + 1, EP - np.arange(EC) // 2]).astype(np.float32),
        "iota8_c": np.tile(np.arange(EXP, dtype=np.float32), (P, 1)),
    }
    nc = bacc.Bacc("TRN2", target_bir_lowering=False, num_devices=1)
    data = {n: np.ascontiguousarray(v) for n, v in data.items()}
    aps = {n: nc.dram_tensor(n, v.shape, mybir.dt.from_np(v.dtype), kind="ExternalInput").ap() for n, v in data.items()}
    out = nc.dram_tensor("out", (N, D), f32, kind="ExternalOutput").ap()
    build(nc, out=out, **aps)
    r = run_bass_kernel_spmd(nc, [data], core_ids=[0])
    return r.results[0]["out"]
```

```python
import concourse.bass as bass
from concourse import mybir
from contextlib import ExitStack

N, D, P = 1024, 512, 128
NT, KT = N // P, D // P
H = 2
NH, DH, M = 8, 64, 256
MT = M // P
E_TOT = 2 * 8192 + 1024
EC = E_TOT // P
GC = 4
EG = EC // GC
EXP, EF = 8, 32
FC = 4
LAYERS = 2
EPS_LN, EPS_MOE, EPS_K = 1e-5, 1e-6, 1e-4
DN = float(DH) ** -0.25
SLOTS, PIECES = 4, 2
MIX_SLOTS = 4 + 2 * FC
GNN_SLOTS = 4
N_SLOTS = LAYERS * MIX_SLOTS + LAYERS * GNN_SLOTS
BANKS = 4

f32, f32r = mybir.dt.float32, mybir.dt.float32r
bf16, f16, i32, u32 = mybir.dt.bfloat16, mybir.dt.float16, mybir.dt.int32, mybir.dt.uint32
RMAX = bass.bass_isa.ReduceOp.max
ALU, ACT, AX = mybir.AluOpType, mybir.ActivationFunctionType, mybir.AxisListType


def numbered(names):
    return {name: i for i, name in enumerate(names)}


STEPS = NH // 2 * (NT // 2)


def by_halves(product):
    return [(*product, m, h) for h in range(H) for m in range(KT)]


def normed_product(turned, product):
    blocks = by_halves(product)
    turns = [[(turned, h, k) for k in range(KT)] for h in range(H)]
    return turns[0] + blocks[:KT - 1] + turns[1] + blocks[KT - 1:]


QK_ORDER = normed_product("n1", ("q",)) + by_halves(("k",))
F0_ORDER = normed_product("n2", ("f", 0))
DIAG_ORDER = [name for name in QK_ORDER if name[0] != "n1"]
MIX_A = numbered(
    QK_ORDER
    + [("ddq", g, j) for g in range(STEPS) for j in range(2)]
    + [("o", h, k) for h in range(H) for k in range(KT)]
    + F0_ORDER
    + [block for c in range(1, FC) for block in by_halves(("f", c))]
)


def attention_order():
    for g in range(STEPS + 2):
        pair, s = divmod(g, NT // 2)
        if s == 0 and g < STEPS:
            yield "ctx", pair
            if pair + 1 < NH // 2:
                yield "ddk", pair + 1
        if g < STEPS:
            yield "ddq", g
        if 1 <= g <= STEPS:
            yield "tr", g - 1
        if g >= 2:
            yield "at", g - 2


def ring_v_attention():
    for what, g in attention_order():
        if what == "ddk":
            yield from (("ddk", g, s, j) for s in range(NT // 2) for j in range(2))
        elif what != "ddq":
            yield from ((what, g, j) for j in range(2))


FFN_ORDER = [("f", 0), ("f", 1), ("g", 0), ("f", 2), ("g", 1), ("f", 3), ("g", 2), ("g", 3)]
MIX_V = numbered(
    [("diag", name) for name in DIAG_ORDER]
    + [("ddk", 0, s, j) for s in range(NT // 2) for j in range(2)]
    + [("v", t) for t in range(NT)]
    + list(ring_v_attention())
    + [("wo", t) for t in range(NT)]
    + [("g", c, t) for c in range(FC) for t in range(NT)]
)
NA, NV = len(MIX_A), len(MIX_V)
assert NA % BANKS == 0 and NV % BANKS == 0
MIX_SPLIT = numbered([n for n in MIX_A if n[0] in ("n1", "o", "n2", "f")])
NS = len(MIX_SPLIT)
MIX_W = numbered(["q", "k", "v", "o"] + [w for w in FFN_ORDER])

GNN_A = numbered([(w, h, m) for w in ("g", "l") for h in range(H) for m in range(KT)])
GNN_V = numbered([("p", t) for t in range(NT)])


def build(nc, x, ends_c, wstream, cols, rows, projt, gcols, b1col, small, w2, ident_c, headmask_c,
          repl_c, iota_c, group_c, iota8_c, xt_d, out):
    ctx = ExitStack()
    with ctx:
        sem = lambda name: ctx.enter_context(nc.semaphore(name))
        sb = lambda name, shape, dt=f32: ctx.enter_context(nc.sbuf_tensor(name, shape, dt))

        ident = sb("ident", [P, P])
        iota8 = sb("iota8", [P, EXP])
        headmask = sb("headmask", [P, 2])
        proj_sb = sb("proj_sb", [P, M])
        col_sb = sb("col_sb", [P, 40])
        gcol_sb = sb("gcol_sb", [P, LAYERS * 8])
        b1_sb = sb("b1_sb", [P, 2])
        ndiag = sb("ndiag", [P, 2, NT, NH])
        stats = sb("stats", [P, NT, 6])
        mv = sb("mv", [P, 2 * NT, 2])
        vare = sb("vare", [P, 2 * NT])
        rstd = sb("rstd", [P, 2 * NT])
        nhalf = sb("nhalf", [P, 2 * NT])
        kmax = sb("kmax", [P, NH // 2, 2, NT // 2])
        kmax1 = sb("kmax1", [P, NH // 2, 2])
        kall = sb("kall", [P, NH // 2, 2])
        nkall = sb("nkall", [P, NH // 2, 2])
        kbias = sb("kbias", [P, NH // 2, 2, NT])
        qmax = sb("qmax", [P, 2, 2, 2])
        qbias = sb("qbias", [P, STEPS, 2, 2])
        rden = sb("rden", [P, 2, 2, 2])
        vsum = sb("vsum", [P, NH // 2, 2 * (DH + 1)])
        eps_k = sb("eps_k", [P, 1])
        ends_f = sb("ends_f", [P, 2, EC])
        span_p = sb("span_p", [P, 2, NT])
        span = sb("span", [P, 2, NT])
        bound = sb("bound", [P, 5, NT])
        bound_i = sb("bound_i", [P, 5, NT], i32)
        most_b = sb("most_b", [P, 2, NT])
        most_p = sb("most_p", [P, 1])
        most = sb("most", [P, 1])
        most_i = sb("most_i", [P, 1], i32)

        KB = 1024
        offs, top = {}, (nc.sbuf_base + 31) // 32 * 32
        for name, size in [("slots", 64 * KB), ("stage", 8 * KB), ("xm", 16 * KB), ("ht", 32 * KB), ("q", 16 * KB),
                           ("k", 16 * KB), ("v", 16 * KB + 256), ("nat", 16 * KB), ("work", 8 * KB), ("rows", 6 * KB),
                           ("ctx", 2 * KB + 32)]:
            offs[name] = top
            top += size
        assert top <= nc.sbuf_usable_end
        arena = sb("arena", [P, (top - offs["slots"]) // 4])
        at = lambda name, shape, dt, region, skip=0: nc.alloc_sbuf_tensor_at(name, shape, dt, offset=offs[region] + skip)
        Whi = at("w_hi", [P, SLOTS, KT, 512], f32r, "slots")
        Wlo = at("w_lo", [P, SLOTS, KT, 512], f32r, "slots", 32 * KB)
        stage = at("stage", [P, 2, 1024], f32, "stage")
        Xm = at("xm", [P, NT, D], f32, "xm")
        hT = at("ht_hi", [P, KT, N], f32r, "ht"), at("ht_lo", [P, KT, N], f32r, "ht", 16 * KB)
        qT = at("q_t", [P, KT, N], f32, "q")
        kT = at("k_t", [P, KT, N], f32, "k")
        V = at("v_sb", [P, NT, NH // 2, 2 * (DH + 1)], f32, "v")
        nat = at("nat", [P, NT, D], f32, "nat")
        nat1 = at("nat1", [P, NT, D], f32, "k")
        sq = at("sq", [P, 2, 512], f32, "nat")
        expk = at("expk", [P, 2, NT, M], f32, "nat")
        work = at("work", [P, 4, 512], f32, "work")
        rows_sb = at("rows_sb", [P, 3, D], f32, "rows")
        ctx_sb = at("ctx_sb", [P, 2, 2, MT, DH + 1], f32, "ctx")
        fT = [(at("f0_hi", [P, KT, N], f32r, "q"), at("f0_lo", [P, KT, N], f32r, "k")),
              (at("f1_hi", [P, KT, N], f32r, "v"), at("f1_lo", [P, KT, N], f32r, "v", 16 * KB))]
        xt = at("xt_hi", [P, KT, N], f32r, "slots", 16 * KB), at("xt_lo", [P, KT, N], f32r, "slots", 48 * KB)
        x_again = at("x_again", [P, NT, D], f32, "q")
        adj = at("adj", [P, NT, N], f32, "q")
        Pr = at("p_hi", [P, NT, D], f32r, "v"), at("p_lo", [P, NT, D], f32r, "v", 16 * KB)
        ends_i = at("ends_i", [P, 2, EC], i32, "q")
        block_i = at("block_i", [P, EC], i32, "q", 2 * EC * 4)
        block_f = at("block_f", [P, EC], f32, "q", 3 * EC * 4)
        group_no = at("group_no", [P, 2, EC], f32, "q", 4 * EC * 4)
        spans = at("spans", [P, 2, NT, EC], f32, "q", 6 * EC * 4)
        hot_src = at("hot_src", [P, GC, N], bf16, "work")
        iota = at("iota", [P, N], f16, "rows")
        hot_dst = at("hot_dst", [P, GC, P], bf16, "rows", 2 * KB)
        zeros = at("zeros", [P, P], bf16, "rows", 3 * KB)
        adj_nat = [at("adj_nat0", [P, 512], f32, "ctx"), at("adj_nat1", [P, 512], f32, "rows", 3 * KB + 256)]
        hsum = at("hsum", [P, KT, N], f32, "q")
        Xf = at("xf", [P, NT, D], f32, "k")
        h1 = at("h1", [P, 2, N], f32, "q")
        small_sb = at("small_sb", [EXP, 3, D], f32, "q", 8 * KB)
        repl = at("repl", [EXP, 2 * P], f32, "q", 14 * KB)
        hm = [at(f"hm{k}", [P, 2, N], f32, "v", 8 * KB * k) for k in range(2)]
        hotT = [at(f"hot_t{k}", [EXP, N], f32, "v", 16 * KB + 256 + 4 * KB * k) for k in range(3)]
        w2_sb = at("w2_sb", [P, 2, D], f32, "v", 28 * KB + 256)
        zz = [at(f"z{k}", [P, NT, D], f32, "ht", 16 * KB * k) for k in range(2)]
        logit = at("logit", [P, NT, EXP], f32, "work")
        best = at("best", [P, NT, 8], f32, "work", 256)
        besti = at("besti", [P, NT, 8], u32, "work", 512)
        bestf = at("bestf", [P, NT, 8], f32, "work", 768)
        hot = at("hot", [P, 3, NT, EXP], f32, "work", 1024)
        hotw = at("hotw", [P, NT, EXP], f32, "work", 1792)
        gate = at("gate", [P, 4, NT], f32, "work", 2048)
        gscale = at("gscale", [P, 2, NT], f32, "work", 3264)
        ut = at("ut", [P, 2, D], f32, "work", 4 * KB)

        psA = ctx.enter_context(nc.psum_tensor("ps_a", [P, BANKS, 512], f32))
        psV = ctx.enter_context(nc.psum_tensor("ps_v", [P, BANKS, 512], f32))

        a_full, a_empty = sem("a_full"), sem("a_empty")
        v_full, v_empty = sem("v_full"), sem("v_empty")
        consts_in, x_in, par_in, ends_in, iota_in = (sem(s) for s in
            ("consts_in", "x_in", "par_in", "ends_in", "iota_in"))
        xt_stored, xt_in = sem("xt_stored"), sem("xt_in")
        w_in = [sem("w_in0"), sem("w_in1")]
        w_split = sem("w_split")
        staged, split = sem("staged"), sem("split")
        sq_ready = sem("sq_ready")
        normed = sem("normed")
        var_ready, eps_added, rstd_ready = sem("var_ready"), sem("eps_added"), sem("rstd_ready")
        kmax_ready, kall_ready, kbias_ready = sem("kmax_ready"), sem("kall_ready"), sem("kbias_ready")
        expk_done, vsum_added = sem("expk_done"), sem("vsum_added")
        qbias_ready = sem("qbias_ready")
        bias_added = sem("bias_added")
        v_chain = sem("v_chain")
        p_chain = sem("p_chain")
        hot_ready, hot_used = sem("hot_ready"), sem("hot_used")
        span_ready, span_all, bounds_ready = sem("span_ready"), sem("span_all"), sem("bounds_ready")
        most_ready, most_all, most_loaded = sem("most_ready"), sem("most_all"), sem("most_loaded")
        zeros_ready = sem("zeros_ready")
        adj_full, adj_copied, adj_turned, adj_done = (sem(s) for s in
            ("adj_full", "adj_copied", "adj_turned", "adj_done"))
        gate_in, gate_exp = sem("gate_in"), sem("gate_exp")
        hots_ready, y_ready, stored = sem("hots_ready"), sem("y_ready"), sem("stored")
        rows_in, moe_in = sem("rows_in"), sem("moe_in")
        w_high, high, p_high = sem("w_high"), sem("high"), sem("p_high")
        held = sem("held")
        stats_done, x_normed, nkall_done = sem("stats_done"), sem("x_normed"), sem("nkall_done")
        qmax_done, rden_done, ends_done = sem("qmax_done"), sem("rden_done"), sem("ends_done")

        XT = H * KT
        A_BASE, V_BASE, S_BASE = XT + LAYERS * NA, LAYERS * NV, XT + LAYERS * NS
        GA = A_BASE
        MA_T = GA + LAYERS * 16
        MA_H = MA_T + H * KT
        GV = V_BASE
        GV_X = GV + LAYERS * NT
        MV_L = GV_X + NT
        MV_O = MV_L + 1
        MV_R = MV_O + 6
        MV_Z = MV_R + 8
        MV_G = MV_Z + 2 * NT
        SP_G = S_BASE
        SP_M = SP_G + LAYERS * 16
        NORM_X, NORM_MIX = 0, 2 * NT
        NORM_M = LAYERS * NORM_MIX + NT // 2
        LN_FIRST, LN_MIX, LN_M, LN_Y = 2, 4, 4 + 4 * LAYERS, 6 + 4 * LAYERS
        W_GNN = LAYERS * MIX_SLOTS

        def free(i):
            return i + 1

        def done(i):
            return i + (1 + BANKS)

        def hold(engine):
            engine.sem_inc(held, 1)

        def nodes(t):
            return slice(t * P, (t + 1) * P)

        def half(h):
            return slice(h * 512, (h + 1) * 512)

        def group_bounds(engine, b):
            load = lambda n, least, most: engine.value_load(bound_i[0:1, n, bass.ds(b, 1)], min_val=least, max_val=most)
            return load(0, 0, EG - 1), load(1, 1, EG), load(4, 0, (NT + 1) * EG)

        block = ctx.enter_context(nc.Block())

        @block.sync
        def _(sp):
            sp.dma_start(ends_i[:], ends_c).then_inc(ends_in, 16)
            sp.dma_start(group_no[:], group_c.partition_broadcast(P)).then_inc(ends_in, 16)
            sp.dma_start(ident[:], ident_c).then_inc(consts_in, 16)
            sp.dma_start(headmask[:], headmask_c).then_inc(consts_in, 16)
            sp.dma_start(gcol_sb[:], gcols).then_inc(consts_in, 16)
            sp.dma_start(b1_sb[:], b1col).then_inc(consts_in, 16)
            sp.dma_start(iota8[:], iota8_c).then_inc(consts_in, 16)

            for j in range(PIECES):
                sp.dma_start(stage[:, j, :], wstream[0, j]).then_inc(w_in[j], 16)

            def load(s):
                for j in range(PIECES):
                    sp.wait_ge(w_split, s * PIECES + (j - 1))
                    sp.dma_start(stage[:, j, :], wstream[s, j]).then_inc(w_in[j], 16)

            load(1)
            sp.wait_ge(split, done(XT - 1))
            for i in range(2):
                sp.dma_start(xt_d[i], xt[i][:].bitcast(f32)).then_inc(xt_stored, 16)
            with sp.Fori(2, N_SLOTS) as s:
                load(s)
            for t in range(NT):
                sp.wait_ge(v_empty, done(MV_G + 2 * NT + t))
                sp.dma_start(out[t * P:(t + 1) * P, :], Xm[:, t, :]).then_inc(stored, 16)
            sp.wait_ge(stored, 16 * NT)

        @block.tensor
        def _(pe):
            def mm3(ps, left, right, first, last):
                nc.tensor.matmul(ps, left[0], right[0], start=first, stop=False)
                nc.tensor.matmul(ps, left[0], right[1], start=False, stop=False)
                return nc.tensor.matmul(ps, left[1], right[0], start=False, stop=last)

            def part(tensors, k, columns):
                return tensors[0][:, k, columns], tensors[1][:, k, columns]

            def weight(slot, k, columns=slice(0, 512)):
                return Whi[:, slot, k, columns], Wlo[:, slot, k, columns]

            def bank_a(i, base=0):
                pe.wait_ge(a_empty, base + free(i))
                return psA[:, i % BANKS, :]

            def bank_v(i, base=0):
                pe.wait_ge(v_empty, base + free(i))
                return psV[:, i % BANKS, :]

            def turn(ps, sources, full):
                for n, source in enumerate(sources):
                    last = nc.tensor.transpose(ps[:, nodes(n)], source, ident[:])
                last.then_inc(full, 1)

            def into_t(w, right, m, h, ps):
                for k in range(KT):
                    last = mm3(ps, w(k, nodes(m)), part(right, k, half(h)), k == 0, k == KT - 1)
                return last

            def into_nat(w, left, t, ps):
                for k in range(KT):
                    last = mm3(ps, part(left, k, nodes(t)), w(k), k == 0, k == KT - 1)
                return last

            def slot_of(n):
                return lambda k, columns=slice(0, 512): weight(n, k, columns)

            pe.wait_ge(consts_in, 80)

            for n in range(XT):
                h, k = divmod(n, KT)
                if k == 0:
                    pe.wait_ge(x_normed, 4 * (h + 1))
                turn(bank_a(n), [Xm[:, 4 * h + i, nodes(k)] for i in range(4)], a_full)

            def mix_layer(L):
                a0, v0, s0 = L * NA + XT, L * NV, L * NS + XT

                def bank(ring, name):
                    return bank_a(MIX_A[name], a0) if ring == "a" else bank_v(MIX_V[name], v0)

                def written_a(name):
                    pe.wait_ge(a_empty, a0 + done(MIX_A[name]))

                def written_v(name):
                    pe.wait_ge(v_empty, v0 + done(MIX_V[name]))

                def weight_slot(name):
                    pe.wait_ge(w_split, L * (MIX_SLOTS * PIECES) + (MIX_W[name] + 1) * PIECES)
                    return slot_of(MIX_W[name] % SLOTS)

                def need_split(name):
                    pe.wait_ge(split, s0 + done(MIX_SPLIT[name]))

                def turn_normed(name):
                    which, h, k = name
                    source = nat1 if which == "n1" else nat
                    pe.wait_ge(normed, L * NORM_MIX + (NT * (which == "n2") + 4 * (h + 1)))
                    turn(bank("a", name), [source[:, 4 * h + n, nodes(k)] for n in range(4)], a_full)

                def diag(i):
                    ps = bank("v", ("diag", DIAG_ORDER[i]))
                    pe.wait_ge(sq_ready, L * 16 + (i + 1))
                    for n in range(4):
                        last = nc.tensor.matmul(ps[:, 2 * n:2 * n + 2], sq[:, i % 2, nodes(n)], headmask[:],
                                                start=True, stop=True)
                    last.then_inc(v_full, 1)

                products = 0
                for name in QK_ORDER:
                    if name[0] == "n1":
                        turn_normed(name)
                        continue
                    which, m, h = name
                    slot = weight_slot(which)
                    need_split(("n1", h, KT - 1))
                    into_t(slot, hT, m, h, bank("a", name)).then_inc(a_full, 1)
                    if products:
                        diag(products - 1)
                    products += 1
                diag(products - 1)

                pe.wait_ge(par_in, L * 32 + 32)

                def scores(source, pair, s, banks, full):
                    for n in range(2):
                        for j in range(2):
                            head = slice(DH * j, DH * (j + 1))
                            last = nc.tensor.matmul(banks[j][:, M * n:M * (n + 1)],
                                                    source[head, pair, nodes(2 * s + n)], proj_sb[head, :],
                                                    start=True, stop=True)
                            if n == 1:
                                last.then_inc(full, 1)

                def ddk(pair):
                    for s in range(NT // 2):
                        scores(kT, pair, s, [bank("v", ("ddk", pair, s, j)) for j in range(2)], v_full)

                written_a(("k", KT - 1, H - 1))
                ddk(0)
                slot = weight_slot("v")
                for t in range(NT):
                    into_nat(slot, hT, t, bank("v", ("v", t))).then_inc(v_full, 1)
                written_v(("v", NT - 1))

                for what, g in attention_order():
                    pair, s = divmod(g, NT // 2)
                    if what == "ddk":
                        ddk(g)
                    elif what == "ddq":
                        scores(qT, pair, s, [bank("a", ("ddq", g, j)) for j in range(2)], a_full)
                    else:
                        for j in range(2):
                            ps = bank("v", (what, g, j))
                            if what == "ctx":
                                pe.wait_ge(expk_done, L * NH * NT + (2 * g + j + 1) * NT)
                                if g == 0 and j == 0:
                                    pe.wait_ge(vsum_added, L * (NT - 1) + NT)
                                of_head = slice((DH + 1) * j, (DH + 1) * (j + 1))
                                for m in range(MT):
                                    context = ps[:, m * (DH + 1):(m + 1) * (DH + 1)]
                                    for t in range(NT):
                                        nc.tensor.matmul(context, expk[:, j, t, nodes(m)], V[:, t, g, of_head],
                                                         start=t == 0, stop=False)
                                    last = nc.tensor.matmul(context, eps_k[:].to_broadcast([P, P]), vsum[:, g, of_head],
                                                            start=False, stop=True)
                                last.then_inc(v_full, 1)
                            elif what == "tr":
                                written_a(("ddq", g, j))
                                turn(ps, [work[:, j, M * n + m * P:M * n + (m + 1) * P]
                                          for m in range(MT) for n in range(2)], v_full)
                            else:
                                written_v(("tr", g, j))
                                for n in range(2):
                                    for m in range(MT):
                                        last = nc.tensor.matmul(ps[:, n * (DH + 1):(n + 1) * (DH + 1)],
                                                                work[:, 2 + j, nodes(2 * m + n)],
                                                                ctx_sb[:, pair % 2, j, m, :],
                                                                start=m == 0, stop=m == MT - 1)
                                last.then_inc(v_full, 1)

                written_v(("at", STEPS - 1, 1))
                for h in range(H):
                    for k in range(KT):
                        turn(bank("a", ("o", h, k)), [V[:, 4 * h + n, k, 1:1 + P] for n in range(4)], a_full)
                slot = weight_slot("o")
                for t in range(NT):
                    need_split(("o", t // 4, KT - 1))
                    into_nat(slot, hT, t, bank("v", ("wo", t))).then_inc(v_full, 1)
                    if t == NT - 3:
                        for name in F0_ORDER[:KT]:
                            turn_normed(name)

                for kind, c in FFN_ORDER:
                    slot = weight_slot((kind, c))
                    if kind == "f":
                        for name in by_halves(("f", c)) if c else F0_ORDER[KT:]:
                            if name[0] == "n2":
                                turn_normed(name)
                                continue
                            _, _, m, h = name
                            need_split(("n2", h, KT - 1))
                            into_t(slot, hT, m, h, bank("a", name)).then_inc(a_full, 1)
                    else:
                        need_split(("f", c, KT - 1, H - 1))
                        for t in range(NT):
                            into_nat(slot, fT[c % 2], t, bank("v", ("g", c, t))).then_inc(v_full, 1)

            with pe.Fori(0, LAYERS) as L:
                mix_layer(L)

            pe.wait_ge(a_empty, done(A_BASE - 1))
            pe.wait_ge(bounds_ready, 1)
            pe.wait_ge(zeros_ready, 1)
            pe.wait_ge(iota_in, 16)
            pe.wait_ge(xt_in, 32)
            pe.wait_ge(w_split, (W_GNN + 1) * PIECES)
            for b in range(NT):
                first, end, base = group_bounds(pe, b)
                pe.wait_ge(adj_copied, b + 1)
                for s in range(2):
                    nc.tensor.matmul(psA[:, s, :], zeros[:], iota[:, half(s)], start=True, stop=False)
                with pe.Fori(first, end) as c:
                    for u in range(2):
                        pe.wait_ge(hot_ready, (c + base) * 2 + (u + 1))
                        for chunk in (2 * u, 2 * u + 1):
                            for s in range(2):
                                last = nc.tensor.matmul(psA[:, s, :], hot_dst[:, chunk, :], hot_src[:, chunk, half(s)],
                                                        start=False, stop=False)
                        last.then_inc(hot_used, 1)
                for s in range(2):
                    last = nc.tensor.matmul(psA[:, s, :], zeros[:], iota[:, half(s)], start=False, stop=True)
                last.then_inc(adj_full, 1)
                ps = bank_v(GV + b)
                for k in range(KT):
                    last = mm3(ps, part(hT, k, nodes(b)), weight(0, k), k == 0, k == KT - 1)
                last.then_inc(v_full, 1)
                pe.wait_ge(adj_copied, b + 2)
                pe.wait_ge(adj_done, b * 2 + 2)
                for s in range(2):
                    turn(psA[:, 2 + s, :], [adj_nat[s][:, nodes(n)] for n in range(4)], adj_turned)
            pe.wait_ge(adj_done, 2 * NT + 2)
            pe.wait_ge(most_loaded, 1)
            largest = pe.value_load(most_i[0:1, 0:1], min_val=0, max_val=E_TOT)

            with pe.Fori(0, LAYERS) as L:
                w0 = L * (GNN_SLOTS * PIECES)
                pe.wait_ge(w_split, w0 + (W_GNN + 2) * PIECES)
                for h in range(H):
                    for m in range(KT):
                        ps = bank_a(GA + h * KT + m, L * 16)
                        for k in range(KT - 1):
                            mm3(ps, weight(1, k, nodes(m)), part(hT, k, half(h)), k == 0, False)
                        pe.wait_ge(v_empty, L * NT + done(GV + NT - 1))
                        with pe.If(largest <= 4096):
                            for t in range(NT):
                                for i in range(2):
                                    nc.tensor.matmul(ps, Pr[i][:, t, nodes(m)], adj[:, t, half(h)].bitcast(f32r),
                                                     start=False, stop=False)
                        with pe.Else():
                            for t in range(NT):
                                for i in range(2):
                                    nc.tensor.matmul(ps, Pr[i][:, t, nodes(m)].bitcast(f32), adj[:, t, half(h)],
                                                     start=False, stop=False)
                        mm3(ps, weight(1, KT - 1, nodes(m)), part(hT, KT - 1, half(h)), False,
                            True).then_inc(a_full, 1)
                pe.wait_ge(w_split, w0 + (W_GNN + 3) * PIECES)
                for h in range(H):
                    pe.wait_ge(split, L * 16 + done(SP_G + KT * (h + 1) - 1))
                    for m in range(KT):
                        into_t(slot_of(2), hT, m, h, bank_a(GA + 8 + h * KT + m, L * 16)).then_inc(a_full, 1)
                with pe.If(L < LAYERS - 1):
                    pe.wait_ge(w_split, w0 + (W_GNN + GNN_SLOTS + 1) * PIECES)
                    pe.wait_ge(split, L * 16 + done(SP_G + 15))
                    for t in range(NT):
                        into_nat(slot_of(0), hT, t, bank_v(GV + NT + t, L * NT)).then_inc(v_full, 1)

            pe.wait_ge(y_ready, KT)
            for t in range(NT):
                turn(bank_v(GV_X + t), [hsum[:, k, nodes(t)] for k in range(KT)], v_full)

            for h in range(H):
                pe.wait_ge(normed, NORM_M + 4 * (h + 1))
                for k in range(KT):
                    turn(bank_a(MA_T + h * KT + k), [Xf[:, 4 * h + n, nodes(k)] for n in range(4)], a_full)
            x0 = GNN_SLOTS - 1
            w1 = [w[:, x0, 0:2, :].rearrange("p a b -> p (a b)").rearrange("p (k n) -> p k n", k=KT) for w in (Whi, Wlo)]
            router = [w[:, x0, 2, 0:KT * EXP].rearrange("p (k n) -> p k n", k=KT) for w in (Whi, Wlo)]
            pe.wait_ge(w_split, N_SLOTS * PIECES)
            pe.wait_ge(split, done(SP_M + 7))
            ps = bank_v(MV_L)
            for t in range(NT):
                for k in range(KT):
                    last = mm3(ps[:, t * EXP:(t + 1) * EXP], part(hT, k, nodes(t)), (router[0][:, k, :], router[1][:, k, :]),
                               k == 0, k == KT - 1)
            last.then_inc(v_full, 1)
            for m in range(2):
                for h in range(H):
                    ps = bank_a(MA_H + 2 * m + h)
                    for k in range(KT):
                        last = mm3(ps, part(w1, k, nodes(m)), part(hT, k, half(h)), k == 0, k == KT - 1)
                    last.then_inc(a_full, 1)
            pe.wait_ge(hots_ready, 1)
            for q in range(3):
                for h in range(H):
                    ps = bank_v(MV_O + 2 * q + h)
                    for n in range(4):
                        last = nc.tensor.transpose(ps[0:EXP, nodes(n)], hot[:, q, 4 * h + n, :], ident[:])
                    last.then_inc(v_full, 1)
            pe.wait_ge(moe_in, 48)
            pe.wait_ge(v_empty, done(MV_O + 5))
            for q in range(2):
                for m in range(2):
                    for h in range(H):
                        nc.tensor.matmul(bank_v(MV_R + 4 * q + 2 * m + h), repl[:, nodes(m)], hotT[q][:, half(h)],
                                         start=True, stop=True).then_inc(v_full, 1)
            for q in range(2):
                pe.wait_ge(v_empty, done(MV_R + 4 * q + 3))
                for t in range(NT):
                    ps = bank_v(MV_Z + q * NT + t)
                    for m in range(2):
                        nc.tensor.matmul(ps, hm[q][:, m, nodes(t)], w2_sb[:, m, :], start=m == 0, stop=False)
                    nc.tensor.matmul(ps, hotT[q][:, nodes(t)], small_sb[:, 0, :], start=False,
                                     stop=True).then_inc(v_full, 1)
            for q in range(3):
                for t in range(NT):
                    nc.tensor.matmul(bank_v(MV_G + q * NT + t), hotT[q][:, nodes(t)], small_sb[:, 1 + q // 2, :],
                                     start=True, stop=True).then_inc(v_full, 1)

        @block.scalar
        def _(act):
            act.sem_inc(a_empty, BANKS)
            for t in range(NT):
                act.dma_start(nat[:, t, :], x[t * P:(t + 1) * P, :]).then_inc(x_in, 16)

            def evacuate(i, n, base_a, base_s, func, own_wait=False, **how):
                act.wait_ge(a_full, base_a + (i + 1))
                act.wait_ge(split, base_s + free(n))
                if own_wait:
                    hold(act)
                nc.scalar.activation(work[:, n % 4, :], psA[:, i % BANKS, :], func, **how).then_inc(a_empty, 1)

            for n in range(XT):
                evacuate(n, n, 0, 0, ACT.Copy)

            def mix_layer(L):
                a0, s0, v0 = L * NA + XT, L * NS + XT, L * NV
                act.wait_ge(a_empty, a0 + BANKS)
                act.wait_ge(bias_added, L * 2 * NT + 1)
                act.wait_ge(v_empty, v0 + 1)
                act.dma_start(col_sb[:], cols[L]).then_inc(par_in, 16)
                act.dma_start(proj_sb[:], projt[L]).then_inc(par_in, 16)
                act.dma_start(rows_sb[:], rows[L].partition_broadcast(P)).then_inc(rows_in, 16)
                act.wait_ge(par_in, L * 32 + 32)

                def out(name, func, **how):
                    evacuate(MIX_A[name], MIX_SPLIT[name], a0, s0, func, **how)

                def column(n):
                    return col_sb[:, n:n + 1]

                n = 0
                for name in QK_ORDER:
                    if name[0] == "n1":
                        k = name[2]
                        out(name, ACT.Identity, scale=column(k), bias=column(4 + k))
                        continue
                    which, m, h = name
                    i, dest = MIX_A[name], qT if which == "q" else kT
                    bias = column(8 + 4 * (which == "k") + m)
                    act.wait_ge(a_full, a0 + (i + 1))
                    if n >= 2:
                        act.wait_ge(v_full, v0 + (MIX_V[("diag", DIAG_ORDER[n - 2])] + 1))
                    nc.scalar.activation(sq[:, n % 2, :], psA[:, i % BANKS, :], ACT.Square,
                                         bias=bias).then_inc(sq_ready, 1)
                    nc.scalar.activation(dest[:, m, half(h)], psA[:, i % BANKS, :],
                                         ACT.Identity, bias=bias).then_inc(a_empty, 1)
                    n += 1

                def exp_k(pair, first, last):
                    act.wait_ge(kbias_ready, L * (NH // 2) + (pair + 1))
                    for n in range(first, last):
                        j, t = divmod(n, NT)
                        nc.scalar.activation(expk[:, j, t, :], expk[:, j, t, :], ACT.Exp, scale=DN,
                                             bias=kbias[:, pair, j, t:t + 1]).then_inc(expk_done, 1)

                exp_k(0, 0, 2 * NT)
                for g in range(STEPS):
                    pair, s = divmod(g, NT // 2)
                    for j in range(2):
                        i = MIX_A[("ddq", g, j)]
                        act.wait_ge(qbias_ready, L * 2 * STEPS + (2 * g + j + 1))
                        if g:
                            act.wait_ge(v_full, v0 + (MIX_V[("tr", g - 1, j)] + 1))
                        for n in range(2):
                            last = nc.scalar.activation(work[:, j, M * n:M * (n + 1)],
                                                        psA[:, i % BANKS, M * n:M * (n + 1)], ACT.Exp, scale=DN,
                                                        bias=qbias[:, g, j, n:n + 1])
                        last.then_inc(a_empty, 1)
                    if s and pair + 1 < NH // 2:
                        exp_k(pair + 1, (0, 6, 11)[s - 1], (6, 11, 16)[s - 1])
                for h in range(H):
                    for k in range(KT):
                        out(("o", h, k), ACT.Copy)
                for c in range(FC):
                    for name in by_halves(("f", c)) if c else F0_ORDER:
                        if name[0] == "n2":
                            k = name[2]
                            out(name, ACT.Identity, scale=column(16 + k), bias=column(20 + k))
                        else:
                            out(name, ACT.Gelu_apprx_tanh, bias=column(24 + 4 * c + name[2]))

            with act.Fori(0, LAYERS) as L:
                mix_layer(L)

            def gbias(L, n):
                return gcol_sb[:, bass.ds(L * 8 + n, 1)]

            act.wait_ge(bias_added, LAYERS * 2 * NT + 1)
            act.dma_start(iota[:], iota_c.partition_broadcast(P)).then_inc(iota_in, 16)
            act.wait_ge(a_full, A_BASE)
            act.wait_ge(xt_stored, 32)
            for i in range(2):
                act.dma_start(hT[i][:].bitcast(f32), xt_d[i]).then_inc(xt_in, 16)
            act.wait_ge(v_full, V_BASE - NT)
            for t in range(NT):
                act.dma_start(x_again[:, t, :], x[t * P:(t + 1) * P, :]).then_inc(x_in, 16)
            act.sem_inc(adj_copied, 1)
            act.sem_inc(adj_done, 2)
            with act.Fori(0, NT) as b:
                act.wait_ge(adj_full, b + 1)
                hold(act)
                for s in range(2):
                    last = nc.scalar.activation(adj_nat[s][:], psA[:, s, :], ACT.Copy,
                                                accum_out=most_b[:, s, bass.ds(b, 1)])
                last.then_inc(adj_copied, 1)
                act.wait_ge(bias_added, LAYERS * 2 * NT + NT + 1)
                for s in range(2):
                    act.wait_ge(adj_turned, b * 2 + (s + 1))
                    hold(act)
                    nc.scalar.activation(adj[:, 4 * s:4 * s + 4, bass.ts(b, P)],
                                         psA[:, 2 + s, :].rearrange("p (a b) -> p a b", b=P), ACT.Copy).then_inc(adj_done, 1)
            with act.Fori(0, LAYERS) as L:
                for n in range(H * KT):
                    evacuate(GA + n, SP_G + n, L * 16, L * 16, ACT.Identity, True, bias=gbias(L, n % KT))
                for n in range(H * KT):
                    evacuate(GA + 8 + n, SP_G + 8 + n, L * 16, L * 16, ACT.Relu, True, bias=gbias(L, 4 + n % KT))
            act.wait_ge(v_full, MV_L)
            act.dma_start(small_sb[:], small).then_inc(moe_in, 16)
            act.dma_start(repl[:], repl_c).then_inc(moe_in, 16)
            act.dma_start(w2_sb[:], w2).then_inc(moe_in, 16)
            for n in range(H * KT):
                evacuate(MA_T + n, SP_M + n, 0, 0, ACT.Copy)
            for m in range(2):
                for h in range(H):
                    i = MA_H + 2 * m + h
                    act.wait_ge(a_full, i + 1)
                    nc.scalar.activation(h1[:, m, half(h)], psA[:, i % BANKS, :], ACT.Relu,
                                         bias=b1_sb[:, m:m + 1]).then_inc(a_empty, 1)
            act.wait_ge(gate_in, 1)
            nc.scalar.activation(gate[:, 1, :], gate[:, 0, :], ACT.Exp).then_inc(gate_exp, 1)

        @block.gpsimd
        def _(pool):
            pool.sem_inc(bias_added, 1)
            nc.gpsimd.memset(nhalf[:], -0.5).then_inc(p_chain, 1)
            pool.wait_ge(p_chain, 1)
            nc.gpsimd.memset(eps_k[:], EPS_K).then_inc(vsum_added, 1)

            def split_weight(s, slot, pieces=range(PIECES)):
                for j in pieces:
                    whole = slice(2 * j, 2 * j + 2)
                    hi, lo = (w[:, slot, whole, :].rearrange("p a b -> p (a b)") for w in (Whi, Wlo))
                    pool.wait_ge(w_in[j], s * 16 + 16)
                    hold(pool)
                    nc.gpsimd.tensor_copy(hi, stage[:, j, :]).then_inc(w_high, 1)
                    pool.wait_ge(w_high, s * PIECES + (j + 1))
                    nc.gpsimd.tensor_tensor(lo, stage[:, j, :], hi.bitcast(f32), ALU.subtract).then_inc(w_split, 1)

            def inverse_deviation(base, n, columns, eps=EPS_LN):
                pool.wait_ge(var_ready, base + (n + 1))
                hold(pool)
                nc.gpsimd.tensor_scalar(vare[:, columns], mv[:, columns, 1], eps, None, ALU.add).then_inc(eps_added, 1)
                pool.wait_ge(eps_added, base + (n + 1))
                nc.gpsimd.tensor_tensor(rstd[:, columns], vare[:, columns], nhalf[:, columns], ALU.pow).then_inc(rstd_ready, 1)

            def both_halves(base, n, eps=EPS_LN):
                for h in range(H):
                    inverse_deviation(base, n + h, slice(4 * h, 4 * h + 4), eps)

            pool.wait_ge(span_ready, 1)
            nc.gpsimd.partition_all_reduce(span[:].rearrange("p a b -> p (a b)"), span_p[:].rearrange("p a b -> p (a b)"),
                                           P, RMAX).then_inc(span_all, 1)
            split_weight(0, 0, [0])
            both_halves(0, 0)
            split_weight(0, 0, [1])
            both_halves(0, LN_FIRST)
            split_weight(1, 1)
            pool.wait_ge(xt_stored, 32)
            for n in range(2, 4):
                split_weight(n, n)

            def mix_layer(L):
                a0, v0 = L * NA + XT, L * NV
                w_base = L * MIX_SLOTS

                def load(n, last_user):
                    ring, name = last_user
                    if ring == "a":
                        pool.wait_ge(a_full, a0 + (MIX_A[name] + 1))
                    else:
                        pool.wait_ge(v_full, v0 + (MIX_V[name] + 1))
                    split_weight(w_base + n, n % SLOTS)

                def add_row(r, ready):
                    pool.wait_ge(rows_in, L * 16 + 16)
                    pool.wait_ge(normed, L * NORM_MIX + ready)
                    for t in range(NT):
                        nc.gpsimd.tensor_tensor(Xm[:, t, :], Xm[:, t, :], rows_sb[:, r, :], ALU.add).then_inc(bias_added, 1)

                add_row(1, NT)
                for pair in range(NH // 2):
                    pool.wait_ge(kmax_ready, L * (NH // 2) + (pair + 1))
                    hold(pool)
                    nc.gpsimd.partition_all_reduce(kall[:, pair, :], kmax1[:, pair, :], P, RMAX).then_inc(kall_ready, 1)
                    if pair == 0:
                        for t in range(1, NT):
                            pool.wait_ge(v_empty, v0 + done(MIX_V[("v", t)]))
                            if t > 1:
                                pool.wait_ge(vsum_added, L * (NT - 1) + t)
                            nc.gpsimd.tensor_tensor(vsum[:], V[:, 0, :, :] if t == 1 else vsum[:], V[:, t, :, :],
                                                    ALU.add).then_inc(vsum_added, 1)
                    if pair < 3:
                        load(4 + pair, (("a", ("q", KT - 1, H - 1)), ("a", ("k", KT - 1, H - 1)), ("v", ("v", NT - 1)))[pair])
                both_halves(L * 4, LN_MIX)
                add_row(2, 2 * NT)
                load(7, ("v", ("wo", NT - 1)))
                for n in range(8, 16):
                    kind, c = FFN_ORDER[n - 8]
                    if n == 15:
                        both_halves(L * 4, LN_MIX + 2)
                    load(n, ("a", ("f", c, KT - 1, H - 1)) if kind == "f" else ("v", ("g", c, NT - 1)))

            with pool.Fori(0, LAYERS) as L:
                mix_layer(L)

            pool.wait_ge(x_in, 2 * 16 * NT)
            pool.wait_ge(normed, NORM_M)
            pool.wait_ge(stats_done, LN_M)
            for t in range(NT):
                nc.gpsimd.tensor_tensor(Xm[:, t, :], Xm[:, t, :], x_again[:, t, :], ALU.add).then_inc(bias_added, 1)
            pool.wait_ge(most_ready, 1)
            nc.gpsimd.partition_all_reduce(most[:], most_p[:], P, RMAX).then_inc(most_all, 1)
            pool.wait_ge(v_full, GV + NT)
            split_weight(W_GNN + 4, 0)
            pool.wait_ge(a_full, GA + 8)
            split_weight(W_GNN + 5, 1)
            pool.wait_ge(a_full, GA + 16)
            split_weight(W_GNN + 6, 2)
            split_weight(W_GNN + 7, 3)
            both_halves(0, LN_M)
            for q in range(2):
                inverse_deviation(0, LN_Y + q, slice(NT * q, NT * (q + 1)), EPS_MOE)

        @block.vector
        def _(dve):
            dve.sem_inc(v_empty, BANKS)
            dve.sem_inc(split, BANKS)

            def statistics(source, columns, last_of=4):
                for t in columns:
                    last = nc.vector.bn_stats(stats[:, t % NT, :], source(t))
                    if (t + 1) % last_of == 0:
                        last.then_inc(stats_done, 1)

            def aggregate(columns, count):
                dve.wait_ge(stats_done, count)
                hold(dve)
                for t in columns:
                    last = nc.vector.bn_aggr(mv[:, t, :], stats[:, t % NT, :])
                last.then_inc(var_ready, 1)

            def half_tiles(h):
                return range(4 * h, 4 * h + 4)

            def deviations(source, base=0, n=0):
                for h in range(H):
                    statistics(source, half_tiles(h))
                    aggregate(half_tiles(h), base + (n + h + 1))

            def normalise_half(source, dest, sem_, h, base=0, n=0):
                dve.wait_ge(rstd_ready, base + (n + h + 1))
                for t in half_tiles(h):
                    nc.vector.tensor_scalar(dest[:, t, :], source(t), mv[:, t, 0:1], rstd[:, t:t + 1],
                                            ALU.subtract, ALU.mult).then_inc(sem_, 1)

            def normalise(source, dest, sem_, base=0, n=0):
                deviations(source, base, n)
                for h in range(H):
                    normalise_half(source, dest, sem_, h, base, n)

            def split_block(n, base, hi, lo, after=None):
                dve.wait_ge(a_empty, after)
                nc.vector.tensor_copy(hi, work[:, n % 4, :]).then_inc(high, 1)
                dve.wait_ge(high, base + (n + 1))
                nc.vector.tensor_tensor(lo, work[:, n % 4, :], hi.bitcast(f32), ALU.subtract).then_inc(split, 1)

            steps = [0]

            def then(instruction):
                steps[0] += 1
                instruction.then_inc(v_chain, 1)
                dve.wait_ge(v_chain, steps[0])

            dve.wait_ge(ends_in, 32)
            nc.vector.tensor_copy(ends_f[:], ends_i[:])
            then(nc.vector.tensor_scalar(block_i[:], ends_i[:, 1, :], 7, None, ALU.arith_shift_right))
            then(nc.vector.tensor_copy(block_f[:], block_i[:]))
            for r in range(2):
                for b in range(NT):
                    last = nc.vector.scalar_tensor_tensor(out=spans[:, r, b, :], in0=block_f[:], scalar=float(b),
                                                          in1=group_no[:, r, :], op0=ALU.is_equal, op1=ALU.mult)
            then(last)
            nc.vector.tensor_reduce(span_p[:], spans[:], axis=AX.X, op=ALU.max).then_inc(span_ready, 1)

            dve.wait_ge(x_in, 16 * NT)
            residual = lambda t: Xm[:, t, :]
            normalise(lambda t: nat[:, t, :], Xm, x_normed)
            dve.wait_ge(x_normed, NT)
            deviations(residual, 0, LN_FIRST)

            def split_input(h):
                for k in range(KT):
                    n = h * KT + k
                    split_block(n, 0, xt[0][:, k, half(h)], xt[1][:, k, half(h)], after=done(n))

            split_input(0)
            normalise_half(residual, nat1, normed, 0, 0, LN_FIRST)
            split_input(1)

            def mix_layer(L):
                a0, v0, s0 = L * NA + XT, L * NV, L * NS + XT

                def job(*name):
                    i = MIX_V[name]
                    dve.wait_ge(v_full, v0 + (i + 1))
                    return psV[:, i % BANKS, :]

                def split_t(name, tensors, k, h):
                    split_block(MIX_SPLIT[name], s0, tensors[0][:, k, half(h)], tensors[1][:, k, half(h)],
                                after=a0 + done(MIX_A[name]))

                for k in range(KT):
                    split_t(("n1", 0, k), hT, k, 0)
                normalise_half(residual, nat1, normed, 1, L * 4, LN_FIRST)

                def minus_half_norms(i):
                    which, m, h = DIAG_ORDER[i]
                    ps = job("diag", DIAG_ORDER[i])
                    nc.vector.tensor_scalar(ndiag[:, int(which == "k"), 4 * h:4 * h + 4, 2 * m:2 * m + 2],
                                            ps[:, 0:8].rearrange("p (t j) -> p t j", j=2), -0.5 * DN * DN, None,
                                            ALU.mult).then_inc(v_empty, 1)

                for i in range(2):
                    minus_half_norms(i)
                for k in range(KT):
                    split_t(("n1", 1, k), hT, k, 1)
                for i in range(2, len(DIAG_ORDER)):
                    minus_half_norms(i)

                def ddk(pair):
                    for s in range(NT // 2):
                        for j in range(2):
                            ps = job("ddk", pair, s, j)
                            nc.vector.tensor_scalar(expk[:, j, 2 * s:2 * s + 2, :],
                                                    ps.rearrange("p (t m) -> p t m", m=M), 1.0, -3.0e38, ALU.mult, ALU.max,
                                                    accum_out=kmax[:, pair, j, s:s + 1]).then_inc(v_empty, 1)
                    dve.wait_ge(v_empty, v0 + done(MIX_V[("ddk", pair, NT // 2 - 1, 1)]))
                    nc.vector.tensor_reduce(kmax1[:, pair, :], kmax[:, pair, :, :], axis=AX.X,
                                            op=ALU.max).then_inc(kmax_ready, 1)

                def k_bias(pair):
                    dve.wait_ge(kall_ready, L * (NH // 2) + (pair + 1))
                    nc.vector.tensor_scalar(nkall[:, pair, :], kall[:, pair, :], -DN, None, ALU.mult).then_inc(nkall_done, 1)
                    dve.wait_ge(nkall_done, L * (NH // 2) + (pair + 1))
                    for j in range(2):
                        last = nc.vector.tensor_scalar(kbias[:, pair, j, :], ndiag[:, 1, :, 2 * pair + j],
                                                       nkall[:, pair, j:j + 1], None, ALU.add)
                    last.then_inc(kbias_ready, 1)

                ddk(0)
                k_bias(0)
                dve.wait_ge(rows_in, L * 16 + 16)
                nc.vector.memset(V[:, :, :, 0:2 * DH + 2:2 * DH + 1], 1.0)
                for t in range(NT):
                    ps = job("v", t)
                    nc.vector.tensor_tensor(V[:, t, :, 1:1 + P], ps.rearrange("p (h d) -> p h d", d=P),
                                            rows_sb[:, 0, :].rearrange("p (h d) -> p h d", d=P), ALU.add).then_inc(v_empty, 1)

                for what, g in attention_order():
                    pair, s = divmod(g, NT // 2)
                    if what == "ddk":
                        ddk(g)
                        continue
                    for j in range(2):
                        if what == "ctx":
                            ps = job("ctx", g, j)
                            nc.vector.tensor_copy(ctx_sb[:, g % 2, j, :, :],
                                                  ps[:, 0:MT * (DH + 1)].rearrange("p (m d) -> p m d", m=MT)).then_inc(v_empty, 1)
                        elif what == "ddq":
                            i = MIX_A[("ddq", g, j)]
                            dve.wait_ge(a_full, a0 + (i + 1))
                            nc.vector.tensor_reduce(qmax[:, g % 2, j, :], psA[:, i % BANKS, :].rearrange("p (t m) -> p t m", m=M),
                                                    axis=AX.X, op=ALU.max).then_inc(qmax_done, 1)
                            dve.wait_ge(qmax_done, L * 2 * STEPS + (2 * g + j + 1))
                            nc.vector.scalar_tensor_tensor(out=qbias[:, g, j, :], in0=qmax[:, g % 2, j, :], scalar=-DN,
                                                           in1=ndiag[:, 0, 2 * s:2 * s + 2, 2 * pair + j], op0=ALU.mult,
                                                           op1=ALU.add).then_inc(qbias_ready, 1)
                        elif what == "tr":
                            ps = job("tr", g, j)
                            if g:
                                dve.wait_ge(v_full, v0 + (MIX_V[("at", g - 1, j)] + 1))
                            nc.vector.tensor_scalar(work[:, 2 + j, :], ps, EPS_K, None, ALU.add).then_inc(v_empty, 1)
                        else:
                            ps = job("at", g, j)[:, 0:2 * (DH + 1)].rearrange("p (t d) -> p t d", t=2)
                            nc.vector.reciprocal(rden[:, g % 2, j, :], ps[:, :, DH * j]).then_inc(rden_done, 1)
                            dve.wait_ge(rden_done, L * 2 * STEPS + (2 * g + j + 1))
                            nc.vector.tensor_tensor(V[:, 2 * s:2 * s + 2, pair, 1 + DH * j:1 + DH * (j + 1)], ps[:, :, 1 - j:1 - j + DH],
                                                    rden[:, g % 2, j, :].unsqueeze(2).to_broadcast([P, 2, DH]),
                                                    ALU.mult).then_inc(v_empty, 1)
                    if what == "ddq" and s == 0 and pair + 1 < NH // 2:
                        k_bias(pair + 1)
                for h in range(H):
                    for k in range(KT):
                        split_t(("o", h, k), hT, k, h)

                def onto_residual(name, t):
                    ps = job(*name)
                    nc.vector.tensor_tensor(Xm[:, t, :], ps, Xm[:, t, :], ALU.add).then_inc(v_empty, 1)

                def final_residual(name, t, n):
                    onto_residual(name, t)
                    dve.wait_ge(v_empty, v0 + done(MIX_V[name]))
                    statistics(residual, [t])
                    if t % 4 == 3:
                        aggregate(half_tiles(t // 4), L * 4 + (n + t // 4 + 1))

                dve.wait_ge(bias_added, L * 2 * NT + (NT + 1))
                for t in range(NT):
                    final_residual(("wo", t), t, LN_MIX)
                    if t == 4:
                        normalise_half(residual, nat, normed, 0, L * 4, LN_MIX)
                    if t == NT - 3:
                        for name in F0_ORDER[:KT]:
                            split_t(name, hT, name[2], 0)
                normalise_half(residual, nat, normed, 1, L * 4, LN_MIX)
                for kind, c in FFN_ORDER:
                    if kind == "f":
                        for name in by_halves(("f", c)) if c else F0_ORDER[KT:]:
                            if name[0] == "n2":
                                split_t(name, hT, name[2], 1)
                            else:
                                split_t(name, fT[c % 2], *name[2:])
                    else:
                        if c:
                            dve.wait_ge(v_empty, v0 + done(MIX_V[("g", c - 1, NT - 1)]))
                        else:
                            dve.wait_ge(bias_added, L * 2 * NT + (2 * NT + 1))
                        for t in range(NT):
                            if c < FC - 1:
                                onto_residual(("g", c, t), t)
                                continue
                            final_residual(("g", c, t), t, LN_MIX + 2)
                            if t == 5:
                                normalise_half(residual, nat1, normed, 0, L * 4, LN_MIX + 2)

            with dve.Fori(0, LAYERS) as L:
                mix_layer(L)

            dve.wait_ge(span_all, 1)
            first_, end_, count_, before_, base_ = (bound[:, n, :] for n in range(5))
            then(nc.vector.tensor_scalar(end_, span[:, 0, :], 1.0, None, ALU.max))
            then(nc.vector.tensor_scalar(first_, span[:, 1, :], -1.0, float(EG), ALU.mult, ALU.add))
            then(nc.vector.tensor_scalar(count_, end_, 1.0, None, ALU.subtract))
            then(nc.vector.tensor_tensor(first_, first_, count_, ALU.min))
            then(nc.vector.tensor_tensor(count_, end_, first_, ALU.subtract))
            then(nc.vector.memset(before_[:, 0:1], 0.0))
            for b in range(NT - 1):
                then(nc.vector.tensor_tensor(before_[:, b + 1:b + 2], before_[:, b:b + 1], count_[:, b:b + 1], ALU.add))
            then(nc.vector.tensor_tensor(base_, before_, first_, ALU.subtract))
            then(nc.vector.tensor_scalar(base_, base_, float(EG), None, ALU.add))
            then(nc.vector.tensor_copy(bound_i[:], bound[:]))
            nc.vector.engine_nop().then_inc(bounds_ready, 1)
            nc.vector.memset(zeros[:], 0.0).then_inc(zeros_ready, 1)
            dve.wait_ge(iota_in, 16)
            dve.sem_inc(hot_ready, 2 * EG)
            dve.sem_inc(hot_used, 2 * EG + 2)

            def take_p(t, i, base, p_base):
                dve.wait_ge(v_full, base + (i + 1))
                hold(dve)
                nc.vector.tensor_copy(Pr[0][:, t, :], psV[:, i % BANKS, :]).then_inc(p_high, 1)
                dve.wait_ge(p_high, p_base)
                nc.vector.tensor_tensor(Pr[1][:, t, :], psV[:, i % BANKS, :], Pr[0][:, t, :].bitcast(f32),
                                        ALU.subtract).then_inc(v_empty, 1)

            def one_hots(b):
                first, end, base = group_bounds(dve, b)
                with dve.Fori(first, end) as c:
                    for u in range(2):
                        dve.wait_ge(hot_used, (c + base) * 2 + (u + 1))
                        for chunk in (2 * u, 2 * u + 1):
                            edge = c * GC + chunk
                            nc.vector.tensor_scalar(hot_dst[:, chunk, :], iota[:, bass.ts(b, P)],
                                                    ends_f[:, 1, bass.ds(edge, 1)], None, ALU.is_equal)
                            last = nc.vector.tensor_scalar(hot_src[:, chunk, :], iota[:],
                                                           ends_f[:, 0, bass.ds(edge, 1)], None, ALU.is_equal)
                        last.then_inc(hot_ready, 1)

            one_hots(0)
            for b in range(1, NT):
                one_hots(b)
                take_p(b - 1, GV + b - 1, 0, b)
            take_p(NT - 1, GV + NT - 1, 0, NT)
            dve.wait_ge(adj_copied, NT + 1)
            nc.vector.tensor_reduce(most_p[:], most_b[:].rearrange("p a b -> p (a b)"), axis=AX.X,
                                    op=ALU.max).then_inc(most_ready, 1)
            dve.wait_ge(most_all, 1)
            nc.vector.tensor_copy(most_i[:], most[:]).then_inc(most_loaded, 1)
            with dve.Fori(0, LAYERS) as L:
                for n in range(2 * H * KT):
                    stage_, h, m = n // 8, n // KT % H, n % KT
                    dve.wait_ge(a_full, L * 16 + (GA + 8 * stage_ + KT * h + KT))
                    split_block(SP_G + n, L * 16, hT[0][:, m, half(h)], hT[1][:, m, half(h)],
                                after=L * 16 + done(GA + n))
                with dve.If(L < LAYERS - 1):
                    for t in range(NT):
                        take_p(t, GV + NT + t, L * NT, L * NT + (NT + t + 1))
            dve.wait_ge(split, done(SP_M - 1))
            for k in range(KT):
                nc.vector.tensor_tensor(hsum[:, k, :], hT[0][:, k, :].bitcast(f32), hT[1][:, k, :].bitcast(f32),
                                        ALU.add).then_inc(y_ready, 1)
            for t in range(NT):
                i = GV_X + t
                dve.wait_ge(v_full, i + 1)
                nc.vector.tensor_tensor(Xm[:, t, :], psV[:, i % BANKS, :], Xm[:, t, :], ALU.add).then_inc(v_empty, 1)

            dve.wait_ge(v_empty, done(MV_L - 1))
            normalise(lambda t: Xm[:, t, :], Xf, normed, 0, LN_M)
            for n in range(H * KT):
                h, k = divmod(n, KT)
                split_block(SP_M + n, 0, hT[0][:, k, half(h)], hT[1][:, k, half(h)], after=done(MA_T + n))

            dve.wait_ge(v_full, MV_L + 1)
            dve.wait_ge(split, done(SP_M + 7))
            nc.vector.tensor_copy(logit[:], psV[:, MV_L % BANKS, 0:NT * EXP].rearrange("p (t e) -> p t e", e=EXP)).then_inc(v_empty, 1)
            dve.wait_ge(v_empty, done(MV_L))
            for t in range(NT):
                last = nc.vector.max(best[:, t, :], logit[:, t, :])
            then(last)
            for t in range(NT):
                last = nc.vector.max_index(besti[:, t, :], best[:, t, :], logit[:, t, :])
            then(last)
            nc.vector.tensor_tensor(gate[:, 0, :], best[:, :, 1], best[:, :, 0], ALU.subtract).then_inc(gate_in, 1)
            then(nc.vector.tensor_copy(bestf[:], besti[:]))
            for q in range(2):
                for t in range(NT):
                    last = nc.vector.tensor_scalar(hot[:, q, t, :], iota8[:], bestf[:, t, q:q + 1], None, ALU.is_equal)
            then(last)
            dve.wait_ge(gate_exp, 1)
            then(nc.vector.tensor_scalar(gate[:, 2, :], gate[:, 1, :], 1.0, None, ALU.add))
            then(nc.vector.reciprocal(gate[:, 2, :], gate[:, 2, :]))
            then(nc.vector.tensor_tensor(gate[:, 3, :], gate[:, 1, :], gate[:, 2, :], ALU.mult))
            wide = lambda q: gate[:, 2 + q, :].unsqueeze(2).to_broadcast([P, NT, EXP])
            nc.vector.tensor_tensor(hotw[:], hot[:, 0, :, :], wide(0), ALU.mult)
            then(nc.vector.tensor_tensor(hot[:, 2, :, :], hot[:, 1, :, :], wide(1), ALU.mult))
            then(nc.vector.tensor_tensor(hot[:, 2, :, :], hot[:, 2, :, :], hotw[:], ALU.add))
            nc.vector.engine_nop().then_inc(hots_ready, 1)
            for q in range(3):
                for h in range(H):
                    i = MV_O + 2 * q + h
                    dve.wait_ge(v_full, i + 1)
                    nc.vector.tensor_copy(hotT[q][:, half(h)], psV[0:EXP, i % BANKS, :]).then_inc(v_empty, 1)
            dve.wait_ge(a_empty, done(MA_H + 3))
            for q in range(2):
                for m in range(2):
                    for h in range(H):
                        i = MV_R + 4 * q + 2 * m + h
                        dve.wait_ge(v_full, i + 1)
                        nc.vector.tensor_tensor(hm[q][:, m, half(h)], psV[:, i % BANKS, :], h1[:, m, half(h)],
                                                ALU.mult).then_inc(v_empty, 1)
            for q in range(2):
                for t in range(NT):
                    i = MV_Z + q * NT + t
                    dve.wait_ge(v_full, i + 1)
                    nc.vector.tensor_tensor(zz[q][:, t, :], psV[:, i % BANKS, :], Xf[:, t, :], ALU.add).then_inc(v_empty, 1)
                dve.wait_ge(v_empty, done(MV_Z + q * NT + NT - 1))
                columns = range(q * NT, (q + 1) * NT)
                statistics(lambda c: zz[q][:, c - q * NT, :], columns, NT)
                aggregate(columns, LN_Y + q + 1)
            for q in range(2):
                dve.wait_ge(rstd_ready, LN_Y + q + 1)
                then(nc.vector.tensor_tensor(gscale[:, q, :], rstd[:, q * NT:(q + 1) * NT], gate[:, 2 + q, :], ALU.mult))
                for t in range(NT):
                    i, u = MV_G + q * NT + t, t % 2
                    then(nc.vector.tensor_scalar(ut[:, u, :], zz[q][:, t, :], mv[:, q * NT + t, 0:1], gscale[:, q, t:t + 1],
                                                 ALU.subtract, ALU.mult))
                    dve.wait_ge(v_full, i + 1)
                    nc.vector.tensor_tensor(ut[:, u, :], psV[:, i % BANKS, :], ut[:, u, :], ALU.mult).then_inc(v_empty, 1)
                    dve.wait_ge(v_empty, done(i))
                    then(nc.vector.tensor_tensor(Xm[:, t, :], Xm[:, t, :], ut[:, u, :], ALU.add))
            for t in range(NT):
                i = MV_G + 2 * NT + t
                dve.wait_ge(v_full, i + 1)
                nc.vector.tensor_tensor(Xm[:, t, :], psV[:, i % BANKS, :], Xm[:, t, :], ALU.add).then_inc(v_empty, 1)


def kernel(**inputs):
    import numpy as np
    import concourse.bacc as bacc
    from concourse.bass_utils import run_bass_kernel_spmd

    a = {k: np.asarray(v) for k, v in inputs.items()}
    g = lambda k: a["L0_gnn_" + k]
    m = lambda k: a["L0_mix_" + k]
    e = lambda k: a["L0_ffn_" + k]

    def slot(w):
        return w.reshape(PIECES, 2, P, 512).transpose(0, 2, 1, 3).reshape(PIECES, P, 1024)

    def columns(v):
        return v.reshape(-1, P).T

    slots = []
    for l in range(LAYERS):
        slots += [slot(m(n)[l]) for n in ("Wq", "Wk", "Wv", "Wo")]
        for kind, c in FFN_ORDER:
            piece = slice(512 * c, 512 * (c + 1))
            slots.append(slot(m("W1")[l][:, piece] if kind == "f" else m("W2")[l][piece, :]))
    w1 = e("w1").transpose(1, 0, 2).reshape(KT, P, EXP * EF).transpose(1, 0, 2).reshape(P, 1024)
    router = np.zeros((P, 1024), np.float32)
    router[:, :KT * EXP] = e("router_w").reshape(KT, P, EXP).transpose(1, 0, 2).reshape(P, KT * EXP)
    experts = np.stack([w1, router])
    for l in "12":
        slots += [slot(g(n + l).T) for n in ("W_rel", "W_root", "W_lin")] + [experts]
    hidden = np.arange(2 * P)
    data = {
        "x": a["x"],
        "ends_c": np.stack([a[n].reshape(EC, P).T for n in ("src", "dst")], axis=1),
        "wstream": np.stack(slots),
        "cols": np.stack([np.concatenate([columns(m(n)[l]) for n in ("ln1_s", "ln1_b", "bq", "bk", "ln2_s", "ln2_b", "b1")],
                                         axis=1) for l in range(LAYERS)]),
        "rows": np.stack([np.stack([m(n)[l] for n in ("bv", "bo", "b2")]) for l in range(LAYERS)]),
        "projt": np.stack([np.concatenate([m("proj")[l].T] * 2) for l in range(LAYERS)]),
        "gcols": np.concatenate([columns(g(n)) for n in ("b_rel1", "b_lin1", "b_rel2", "b_lin2")], axis=1),
        "b1col": columns(e("b1").reshape(-1)),
        "small": np.stack([e(n) for n in ("b2", "gamma", "beta")], axis=1),
        "w2": e("w2").reshape(2, P, D).transpose(1, 0, 2),
        "ident_c": np.eye(P, dtype=np.float32),
        "headmask_c": (np.arange(P)[:, None] // DH == np.arange(2)).astype(np.float32),
        "repl_c": (hidden // EF == np.arange(EXP)[:, None]).astype(np.float32),
        "iota_c": np.arange(N, dtype=np.float16),
        "group_c": np.stack([np.arange(EC) // GC + 1, EG - np.arange(EC) // GC]).astype(np.float32),
        "iota8_c": np.tile(np.arange(EXP, dtype=np.float32), (P, 1)),
    }
    nc = bacc.Bacc("TRN2", target_bir_lowering=False, num_devices=1)
    data = {n: np.ascontiguousarray(v) for n, v in data.items()}
    aps = {n: nc.dram_tensor(n, v.shape, mybir.dt.from_np(v.dtype), kind="ExternalInput").ap() for n, v in data.items()}
    out = nc.dram_tensor("out", (N, D), f32, kind="ExternalOutput").ap()
    xt_d = nc.dram_tensor("xt_d", (2, P, KT, N), f32, kind="Internal").ap()
    build(nc, xt_d=xt_d, out=out, **aps)
    r = run_bass_kernel_spmd(nc, [data], core_ids=[0])
    return r.results[0]["out"]
```

```python
import concourse.bass as bass
from concourse import mybir
from contextlib import ExitStack

N, D, P = 1024, 512, 128
NT, KT = N // P, D // P
H = 2
NH, DH, M = 8, 64, 256
MT = M // P
E_TOT = 2 * 8192 + 1024
EC = E_TOT // P
GC = 4
EG = EC // GC
EXP, EF = 8, 32
SET = 32
FC = 4
LAYERS = 2
EPS_LN, EPS_MOE, EPS_K = 1e-5, 1e-6, 1e-4
DN = float(DH) ** -0.25
SLOTS, PIECES = 4, 2
MIX_SLOTS = 4 + 2 * FC
GNN_SLOTS = 4
HELPED = 2
N_SLOTS = LAYERS * MIX_SLOTS + LAYERS * GNN_SLOTS
BANKS = 4

f32, f32r = mybir.dt.float32, mybir.dt.float32r
bf16, f16, i32, u32 = mybir.dt.bfloat16, mybir.dt.float16, mybir.dt.int32, mybir.dt.uint32
RMAX = bass.bass_isa.ReduceOp.max
ALU, ACT, AX = mybir.AluOpType, mybir.ActivationFunctionType, mybir.AxisListType


def numbered(names):
    return {name: i for i, name in enumerate(names)}


STEPS = NH // 2 * (NT // 2)


def by_halves(product):
    return [(*product, m, h) for h in range(H) for m in range(KT)]


def normed_product(turned, product):
    blocks = by_halves(product)
    turns = [[(turned, h, k) for k in range(KT)] for h in range(H)]
    return turns[0] + blocks[:KT - 1] + turns[1] + blocks[KT - 1:]


F0_ORDER = normed_product("n2", ("f", 0))
N1_ORDER = [("n1", h, k) for h in range(H) for k in range(KT)]
QK_ORDER = by_halves(("k",)) + by_halves(("q",))
MIX_A = numbered(
    N1_ORDER + QK_ORDER
    + [("ddq", g, j) for g in range(STEPS) for j in range(2)]
    + [("o", h, k) for h in range(H) for k in range(KT)]
    + F0_ORDER
    + [block for c in range(1, FC) for block in by_halves(("f", c))]
)


def attention_order():
    for g in range(STEPS + 2):
        pair, s = divmod(g, NT // 2)
        if s == 0 and g < STEPS:
            yield "ctx", pair
            if pair + 1 < NH // 2:
                yield "ddk", pair + 1
        if g < STEPS:
            yield "ddq", g
        if 1 <= g <= STEPS:
            yield "tr", g - 1
        if g >= 2:
            yield "at", g - 2


def ddk_jobs(pair):
    return [("ddk", pair, s, j) for s in range(NT // 2) for j in range(2)]


def ring_v_attention():
    for what, g in attention_order():
        if what == "ddk":
            yield from ddk_jobs(g)
        elif what != "ddq":
            yield from ((what, g, j) for j in range(2))
            if (what, g) == ("ctx", 0):
                yield "turned", 3


FFN_ORDER = [("f", 0), ("f", 1), ("g", 0), ("f", 2), ("g", 1), ("f", 3), ("g", 2), ("g", 3)]
MIX_V = numbered(
    [("v", t) for t in range(NT)]
    + [("norm", 0), ("turned", 0), ("norm", 1)]
    + ddk_jobs(0)
    + [("turned", 1), ("norm", 2), ("turned", 2), ("norm", 3)]
    + list(ring_v_attention())
    + [("wo", t) for t in range(NT)]
    + [("g", c, t) for c in range(FC) for t in range(NT)]
)
NA, NV = len(MIX_A), len(MIX_V)
assert NA % BANKS == 0 and NV % BANKS == 0
MIX_SPLIT = numbered([n for n in MIX_A if n[0] in ("n1", "o", "n2", "f")])
NS = len(MIX_SPLIT)
MIX_W = numbered(["q", "v", "k", "o"] + FFN_ORDER)


def expert_order():
    for step in range(NT + NT // 2):
        if step < NT:
            yield from (("z", q, step) for q in range(2))
        if step >= NT // 2:
            yield from (("gamma", q, step - NT // 2) for q in range(2))
            yield "beta", step - NT // 2


EXPERT_V = numbered(
    ["logits"]
    + [("hot", h) for h in range(H)]
    + [("mask", q, m, h) for h in range(H) for q in range(2) for m in range(2)]
    + list(expert_order())
)


def build(nc, x, ends_c, wstream, cols, rows, projt, gcols, b1col, small, w2, ident_c, headmask_c,
          repl_c, iota_c, group_c, iota8_c, high_c, lin_row_c, xt_d, out):
    ctx = ExitStack()
    with ctx:
        sem = lambda name: ctx.enter_context(nc.semaphore(name))
        sb = lambda name, shape, dt=f32: ctx.enter_context(nc.sbuf_tensor(name, shape, dt))

        ident = sb("ident", [P, P])
        iota8 = sb("iota8", [P, 2 * EXP])
        high_rows = sb("high_rows", [3 * SET, 2])
        headmask = sb("headmask", [P, KT, NH])
        headmask_r = sb("headmask_r", [P, KT, NH], f32r)
        proj_r = sb("proj_hi", [P, M], f32r), sb("proj_lo", [P, M], f32r)
        col_sb = sb("col_sb", [P, 40])
        gcol_sb = sb("gcol_sb", [P, LAYERS * 8])
        b1_sb = sb("b1_sb", [P, 2])
        ndiag = sb("ndiag", [P, 2, NT, NH])
        stats = sb("stats", [P, NT, 6])
        mv = sb("mv", [P, 2 * NT, 2])
        vare = sb("vare", [P, 2 * NT])
        rstd = sb("rstd", [P, 2 * NT])
        nhalf = sb("nhalf", [P, 2 * NT])
        kmax = sb("kmax", [P, NH // 2, 2, NT // 2])
        kmax1 = sb("kmax1", [P, NH // 2, 2])
        kall = sb("kall", [P, NH // 2, 2])
        nkall = sb("nkall", [P, NH // 2, 2])
        kbias = sb("kbias", [P, NH // 2, 2, NT])
        qmax = sb("qmax", [P, 2, 2, 2])
        qbias = sb("qbias", [P, 4, 2, 2])
        rden = sb("rden", [P, 2, 2, 2])
        eps_k = sb("eps_k", [P, 1])
        ends_f = sb("ends_f", [P, 2, EC])
        span_p = sb("span_p", [P, 2, NT])
        span = sb("span", [P, 2, NT])
        bound = sb("bound", [P, 5, NT])
        bound_i = sb("bound_i", [P, 5, NT], i32)
        most_b = sb("most_b", [P, 2, NT])
        most_p = sb("most_p", [P, 1])
        most = sb("most", [P, 1])
        most_i = sb("most_i", [P, 1], i32)

        KB = 1024
        offs, top = {}, (nc.sbuf_base + 31) // 32 * 32
        for name, size in [("slots", 64 * KB), ("stage", 8 * KB), ("xm", 16 * KB), ("ht", 32 * KB), ("q", 16 * KB),
                           ("k", 16 * KB), ("v", 16 * KB + 256), ("nat", 16 * KB), ("work", 8 * KB), ("rows", 6 * KB + 32),
                           ("ctx", 2 * KB + 32)]:
            offs[name] = top
            top += size
        assert top <= nc.sbuf_usable_end
        arena = sb("arena", [P, (top - offs["slots"]) // 4])
        at = lambda name, shape, dt, region, skip=0: nc.alloc_sbuf_tensor_at(name, shape, dt, offset=offs[region] + skip)
        Whi = at("w_hi", [P, SLOTS, KT, 512], f32r, "slots")
        Wlo = at("w_lo", [P, SLOTS, KT, 512], f32r, "slots", 32 * KB)
        stage = at("stage", [P, 2, 1024], f32, "stage")
        Xm = at("xm", [P, NT, D], f32, "xm")
        hT = at("ht_hi", [P, KT, N], f32r, "ht"), at("ht_lo", [P, KT, N], f32r, "ht", 16 * KB)
        kS = [at(f"k_stacked{j}", [P, NH // 2, N], f32r, region) for j, region in enumerate("qk")]
        qS = [at(f"q_stacked{j}", [P, NH // 2, N], f32r, "slots", 8 * KB + 32 * KB * j) for j in range(2)]
        V = at("v_sb", [P, NT, NH // 2, 2 * (DH + 1)], f32, "v")
        nat = at("nat", [P, NT, D], f32, "nat")
        nat1 = at("nat1", [P, NT, D], f32, "k")
        sq = at("sq", [P, 2, 512], f32, "work")
        sq_lo = at("sq_lo", [P, 2, 512], f32r, "work")
        sq_hi = at("sq_hi", [P, 2, 512], f32r, "work", 4 * KB)
        norm_rows = at("norm_rows", [NH, 512], f32, "rows")
        expk = at("expk", [P, 2, NT, M], f32, "nat")
        work = at("work", [P, 4, 512], f32, "work")
        rows_sb = at("rows_sb", [P, 3, D], f32, "rows")
        vsum = at("vsum", [P, NH // 2, 2 * (DH + 1)], f32, "rows", 4 * KB)
        proj_sb = at("proj_sb", [P, M], f32, "ctx")
        ctx_sb = at("ctx_sb", [P, 2, 2, MT, DH + 1], f32, "ctx")
        fT = [(at("f0_hi", [P, KT, N], f32r, "q"), at("f0_lo", [P, KT, N], f32r, "k")),
              (at("f1_hi", [P, KT, N], f32r, "v"), at("f1_lo", [P, KT, N], f32r, "v", 16 * KB))]
        xt = at("xt_hi", [P, KT, N], f32r, "slots", 16 * KB), at("xt_lo", [P, KT, N], f32r, "slots", 48 * KB)
        x_again = at("x_again", [P, NT, D], f32, "q")
        adj = at("adj", [P, NT, N], f32, "q")
        Pr = at("p_hi", [P, NT, D], f32r, "v"), at("p_lo", [P, NT, D], f32r, "v", 16 * KB)
        ends_i = at("ends_i", [P, 2, EC], i32, "q")
        block_i = at("block_i", [P, EC], i32, "q", 2 * EC * 4)
        block_f = at("block_f", [P, EC], f32, "q", 3 * EC * 4)
        group_no = at("group_no", [P, 2, EC], f32, "q", 4 * EC * 4)
        spans = at("spans", [P, 2, NT, EC], f32, "q", 6 * EC * 4)
        hot_src = at("hot_src", [P, GC, N], bf16, "work")
        iota = at("iota", [P, N], f16, "rows")
        hot_dst = at("hot_dst", [P, GC, P], bf16, "rows", 2 * KB)
        zeros = at("zeros", [P, P], bf16, "rows", 3 * KB)
        adj_nat = [at("adj_nat0", [P, 512], f32, "ctx"), at("adj_nat1", [P, 512], f32, "rows", 3 * KB + 256)]
        lin_row = at("lin_row", [P, D], f32, "rows")
        lin_sum = at("lin_sum", [P, 2, D], f32, "rows", 2 * KB)
        Xf = at("xf", [P, NT, D], f32, "k")
        h1 = at("h1", [P, 2, N], f32, "q")
        small_sb = at("small_sb", [3 * SET, 2, D], f32, "slots")
        small_hi = at("small_hi", [3 * SET, 2, D], f32r, "slots", 4 * KB)
        small_lo = at("small_lo", [3 * SET, 2, D], f32, "slots", 8 * KB)
        small_r = at("small_r", [3 * SET, 2, D], f32r, "slots", 32 * KB)
        repl = at("repl", [2 * SET, 2 * P], f32, "slots", 36 * KB)
        repl_r = at("repl_r", [2 * SET, 2 * P], f32r, "slots", 37 * KB)
        logit_t = at("logit_t", [2 * EXP, N], f32, "slots", 40 * KB)
        hm = [at(f"hm{k}", [P, 2, N], f32, "v", 8 * KB * k) for k in range(2)]
        hotT = at("hot_t", [3 * SET, N], f32r, "v", 16 * KB + 256)
        w2_sb = at("w2_sb", [P, 2, D], f32, "v", 28 * KB + 256)
        zz = [at(f"z{k}", [P, NT, D], f32, "ht", 16 * KB * k) for k in range(2)]
        logit = at("logit", [P, NT, EXP], f32, "work")
        best = at("best", [P, NT, 8], f32, "work", 256)
        besti = at("besti", [P, NT, 8], u32, "work", 512)
        bestf = at("bestf", [P, NT, 8], f32, "work", 768)
        hot = at("hot", [P, NT, 3 * SET], f32, "stage")
        logit2 = at("logit2", [P, NT, 2 * EXP], f32, "stage", 4 * KB)
        gated = at("gated", [P, 2, NT, EXP], f32, "work", 1024)
        gated_hi = at("gated_hi", [P, NT, EXP], f32r, "work", 1536)
        gate = at("gate", [P, 4, NT], f32, "work", 2048)
        gscale = at("gscale", [P, 2 * NT], f32, "work", 3264)
        gshift = at("gshift", [P, 2 * NT], f32, "work", 3392)
        router_r = at("router_r", [P, KT, 2 * EXP], f32r, "ctx")
        ut = [at("ut0", [P, 2, D], f32, "work", 4 * KB), at("ut1", [P, 2, D], f32, "q", 8 * KB)]
        weighted = [at(f"weighted{n}", [P, 2, D], f32, "v", 20 * KB + 256 + 4 * KB * n) for n in range(2)]

        psA = ctx.enter_context(nc.psum_tensor("ps_a", [P, BANKS, 512], f32))
        psV = ctx.enter_context(nc.psum_tensor("ps_v", [P, BANKS, 512], f32))

        a_full, a_empty = sem("a_full"), sem("a_empty")
        v_full, v_empty = sem("v_full"), sem("v_empty")
        consts_in, x_in, par_in, ends_in, iota_in = (sem(s) for s in
            ("consts_in", "x_in", "par_in", "ends_in", "iota_in"))
        xt_stored, xt_in, xt_high = sem("xt_stored"), sem("xt_in"), sem("xt_high")
        w_in = [sem("w_in0"), sem("w_in1")]
        w_split = sem("w_split")
        split = sem("split")
        sq_ready, sq_summed = sem("sq_ready"), sem("sq_summed")
        sq_high, sq_split = sem("sq_high"), sem("sq_split")
        mask_ready, hi_ready, proj_split = sem("mask_ready"), sem("hi_ready"), sem("proj_split")
        normed = sem("normed")
        var_ready, eps_added, rstd_ready = sem("var_ready"), sem("eps_added"), sem("rstd_ready")
        kmax_ready, kall_ready, kbias_ready = sem("kmax_ready"), sem("kall_ready"), sem("kbias_ready")
        expk_done, vsum_added = sem("expk_done"), sem("vsum_added")
        qbias_ready = sem("qbias_ready")
        bias_added = sem("bias_added")
        v_chain = sem("v_chain")
        p_chain = sem("p_chain")
        hot_ready, hot_used = sem("hot_ready"), sem("hot_used")
        bound_step = sem("bound_step")
        span_ready, span_all, bounds_ready = sem("span_ready"), sem("span_all"), sem("bounds_ready")
        most_ready, most_all, most_loaded = sem("most_ready"), sem("most_all"), sem("most_loaded")
        zeros_ready = sem("zeros_ready")
        adj_full, adj_copied, adj_turned, adj_done = (sem(s) for s in
            ("adj_full", "adj_copied", "adj_turned", "adj_done"))
        gate_in, gate_exp = sem("gate_in"), sem("gate_exp")
        hots_ready, relu_done, summed, stored = sem("hots_ready"), sem("relu_done"), sem("summed"), sem("stored")
        small_step, lin_row_in = sem("small_step"), sem("lin_row_in")
        router_ready, scale_ready, shifted = sem("router_ready"), sem("scale_ready"), sem("shifted")
        rows_in, moe_in = sem("rows_in"), sem("moe_in")
        w_high, high, p_high = sem("w_high"), sem("high"), sem("p_high")
        held = sem("held")
        stats_done, x_normed, nkall_done = sem("stats_done"), sem("x_normed"), sem("nkall_done")
        qmax_done, rden_done = sem("qmax_done"), sem("rden_done")

        XT = H * KT
        A_BASE, V_BASE, S_BASE = XT + LAYERS * NA, LAYERS * NV, LAYERS * NS
        GA = A_BASE
        MA_T = [GA + LAYERS * 16 - 8 + 6 * h for h in range(H)]
        MA_R = [MA_T[1] + KT + h for h in range(H)]
        MA_H = [MA_T[0] + KT, MA_R[1] + 1]
        GV = V_BASE
        GV_X = GV + LAYERS * NT
        MV = GV_X + NT
        SP_G = S_BASE
        SP_M = SP_G + LAYERS * 16 - 8
        NORM_MIX = 2 * NT
        NORM_M = LAYERS * NORM_MIX + NT // 2
        LN_FIRST, LN_MIX, LN_M, LN_Y = 2, 4, 4 + 4 * LAYERS, 6 + 4 * LAYERS
        W_GNN = LAYERS * MIX_SLOTS

        def free(i):
            return i + 1

        def done(i):
            return i + (1 + BANKS)

        def hold(engine):
            engine.sem_inc(held, 1)

        def nodes(t):
            return slice(t * P, (t + 1) * P)

        def half(h):
            return slice(h * 512, (h + 1) * 512)

        def group_bounds(engine, b):
            load = lambda n, least, most: engine.value_load(bound_i[0:1, n, bass.ds(b, 1)], min_val=least, max_val=most)
            return load(0, 0, EG - 1), load(1, 1, EG), load(4, 0, (NT + 1) * EG)

        def expert_done(engine, *name):
            engine.wait_ge(v_empty, done(MV + EXPERT_V[name if len(name) > 1 else name[0]]))

        block = ctx.enter_context(nc.Block())

        @block.sync
        def _(sp):
            sp.dma_start(ends_i[:], ends_c).then_inc(ends_in, 16)
            sp.dma_start(group_no[:], group_c.partition_broadcast(P)).then_inc(ends_in, 16)
            sp.dma_start(ident[:], ident_c).then_inc(consts_in, 16)
            sp.dma_start(headmask[:], headmask_c).then_inc(consts_in, 16)
            sp.dma_start(gcol_sb[:], gcols).then_inc(consts_in, 16)
            sp.dma_start(b1_sb[:], b1col).then_inc(consts_in, 16)
            sp.dma_start(iota8[:], iota8_c).then_inc(consts_in, 16)
            sp.dma_start(high_rows[:], high_c).then_inc(consts_in, 16)

            for j in range(PIECES):
                sp.dma_start(stage[:, j, :], wstream[0, j]).then_inc(w_in[j], 16)

            def load(s):
                for j in range(PIECES):
                    sp.wait_ge(w_split, s * PIECES + (j - 1))
                    sp.dma_start(stage[:, j, :], wstream[s, j]).then_inc(w_in[j], 16)

            load(1)
            load(2)
            sp.wait_ge(a_empty, done(XT - 1))
            for i in range(2):
                sp.dma_start(xt_d[i], xt[i][:].bitcast(f32)).then_inc(xt_stored, 16)
            with sp.Fori(3, N_SLOTS) as s:
                load(s)
            for t in range(NT):
                sp.wait_ge(summed, t + 1)
                sp.dma_start(out[t * P:(t + 1) * P, :], Xm[:, t, :]).then_inc(stored, 16)
            sp.wait_ge(stored, 16 * NT)

        @block.tensor
        def _(pe):
            def mm3(ps, left, right, first, last):
                nc.tensor.matmul(ps, left[0], right[0], start=first, stop=False)
                nc.tensor.matmul(ps, left[0], right[1], start=False, stop=False)
                return nc.tensor.matmul(ps, left[1], right[0], start=False, stop=last)

            def part(tensors, k, columns):
                return tensors[0][:, k, columns], tensors[1][:, k, columns]

            def weight(slot, k, columns=slice(0, 512)):
                return Whi[:, slot, k, columns], Wlo[:, slot, k, columns]

            def bank_a(i, base=0):
                pe.wait_ge(a_empty, base + free(i))
                return psA[:, i % BANKS, :]

            def bank_v(i, base=0):
                pe.wait_ge(v_empty, base + free(i))
                return psV[:, i % BANKS, :]

            def turn(ps, sources, full):
                for n, source in enumerate(sources):
                    last = nc.tensor.transpose(ps[:, nodes(n)], source, ident[:])
                last.then_inc(full, 1)

            def into_t(w, right, m, h, ps):
                for k in range(KT):
                    last = mm3(ps, w(k, nodes(m)), part(right, k, half(h)), k == 0, k == KT - 1)
                return last

            def into_nat(w, left, t, ps):
                for k in range(KT):
                    last = mm3(ps, part(left, k, nodes(t)), w(k), k == 0, k == KT - 1)
                return last

            def slot_of(n):
                return lambda k, columns=slice(0, 512): weight(n, k, columns)

            pe.wait_ge(consts_in, 96)

            pe.wait_ge(mask_ready, 1)
            for n in range(XT):
                h, k = divmod(n, KT)
                if k == 0:
                    pe.wait_ge(x_normed, 4 * (h + 1))
                turn(bank_a(n), [Xm[:, 4 * h + i, nodes(k)] for i in range(4)], a_full)

            def mix_layer(L):
                a0, v0, s0 = L * NA + XT, L * NV, L * NS

                def bank(ring, name):
                    return bank_a(MIX_A[name], a0) if ring == "a" else bank_v(MIX_V[name], v0)

                def written_a(name):
                    pe.wait_ge(a_empty, a0 + done(MIX_A[name]))

                def written_v(name):
                    pe.wait_ge(v_empty, v0 + done(MIX_V[name]))

                def weight_slot(name):
                    pe.wait_ge(w_split, L * (MIX_SLOTS * PIECES) + (MIX_W[name] + 1) * PIECES)
                    return slot_of(MIX_W[name] % SLOTS)

                def need_split(name):
                    pe.wait_ge(split, s0 + done(MIX_SPLIT[name]))

                def turn_normed(name):
                    which, h, k = name
                    source = nat1 if which == "n1" else nat
                    pe.wait_ge(normed, L * NORM_MIX + (NT * (which == "n2") + 4 * (h + 1)))
                    turn(bank("a", name), [source[:, 4 * h + n, nodes(k)] for n in range(4)], a_full)

                def sum_squares(n):
                    _, m, h = QK_ORDER[n]
                    quarter = n // KT
                    if m == 0:
                        bank("v", ("norm", quarter))
                    ps = psV[0:NH, MIX_V[("norm", quarter)] % BANKS, :]
                    pe.wait_ge(sq_split, L * len(QK_ORDER) + (n + 1))
                    for i, squares in enumerate((sq_hi, sq_lo)):
                        last = nc.tensor.matmul(ps, headmask_r[:, m, :], squares[:, n % 2, :], start=m == 0 and i == 0,
                                                stop=m == KT - 1 and i == 1)
                    last.then_inc(*((v_full, 1) if m == KT - 1 else (sq_summed, 1)))

                def turn_norms(quarter):
                    ps = bank("v", ("turned", quarter))
                    hold(pe)
                    written_v(("norm", quarter))
                    hold(pe)
                    for n in range(4):
                        last = nc.tensor.transpose(ps[:, n * NH:(n + 1) * NH], norm_rows[:, nodes(n)], ident[0:NH, 0:NH])
                    last.then_inc(v_full, 1)

                def scores(source, pair, s, banks, full):
                    for n in range(2):
                        for j in range(2):
                            for i in range(2):
                                last = nc.tensor.matmul(banks[j][:, M * n:M * (n + 1)],
                                                        source[j][:, pair, nodes(2 * s + n)], proj_r[i][:],
                                                        start=i == 0, stop=i == 1)
                            if n == 1:
                                last.then_inc(full, 1)

                def ddk(pair):
                    for s in range(NT // 2):
                        scores(kS, pair, s, [bank("v", ("ddk", pair, s, j)) for j in range(2)], v_full)

                for name in N1_ORDER[:KT]:
                    turn_normed(name)
                slot = weight_slot("v")
                for t in range(NT):
                    need_split(("n1", t // 4, KT - 1))
                    into_nat(slot, hT, t, bank("v", ("v", t))).then_inc(v_full, 1)
                    if t == 2:
                        for name in N1_ORDER[KT:]:
                            turn_normed(name)
                for i, name in enumerate(QK_ORDER):
                    which, m, h = name
                    slot = weight_slot(which)
                    into_t(slot, hT, m, h, bank("a", name)).then_inc(a_full, 1)
                    if i:
                        sum_squares(i - 1)
                    if i in (5, 13):
                        turn_norms(i // 4 - 1)
                    if i == 8:
                        pe.wait_ge(proj_split, L * 2 + 2)
                        ddk(0)
                        turn_norms(1)
                sum_squares(len(QK_ORDER) - 1)

                for what, g in attention_order():
                    pair, s = divmod(g, NT // 2)
                    if what == "ddk":
                        ddk(g)
                    elif what == "ddq":
                        scores(qS, pair, s, [bank("a", ("ddq", g, j)) for j in range(2)], a_full)
                    else:
                        if what == "ctx":
                            written_a(("q", g, H - 1))
                        for j in range(2):
                            ps = bank("v", (what, g, j))
                            if what == "ctx":
                                pe.wait_ge(expk_done, L * NH * NT + (2 * g + j + 1) * NT)
                                if g == 0 and j == 0:
                                    pe.wait_ge(vsum_added, L * (NT - 1) + NT)
                                of_head = slice((DH + 1) * j, (DH + 1) * (j + 1))
                                for m in range(MT):
                                    context = ps[:, m * (DH + 1):(m + 1) * (DH + 1)]
                                    for t in range(NT):
                                        nc.tensor.matmul(context, expk[:, j, t, nodes(m)], V[:, t, g, of_head],
                                                         start=t == 0, stop=False)
                                    last = nc.tensor.matmul(context, eps_k[:].to_broadcast([P, P]), vsum[:, g, of_head],
                                                            start=False, stop=True)
                                last.then_inc(v_full, 1)
                            elif what == "tr":
                                written_a(("ddq", g, j))
                                turn(ps, [work[:, j, M * n + m * P:M * n + (m + 1) * P]
                                          for m in range(MT) for n in range(2)], v_full)
                            else:
                                written_v(("tr", g, j))
                                for n in range(2):
                                    for m in range(MT):
                                        last = nc.tensor.matmul(ps[:, n * (DH + 1):(n + 1) * (DH + 1)],
                                                                work[:, 2 + j, nodes(2 * m + n)],
                                                                ctx_sb[:, pair % 2, j, m, :],
                                                                start=m == 0, stop=m == MT - 1)
                                last.then_inc(v_full, 1)
                        if (what, g) == ("ctx", 0):
                            turn_norms(3)

                written_v(("at", STEPS - 1, 1))
                for h in range(H):
                    for k in range(KT):
                        turn(bank("a", ("o", h, k)), [V[:, 4 * h + n, k, 1:1 + P] for n in range(4)], a_full)
                slot = weight_slot("o")
                for t in range(NT):
                    need_split(("o", t // 4, KT - 1))
                    into_nat(slot, hT, t, bank("v", ("wo", t))).then_inc(v_full, 1)
                    if t == NT - 3:
                        for name in F0_ORDER[:KT]:
                            turn_normed(name)

                for kind, c in FFN_ORDER:
                    slot = weight_slot((kind, c))
                    if kind == "f":
                        for name in by_halves(("f", c)) if c else F0_ORDER[KT:]:
                            if name[0] == "n2":
                                turn_normed(name)
                                continue
                            _, _, m, h = name
                            need_split(("n2", h, KT - 1))
                            into_t(slot, hT, m, h, bank("a", name)).then_inc(a_full, 1)
                    else:
                        need_split(("f", c, KT - 1, H - 1))
                        for t in range(NT):
                            into_nat(slot, fT[c % 2], t, bank("v", ("g", c, t))).then_inc(v_full, 1)

            with pe.Fori(0, LAYERS) as L:
                mix_layer(L)

            pe.wait_ge(a_empty, done(A_BASE - 1))
            pe.wait_ge(bounds_ready, 1)
            pe.wait_ge(zeros_ready, 1)
            pe.wait_ge(iota_in, 16)
            pe.wait_ge(xt_in, 32)
            pe.wait_ge(w_split, (W_GNN + 1) * PIECES)
            for b in range(NT):
                first, end, base = group_bounds(pe, b)
                pe.wait_ge(adj_copied, b + 1)
                for s in range(2):
                    nc.tensor.matmul(psA[:, s, :], zeros[:], iota[:, half(s)], start=True, stop=False)
                with pe.Fori(first, end) as c:
                    for u in range(2):
                        pe.wait_ge(hot_ready, (c + base) * 2 + (u + 1))
                        for chunk in (2 * u, 2 * u + 1):
                            for s in range(2):
                                last = nc.tensor.matmul(psA[:, s, :], hot_dst[:, chunk, :], hot_src[:, chunk, half(s)],
                                                        start=False, stop=False)
                        last.then_inc(hot_used, 1)
                for s in range(2):
                    last = nc.tensor.matmul(psA[:, s, :], zeros[:], iota[:, half(s)], start=False, stop=True)
                last.then_inc(adj_full, 1)
                ps = bank_v(GV + b)
                for k in range(KT):
                    last = mm3(ps, part(hT, k, nodes(b)), weight(0, k), k == 0, k == KT - 1)
                last.then_inc(v_full, 1)
                pe.wait_ge(adj_copied, b + 2)
                pe.wait_ge(adj_done, b * 2 + 2)
                for s in range(2):
                    turn(psA[:, 2 + s, :], [adj_nat[s][:, nodes(n)] for n in range(4)], adj_turned)
            pe.wait_ge(adj_done, 2 * NT + 2)
            pe.wait_ge(most_loaded, 1)
            largest = pe.value_load(most_i[0:1, 0:1], min_val=0, max_val=E_TOT)

            with pe.Fori(0, LAYERS) as L:
                w0 = L * (GNN_SLOTS * PIECES)
                pe.wait_ge(w_split, w0 + (W_GNN + 2) * PIECES)
                for h in range(H):
                    for m in range(KT):
                        ps = bank_a(GA + h * KT + m, L * 16)
                        for k in range(KT - 1):
                            mm3(ps, weight(1, k, nodes(m)), part(hT, k, half(h)), k == 0, False)
                        pe.wait_ge(v_empty, L * NT + done(GV + NT - 1))
                        with pe.If(largest <= 4096):
                            for t in range(NT):
                                for i in range(2):
                                    nc.tensor.matmul(ps, Pr[i][:, t, nodes(m)], adj[:, t, half(h)].bitcast(f32r),
                                                     start=False, stop=False)
                        with pe.Else():
                            for t in range(NT):
                                for i in range(2):
                                    nc.tensor.matmul(ps, Pr[i][:, t, nodes(m)].bitcast(f32), adj[:, t, half(h)],
                                                     start=False, stop=False)
                        mm3(ps, weight(1, KT - 1, nodes(m)), part(hT, KT - 1, half(h)), False,
                            True).then_inc(a_full, 1)
                with pe.If(L < LAYERS - 1):
                    pe.wait_ge(w_split, w0 + (W_GNN + 3) * PIECES)
                    for h in range(H):
                        pe.wait_ge(split, L * 16 + done(SP_G + KT * (h + 1) - 1))
                        for m in range(KT):
                            into_t(slot_of(2), hT, m, h, bank_a(GA + 8 + h * KT + m, L * 16)).then_inc(a_full, 1)
                    pe.wait_ge(w_split, w0 + (W_GNN + GNN_SLOTS + 1) * PIECES)
                    for t in range(NT):
                        if t % 4 == 0:
                            pe.wait_ge(split, L * 16 + done(SP_G + 11 + t))
                        into_nat(slot_of(0), hT, t, bank_v(GV + NT + t, L * NT)).then_inc(v_full, 1)

            def turn_experts_input(h):
                pe.wait_ge(normed, NORM_M + 4 * (h + 1))
                for k in range(KT):
                    turn(bank_a(MA_T[h] + k), [Xf[:, 4 * h + n, nodes(k)] for n in range(4)], a_full)

            pe.wait_ge(w_split, (N_SLOTS - 1) * PIECES)
            for t in range(NT):
                if t % 4 == 0:
                    pe.wait_ge(split, done(SP_M - 8 + t + 3))
                into_nat(slot_of(2), hT, t, bank_v(GV_X + t)).then_inc(v_full, 1)
                if t == NT - 3:
                    turn_experts_input(0)

            x0 = GNN_SLOTS - 1
            w1 = [w[:, x0, 0:2, :].rearrange("p a b -> p (a b)").rearrange("p (k n) -> p k n", k=KT) for w in (Whi, Wlo)]

            def expert_bank(*name):
                return bank_v(MV + EXPERT_V[name if len(name) > 1 else name[0]])


            def hidden(h):
                pe.wait_ge(split, done(SP_M + KT * h + 3))
                for m in range(2):
                    ps = bank_a(MA_H[h] + m)
                    for k in range(KT):
                        last = mm3(ps, part(w1, k, nodes(m)), part(hT, k, half(h)), k == 0, k == KT - 1)
                    last.then_inc(a_full, 1)

            def route(h):
                ps = bank_a(MA_R[h])[0:2 * EXP, :]
                pe.wait_ge(split, done(SP_M + KT * h + 3))
                for i in range(2):
                    for k in range(KT):
                        last = nc.tensor.matmul(ps, router_r[:, k, :], hT[i][:, k, half(h)], start=i == 0 and k == 0,
                                                stop=i == 1 and k == KT - 1)
                last.then_inc(a_full, 1)

            pe.wait_ge(w_split, N_SLOTS * PIECES)
            pe.wait_ge(router_ready, 1)
            hidden(0)
            turn_experts_input(1)
            route(0)
            route(1)
            pe.wait_ge(a_empty, done(MA_R[1]))
            ps = expert_bank("logits")
            for t in range(NT):
                last = nc.tensor.transpose(ps[:, t * 2 * EXP:(t + 1) * 2 * EXP], logit_t[:, nodes(t)],
                                           ident[0:2 * EXP, 0:2 * EXP])
            last.then_inc(v_full, 1)
            hidden(1)
            pe.wait_ge(hots_ready, 1)
            for h in range(H):
                ps = expert_bank("hot", h)
                for n in range(4):
                    last = nc.tensor.transpose(ps[0:3 * SET, nodes(n)], hot[:, 4 * h + n, :], ident[:])
                last.then_inc(v_full, 1)
            pe.wait_ge(moe_in, 48)
            pe.wait_ge(small_step, 1)
            def rows_of(q, count=2 * EXP):
                return slice(SET * q, SET * q + count)

            for h in range(H):
                expert_done(pe, "hot", h)
                for q in range(2):
                    for m in range(2):
                        nc.tensor.matmul(expert_bank("mask", q, m, h), repl_r[rows_of(q, EXP), nodes(m)],
                                         hotT[rows_of(q, EXP), half(h)], start=True, stop=True).then_inc(v_full, 1)
            pe.wait_ge(small_step, 5)
            for what, *which in expert_order():
                t = which[-1]
                ps = expert_bank(what, *which)
                if what == "z":
                    q = which[0]
                    expert_done(pe, "mask", q, 1, t // 4)
                    for m in range(2):
                        nc.tensor.matmul(ps, hm[q][:, m, nodes(t)], w2_sb[:, m, :], start=m == 0, stop=False)
                    nc.tensor.matmul(ps, hotT[rows_of(q), nodes(t)], small_r[rows_of(q), 0, :], start=False,
                                     stop=True).then_inc(v_full, 1)
                elif what == "gamma":
                    q = which[0]
                    nc.tensor.matmul(ps, hotT[rows_of(q), nodes(t)], small_r[rows_of(q), 1, :], start=True,
                                     stop=True).then_inc(v_full, 1)
                else:
                    nc.tensor.matmul(ps, hotT[rows_of(2, 3 * EXP), nodes(t)], small_r[rows_of(2, 3 * EXP), 0, :],
                                     start=True, stop=True).then_inc(v_full, 1)

        @block.scalar
        def _(act):
            act.sem_inc(a_empty, BANKS)
            for t in range(NT):
                act.dma_start(nat[:, t, :], x[t * P:(t + 1) * P, :]).then_inc(x_in, 16)

            def evacuate(i, n, base_a, base_s, func, own_wait=False, **how):
                act.wait_ge(a_full, base_a + (i + 1))
                act.wait_ge(split, base_s + free(n))
                if own_wait:
                    hold(act)
                nc.scalar.activation(work[:, n % 4, :], psA[:, i % BANKS, :], func, **how).then_inc(a_empty, 1)

            def load_parameters(L):
                act.dma_start(col_sb[:], cols[L]).then_inc(par_in, 16)
                act.dma_start(proj_sb[:], projt[L]).then_inc(par_in, 16)
                act.dma_start(rows_sb[:], rows[L].partition_broadcast(P)).then_inc(rows_in, 16)

            load_parameters(0)
            for s in range(HELPED):
                for j in range(PIECES):
                    act.wait_ge(w_in[j], s * 16 + 16)
                    nc.scalar.activation(Whi[:, s, 2 * j:2 * j + 2, :].rearrange("p a b -> p (a b)"), stage[:, j, :],
                                         ACT.Copy).then_inc(w_high, 1)
            for n in range(XT):
                h, k = divmod(n, KT)
                act.wait_ge(a_full, n + 1)
                nc.scalar.activation(xt[0][:, k, half(h)], psA[:, n % BANKS, :], ACT.Copy).then_inc(xt_high, 1)
            act.wait_ge(a_empty, done(XT - 1))

            def mix_layer(L):
                a0, s0, v0 = L * NA + XT, L * NS, L * NV
                with act.If(L >= 1):
                    act.wait_ge(a_empty, a0 + BANKS)
                    act.wait_ge(bias_added, L * 2 * NT + 1)
                    act.wait_ge(v_empty, v0 + 1)
                    load_parameters(L)
                act.wait_ge(par_in, L * 32 + 32)

                def out(name, func, **how):
                    evacuate(MIX_A[name], MIX_SPLIT[name], a0, s0, func, **how)

                def column(n):
                    return col_sb[:, n:n + 1]

                for name in N1_ORDER:
                    k = name[2]
                    out(name, ACT.Identity, scale=column(k), bias=column(4 + k))
                act.wait_ge(split, s0 + done(MIX_SPLIT[N1_ORDER[-1]]))

                def exp_k(pair, first, last):
                    act.wait_ge(kbias_ready, L * (NH // 2) + (pair + 1))
                    for n in range(first, last):
                        j, t = divmod(n, NT)
                        nc.scalar.activation(expk[:, j, t, :], expk[:, j, t, :], ACT.Exp, scale=DN,
                                             bias=kbias[:, pair, j, t:t + 1]).then_inc(expk_done, 1)

                for n, name in enumerate(QK_ORDER):
                    which, m, h = name
                    i, dest = MIX_A[name], qS if which == "q" else kS
                    bias = column(8 + 4 * (which == "k") + m)
                    act.wait_ge(a_full, a0 + (i + 1))
                    if n >= 2:
                        if (n - 1) % KT:
                            act.wait_ge(sq_summed, L * 12 + (n - 1 - (n - 1) // KT))
                        else:
                            act.wait_ge(v_full, v0 + (MIX_V[("norm", (n - 2) // KT)] + 1))
                    nc.scalar.activation(sq[:, n % 2, :], psA[:, i % BANKS, :], ACT.Square,
                                         bias=bias).then_inc(sq_ready, 1)
                    for j in range(2):
                        head = slice(DH * j, DH * (j + 1))
                        last = nc.scalar.activation(dest[j][head, m, half(h)], psA[head, i % BANKS, :],
                                                    ACT.Identity, bias=bias[head, :])
                    last.then_inc(hi_ready, 1)
                    if n >= 10:
                        exp_k(0, (2 * NT * (n - 10) + 5) // 6, (2 * NT * (n - 9) + 5) // 6)
                for g in range(STEPS):
                    pair, s = divmod(g, NT // 2)
                    for j in range(2):
                        i = MIX_A[("ddq", g, j)]
                        act.wait_ge(qbias_ready, L * 2 * STEPS + (2 * g + j + 1))
                        if g:
                            act.wait_ge(v_full, v0 + (MIX_V[("tr", g - 1, j)] + 1))
                        for n in range(2):
                            last = nc.scalar.activation(work[:, j, M * n:M * (n + 1)],
                                                        psA[:, i % BANKS, M * n:M * (n + 1)], ACT.Exp, scale=DN,
                                                        bias=qbias[:, g % 4, j, n:n + 1])
                        last.then_inc(a_empty, 1)
                        if s and pair + 1 < NH // 2:
                            part_ = 2 * (s - 1) + j
                            exp_k(pair + 1, (2 * NT * part_ + 5) // 6, (2 * NT * (part_ + 1) + 5) // 6)
                for h in range(H):
                    for k in range(KT):
                        out(("o", h, k), ACT.Copy)
                for c in range(FC):
                    for name in by_halves(("f", c)) if c else F0_ORDER:
                        if name[0] == "n2":
                            k = name[2]
                            out(name, ACT.Identity, scale=column(16 + k), bias=column(20 + k))
                        else:
                            out(name, ACT.Gelu_apprx_tanh, bias=column(24 + 4 * c + name[2]))

            with act.Fori(0, LAYERS) as L:
                mix_layer(L)

            def gbias(L, n):
                return gcol_sb[:, bass.ds(L * 8 + n, 1)]

            act.wait_ge(bias_added, LAYERS * 2 * NT + 1)
            act.dma_start(iota[:], iota_c.partition_broadcast(P)).then_inc(iota_in, 16)
            act.wait_ge(a_full, A_BASE)
            act.wait_ge(xt_stored, 32)
            for i in range(2):
                act.dma_start(hT[i][:].bitcast(f32), xt_d[i]).then_inc(xt_in, 16)
            act.wait_ge(v_full, V_BASE - NT)
            for t in range(NT):
                act.dma_start(x_again[:, t, :], x[t * P:(t + 1) * P, :]).then_inc(x_in, 16)
            act.sem_inc(adj_copied, 1)
            act.sem_inc(adj_done, 2)
            with act.Fori(0, NT) as b:
                act.wait_ge(adj_full, b + 1)
                hold(act)
                for s in range(2):
                    last = nc.scalar.activation(adj_nat[s][:], psA[:, s, :], ACT.Copy,
                                                accum_out=most_b[:, s, bass.ds(b, 1)])
                last.then_inc(adj_copied, 1)
                act.wait_ge(bias_added, LAYERS * 2 * NT + NT + 1)
                for s in range(2):
                    act.wait_ge(adj_turned, b * 2 + (s + 1))
                    hold(act)
                    nc.scalar.activation(adj[:, 4 * s:4 * s + 4, bass.ts(b, P)],
                                         psA[:, 2 + s, :].rearrange("p (a b) -> p a b", b=P), ACT.Copy).then_inc(adj_done, 1)
            act.dma_start(lin_row[:], lin_row_c.partition_broadcast(P)).then_inc(lin_row_in, 16)
            with act.Fori(0, LAYERS) as L:
                for n in range(H * KT):
                    evacuate(GA + n, SP_G + n, L * 16, L * 16, ACT.Identity, True, bias=gbias(L, n % KT))
                with act.If(L < LAYERS - 1):
                    for n in range(H * KT):
                        evacuate(GA + 8 + n, SP_G + 8 + n, L * 16, L * 16, ACT.Relu, True, bias=gbias(L, 4 + n % KT))
            act.dma_start(small_sb[:], small).then_inc(moe_in, 16)
            act.dma_start(repl[:], repl_c).then_inc(moe_in, 16)
            act.dma_start(w2_sb[:], w2).then_inc(moe_in, 16)

            def hidden(h):
                for m in range(2):
                    i = MA_H[h] + m
                    act.wait_ge(a_full, i + 1)
                    nc.scalar.activation(h1[:, m, half(h)], psA[:, i % BANKS, :], ACT.Relu,
                                         bias=b1_sb[:, m:m + 1]).then_inc(a_empty, 1)

            for h in range(H):
                for k in range(KT):
                    evacuate(MA_T[h] + k, SP_M + KT * h + k, 0, 0, ACT.Copy)
                if h == 0:
                    hidden(0)
            for h in range(H):
                act.wait_ge(a_full, MA_R[h] + 1)
                nc.scalar.activation(logit_t[:, half(h)], psA[0:2 * EXP, MA_R[h] % BANKS, :], ACT.Copy).then_inc(a_empty, 1)
            act.wait_ge(gate_in, 1)
            nc.scalar.activation(gate[:, 1, :], gate[:, 0, :], ACT.Exp).then_inc(gate_exp, 1)
            hidden(1)
            for t in range(NT):
                act.wait_ge(scale_ready, t // 4 + 1)
                if t >= 2:
                    expert_done(act, "gamma", 1, t - 2)
                for q in range(2):
                    column = slice(2 * t + q, 2 * t + q + 1)
                    nc.scalar.activation(ut[t % 2][:, q, :], zz[q][:, t, :], ACT.Identity, scale=gscale[:, column],
                                         bias=gshift[:, column]).then_inc(shifted, 1)

        @block.gpsimd
        def _(pool):
            pool.sem_inc(bias_added, 1)
            nc.gpsimd.memset(nhalf[:], -0.5).then_inc(p_chain, 1)
            pool.wait_ge(p_chain, 1)
            nc.gpsimd.memset(eps_k[:], EPS_K).then_inc(vsum_added, 1)

            def low_weight(s, slot):
                for j in range(PIECES):
                    whole = slice(2 * j, 2 * j + 2)
                    hi, lo = (w[:, slot, whole, :].rearrange("p a b -> p (a b)") for w in (Whi, Wlo))
                    pool.wait_ge(w_high, s * PIECES + (j + 1))
                    nc.gpsimd.tensor_tensor(lo, stage[:, j, :], hi.bitcast(f32), ALU.subtract).then_inc(w_split, 1)

            def split_weight(s, slot, pieces=range(PIECES)):
                for j in pieces:
                    whole = slice(2 * j, 2 * j + 2)
                    hi, lo = (w[:, slot, whole, :].rearrange("p a b -> p (a b)") for w in (Whi, Wlo))
                    pool.wait_ge(w_in[j], s * 16 + 16)
                    hold(pool)
                    nc.gpsimd.tensor_copy(hi, stage[:, j, :]).then_inc(w_high, 1)
                    pool.wait_ge(w_high, s * PIECES + (j + 1))
                    nc.gpsimd.tensor_tensor(lo, stage[:, j, :], hi.bitcast(f32), ALU.subtract).then_inc(w_split, 1)

            def inverse_deviation(base, n, columns, eps=EPS_LN):
                pool.wait_ge(var_ready, base + (n + 1))
                hold(pool)
                nc.gpsimd.tensor_scalar(vare[:, columns], mv[:, columns, 1], eps, None, ALU.add).then_inc(eps_added, 1)
                pool.wait_ge(eps_added, base + (n + 1))
                nc.gpsimd.tensor_tensor(rstd[:, columns], vare[:, columns], nhalf[:, columns], ALU.pow).then_inc(rstd_ready, 1)

            def both_halves(base, n, eps=EPS_LN):
                for h in range(H):
                    inverse_deviation(base, n + h, slice(4 * h, 4 * h + 4), eps)

            low_weight(0, 0)
            both_halves(0, 0)
            for s in range(1, HELPED):
                low_weight(s, s)
            both_halves(0, LN_FIRST)
            pool.wait_ge(span_ready, 1)
            nc.gpsimd.partition_all_reduce(span[:].rearrange("p a b -> p (a b)"), span_p[:].rearrange("p a b -> p (a b)"),
                                           P, RMAX).then_inc(span_all, 1)
            pool.wait_ge(span_all, 1)
            bound_steps = [0]

            def then(instruction):
                bound_steps[0] += 1
                instruction.then_inc(bound_step, 1)
                pool.wait_ge(bound_step, bound_steps[0])

            first_, end_, count_, before_, base_ = (bound[:, n, :] for n in range(5))
            nc.gpsimd.tensor_scalar(end_, span[:, 0, :], 1.0, None, ALU.max)
            then(nc.gpsimd.tensor_scalar(count_, span[:, 0, :], 1.0, float(EG), ALU.min, ALU.mult))
            then(nc.gpsimd.tensor_tensor(first_, count_, span[:, 1, :], ALU.subtract))
            nc.gpsimd.memset(before_[:, 0:1], 0.0)
            then(nc.gpsimd.tensor_tensor(count_, end_, first_, ALU.subtract))
            for b in range(NT - 1):
                then(nc.gpsimd.tensor_tensor(before_[:, b + 1:b + 2], before_[:, b:b + 1], count_[:, b:b + 1], ALU.add))
            then(nc.gpsimd.tensor_tensor(base_, before_, first_, ALU.subtract))
            then(nc.gpsimd.tensor_scalar(base_, base_, float(EG), None, ALU.add))
            nc.gpsimd.tensor_copy(bound_i[:], bound[:]).then_inc(bounds_ready, 1)
            pool.wait_ge(xt_stored, 32)
            for n in range(2, 4):
                split_weight(n, n)

            def mix_layer(L):
                a0, v0 = L * NA + XT, L * NV
                w_base = L * MIX_SLOTS

                def load(n, last_user):
                    ring, name = last_user
                    if ring == "a":
                        pool.wait_ge(a_full, a0 + (MIX_A[name] + 1))
                    else:
                        pool.wait_ge(v_full, v0 + (MIX_V[name] + 1))
                    split_weight(w_base + n, n % SLOTS)

                def add_row(r, ready):
                    pool.wait_ge(rows_in, L * 16 + 16)
                    pool.wait_ge(normed, L * NORM_MIX + ready)
                    for t in range(NT):
                        nc.gpsimd.tensor_tensor(Xm[:, t, :], Xm[:, t, :], rows_sb[:, r, :], ALU.add).then_inc(bias_added, 1)

                add_row(2, NT)
                pool.wait_ge(bias_added, L * 2 * NT + (NT + 1))
                for t in range(1, NT):
                    pool.wait_ge(v_empty, v0 + done(MIX_V[("v", t)]))
                    if t > 1:
                        pool.wait_ge(vsum_added, L * (NT - 1) + t)
                    nc.gpsimd.tensor_tensor(vsum[:], V[:, 0, :, :] if t == 1 else vsum[:], V[:, t, :, :],
                                            ALU.add).then_inc(vsum_added, 1)
                for pair in range(NH // 2):
                    pool.wait_ge(kmax_ready, L * (NH // 2) + (pair + 1))
                    hold(pool)
                    nc.gpsimd.partition_all_reduce(kall[:, pair, :], kmax1[:, pair, :], P, RMAX).then_inc(kall_ready, 1)
                    if pair == 0:
                        load(4, ("a", QK_ORDER[-1]))
                load(5, ("a", ("ddq", STEPS - 1, 1)))
                both_halves(L * 4, LN_MIX)
                add_row(1, 2 * NT)
                load(6, ("a", ("ddq", STEPS - 1, 1)))
                load(7, ("v", ("wo", NT - 1)))
                for n in range(8, 16):
                    kind, c = FFN_ORDER[n - 8]
                    if n == 15:
                        both_halves(L * 4, LN_MIX + 2)
                    load(n, ("a", ("f", c, KT - 1, H - 1)) if kind == "f" else ("v", ("g", c, NT - 1)))

            with pool.Fori(0, LAYERS) as L:
                mix_layer(L)

            pool.wait_ge(x_in, 2 * 16 * NT)
            pool.wait_ge(normed, NORM_M)
            pool.wait_ge(stats_done, LN_M)
            for t in range(NT):
                nc.gpsimd.tensor_tensor(Xm[:, t, :], Xm[:, t, :], x_again[:, t, :], ALU.add).then_inc(bias_added, 1)
            pool.wait_ge(most_ready, 1)
            nc.gpsimd.partition_all_reduce(most[:], most_p[:], P, RMAX).then_inc(most_all, 1)
            pool.wait_ge(v_full, GV + NT)
            split_weight(W_GNN + 4, 0)
            pool.wait_ge(a_full, GA + 8)
            split_weight(W_GNN + 5, 1)
            pool.wait_ge(a_full, GA + 16)
            split_weight(W_GNN + 6, 2)
            split_weight(W_GNN + 7, 3)
            both_halves(0, LN_M)
            pool.wait_ge(moe_in, 48)
            pool.wait_ge(consts_in, 96)
            nc.gpsimd.tensor_copy(repl_r[:], repl[:]).then_inc(small_step, 1)
            nc.gpsimd.tensor_copy(small_hi[:], small_sb[:]).then_inc(small_step, 1)
            pool.wait_ge(small_step, 2)
            nc.gpsimd.tensor_tensor(small_lo[:], small_sb[:], small_hi[:].bitcast(f32), ALU.subtract).then_inc(small_step, 1)
            pool.wait_ge(small_step, 3)
            nc.gpsimd.tensor_scalar(small_lo[:], small_lo[:], high_rows[:, 1:2], None, ALU.mult)
            nc.gpsimd.tensor_scalar(small_hi[:].bitcast(f32), small_hi[:].bitcast(f32), high_rows[:, 0:1], None,
                                    ALU.mult).then_inc(small_step, 1)
            pool.wait_ge(small_step, 4)
            nc.gpsimd.tensor_tensor(small_r[:], small_hi[:].bitcast(f32), small_lo[:], ALU.add).then_inc(small_step, 1)

            def add_experts(t):
                expert_done(pool, "gamma", 1, t)
                both = weighted[t % 2]
                nc.gpsimd.tensor_tensor(both[:, 0, :], both[:, 0, :], both[:, 1, :], ALU.add).then_inc(p_chain, 1)
                pool.wait_ge(p_chain, t + 2)
                expert_done(pool, "beta", t)
                nc.gpsimd.tensor_tensor(Xm[:, t, :], Xm[:, t, :], both[:, 0, :], ALU.add).then_inc(summed, 1)

            inverse_deviation(0, LN_Y, slice(0, NT), EPS_MOE)
            for t in range(3):
                add_experts(t)
            inverse_deviation(0, LN_Y + 1, slice(NT, 2 * NT), EPS_MOE)
            for t in range(3, NT):
                add_experts(t)

        @block.vector
        def _(dve):
            dve.sem_inc(v_empty, BANKS)
            dve.sem_inc(split, BANKS)

            def statistics(source, columns, last_of=4):
                for t in columns:
                    last = nc.vector.bn_stats(stats[:, t % NT, :], source(t))
                    if (t + 1) % last_of == 0:
                        last.then_inc(stats_done, 1)

            def aggregate(columns, count):
                dve.wait_ge(stats_done, count)
                hold(dve)
                for t in columns:
                    last = nc.vector.bn_aggr(mv[:, t, :], stats[:, t % NT, :])
                last.then_inc(var_ready, 1)

            def half_tiles(h):
                return range(4 * h, 4 * h + 4)

            def deviations(source, base=0, n=0):
                for h in range(H):
                    statistics(source, half_tiles(h))
                    aggregate(half_tiles(h), base + (n + h + 1))

            def normalise_half(source, dest, sem_, h, base=0, n=0):
                dve.wait_ge(rstd_ready, base + (n + h + 1))
                for t in half_tiles(h):
                    nc.vector.tensor_scalar(dest[:, t, :], source(t), mv[:, t, 0:1], rstd[:, t:t + 1],
                                            ALU.subtract, ALU.mult).then_inc(sem_, 1)

            def normalise(source, dest, sem_, base=0, n=0):
                deviations(source, base, n)
                for h in range(H):
                    normalise_half(source, dest, sem_, h, base, n)

            def split_block(n, base, hi, lo, after=None):
                dve.wait_ge(a_empty, after)
                nc.vector.tensor_copy(hi, work[:, n % 4, :]).then_inc(high, 1)
                dve.wait_ge(high, base + (n + 1))
                nc.vector.tensor_tensor(lo, work[:, n % 4, :], hi.bitcast(f32), ALU.subtract).then_inc(split, 1)

            steps = [0]

            def then(instruction):
                steps[0] += 1
                instruction.then_inc(v_chain, 1)
                dve.wait_ge(v_chain, steps[0])

            dve.wait_ge(ends_in, 32)
            nc.vector.tensor_copy(ends_f[:], ends_i[:])
            then(nc.vector.tensor_scalar(block_i[:], ends_i[:, 1, :], 7, None, ALU.arith_shift_right))
            then(nc.vector.tensor_copy(block_f[:], block_i[:]))
            for r in range(2):
                for b in range(NT):
                    last = nc.vector.scalar_tensor_tensor(out=spans[:, r, b, :], in0=block_f[:], scalar=float(b),
                                                          in1=group_no[:, r, :], op0=ALU.is_equal, op1=ALU.mult)
            then(last)
            nc.vector.tensor_reduce(span_p[:], spans[:], axis=AX.X, op=ALU.max).then_inc(span_ready, 1)
            dve.wait_ge(consts_in, 96)
            nc.vector.tensor_copy(headmask_r[:], headmask[:]).then_inc(mask_ready, 1)

            dve.wait_ge(x_in, 16 * NT)
            residual = lambda t: Xm[:, t, :]
            normalise(lambda t: nat[:, t, :], Xm, x_normed)
            dve.wait_ge(x_normed, NT)
            deviations(residual, 0, LN_FIRST)

            def split_input(h):
                for k in range(KT):
                    n = h * KT + k
                    dve.wait_ge(xt_high, n + 1)
                    nc.vector.tensor_tensor(xt[1][:, k, half(h)], psA[:, n % BANKS, :],
                                            xt[0][:, k, half(h)].bitcast(f32), ALU.subtract).then_inc(a_empty, 1)

            split_input(0)
            normalise_half(residual, nat1, normed, 0, 0, LN_FIRST)
            split_input(1)

            def mix_layer(L):
                a0, v0, s0 = L * NA + XT, L * NV, L * NS

                def job(*name):
                    i = MIX_V[name]
                    dve.wait_ge(v_full, v0 + (i + 1))
                    return psV[:, i % BANKS, :]

                def split_t(name, tensors, k, h):
                    split_block(MIX_SPLIT[name], s0, tensors[0][:, k, half(h)], tensors[1][:, k, half(h)],
                                after=a0 + done(MIX_A[name]))

                for k in range(KT):
                    split_t(("n1", 0, k), hT, k, 0)
                normalise_half(residual, nat1, normed, 1, L * 4, LN_FIRST)
                dve.wait_ge(par_in, L * 32 + 32)
                nc.vector.tensor_copy(proj_r[0][:], proj_sb[:]).then_inc(proj_split, 1)
                dve.wait_ge(proj_split, L * 2 + 1)
                nc.vector.tensor_tensor(proj_r[1][:], proj_sb[:], proj_r[0][:].bitcast(f32),
                                        ALU.subtract).then_inc(proj_split, 1)
                dve.wait_ge(rows_in, L * 16 + 16)
                nc.vector.memset(V[:, :, :, 0:2 * DH + 2:2 * DH + 1], 1.0)
                for t in range(NT):
                    ps = job("v", t)
                    nc.vector.tensor_tensor(V[:, t, :, 1:1 + P], ps.rearrange("p (h d) -> p h d", d=P),
                                            rows_sb[:, 0, :].rearrange("p (h d) -> p h d", d=P), ALU.add).then_inc(v_empty, 1)
                    if t == 2:
                        for k in range(KT):
                            split_t(("n1", 1, k), hT, k, 1)

                def split_squares(n):
                    dve.wait_ge(sq_ready, L * len(QK_ORDER) + (n + 1))
                    nc.vector.tensor_copy(sq_hi[:, n % 2, :], sq[:, n % 2, :]).then_inc(sq_high, 1)
                    dve.wait_ge(sq_high, L * len(QK_ORDER) + (n + 1))
                    nc.vector.tensor_tensor(sq_lo[:, n % 2, :], sq[:, n % 2, :], sq_hi[:, n % 2, :].bitcast(f32),
                                            ALU.subtract).then_inc(sq_split, 1)

                def take_norms(quarter):
                    ps = job("norm", quarter)
                    nc.vector.tensor_scalar(norm_rows[:], ps[0:NH, :], -0.5 * DN * DN, None, ALU.mult).then_inc(v_empty, 1)

                def take_turned(quarter):
                    is_q, h = divmod(quarter, H)
                    ps = job("turned", quarter)
                    nc.vector.tensor_copy(ndiag[:, 1 - is_q, 4 * h:4 * h + 4, :],
                                          ps[:, 0:4 * NH].rearrange("p (t j) -> p t j", j=NH)).then_inc(v_empty, 1)

                def low_parts(n):
                    which, m, h = QK_ORDER[n]
                    i, dest = MIX_A[QK_ORDER[n]], qS if which == "q" else kS
                    column = 8 + 4 * (which == "k") + m
                    dve.wait_ge(hi_ready, L * len(QK_ORDER) + (n + 1))
                    for j in range(2):
                        head, other = (slice(DH * x, DH * (x + 1)) for x in (j, 1 - j))
                        last = nc.vector.scalar_tensor_tensor(out=dest[j][other, m, half(h)], in0=psA[head, i % BANKS, :],
                                                              scalar=col_sb[head, column:column + 1],
                                                              in1=dest[j][head, m, half(h)].bitcast(f32),
                                                              op0=ALU.add, op1=ALU.subtract)
                    last.then_inc(a_empty, 1)

                def ddk(pair):
                    for s in range(NT // 2):
                        for j in range(2):
                            ps = job("ddk", pair, s, j)
                            nc.vector.tensor_scalar(expk[:, j, 2 * s:2 * s + 2, :],
                                                    ps.rearrange("p (t m) -> p t m", m=M), 1.0, -3.0e38, ALU.mult, ALU.max,
                                                    accum_out=kmax[:, pair, j, s:s + 1]).then_inc(v_empty, 1)
                    dve.wait_ge(v_empty, v0 + done(MIX_V[("ddk", pair, NT // 2 - 1, 1)]))
                    nc.vector.tensor_reduce(kmax1[:, pair, :], kmax[:, pair, :, :], axis=AX.X,
                                            op=ALU.max).then_inc(kmax_ready, 1)

                def k_bias(pair):
                    dve.wait_ge(kall_ready, L * (NH // 2) + (pair + 1))
                    nc.vector.tensor_scalar(nkall[:, pair, :], kall[:, pair, :], -DN, None, ALU.mult).then_inc(nkall_done, 1)
                    dve.wait_ge(nkall_done, L * (NH // 2) + (pair + 1))
                    for j in range(2):
                        last = nc.vector.tensor_scalar(kbias[:, pair, j, :], ndiag[:, 1, :, 2 * pair + j],
                                                       nkall[:, pair, j:j + 1], None, ALU.add)
                    last.then_inc(kbias_ready, 1)

                for n in range(len(QK_ORDER)):
                    split_squares(n)
                    low_parts(n)
                    if n in (4, 8, 12):
                        take_norms(n // 4 - 1)
                    if n in (5, 13):
                        take_turned(n // 4 - 1)
                    if n == 8:
                        ddk(0)
                        take_turned(1)
                    if n == 9:
                        k_bias(0)
                take_norms(3)

                for what, g in attention_order():
                    pair, s = divmod(g, NT // 2)
                    if what == "ddk":
                        ddk(g)
                        continue
                    for j in range(2):
                        if what == "ctx":
                            ps = job("ctx", g, j)
                            nc.vector.tensor_copy(ctx_sb[:, g % 2, j, :, :],
                                                  ps[:, 0:MT * (DH + 1)].rearrange("p (m d) -> p m d", m=MT)).then_inc(v_empty, 1)
                        elif what == "ddq":
                            i = MIX_A[("ddq", g, j)]
                            dve.wait_ge(a_full, a0 + (i + 1))
                            nc.vector.tensor_reduce(qmax[:, g % 2, j, :], psA[:, i % BANKS, :].rearrange("p (t m) -> p t m", m=M),
                                                    axis=AX.X, op=ALU.max).then_inc(qmax_done, 1)
                            dve.wait_ge(qmax_done, L * 2 * STEPS + (2 * g + j + 1))
                            nc.vector.scalar_tensor_tensor(out=qbias[:, g % 4, j, :], in0=qmax[:, g % 2, j, :], scalar=-DN,
                                                           in1=ndiag[:, 0, 2 * s:2 * s + 2, 2 * pair + j], op0=ALU.mult,
                                                           op1=ALU.add).then_inc(qbias_ready, 1)
                        elif what == "tr":
                            ps = job("tr", g, j)
                            if g:
                                dve.wait_ge(v_full, v0 + (MIX_V[("at", g - 1, j)] + 1))
                            nc.vector.tensor_scalar(work[:, 2 + j, :], ps, EPS_K, None, ALU.add).then_inc(v_empty, 1)
                        else:
                            ps = job("at", g, j)[:, 0:2 * (DH + 1)].rearrange("p (t d) -> p t d", t=2)
                            nc.vector.reciprocal(rden[:, g % 2, j, :], ps[:, :, DH * j]).then_inc(rden_done, 1)
                            dve.wait_ge(rden_done, L * 2 * STEPS + (2 * g + j + 1))
                            nc.vector.tensor_tensor(V[:, 2 * s:2 * s + 2, pair, 1 + DH * j:1 + DH * (j + 1)], ps[:, :, 1 - j:1 - j + DH],
                                                    rden[:, g % 2, j, :].unsqueeze(2).to_broadcast([P, 2, DH]),
                                                    ALU.mult).then_inc(v_empty, 1)
                    if (what, g) == ("ctx", 0):
                        take_turned(3)
                    if what == "ddq" and s == 0 and pair + 1 < NH // 2:
                        k_bias(pair + 1)
                for h in range(H):
                    for k in range(KT):
                        split_t(("o", h, k), hT, k, h)

                def onto_residual(name, t):
                    ps = job(*name)
                    nc.vector.tensor_tensor(Xm[:, t, :], ps, Xm[:, t, :], ALU.add).then_inc(v_empty, 1)

                def final_residual(name, t, n):
                    onto_residual(name, t)
                    dve.wait_ge(v_empty, v0 + done(MIX_V[name]))
                    statistics(residual, [t])
                    if t % 4 == 3:
                        aggregate(half_tiles(t // 4), L * 4 + (n + t // 4 + 1))

                dve.wait_ge(bias_added, L * 2 * NT + (NT + 1))
                for t in range(NT):
                    final_residual(("wo", t), t, LN_MIX)
                    if t == 4:
                        normalise_half(residual, nat, normed, 0, L * 4, LN_MIX)
                    if t == NT - 3:
                        for name in F0_ORDER[:KT]:
                            split_t(name, hT, name[2], 0)
                normalise_half(residual, nat, normed, 1, L * 4, LN_MIX)
                for kind, c in FFN_ORDER:
                    if kind == "f":
                        for name in by_halves(("f", c)) if c else F0_ORDER[KT:]:
                            if name[0] == "n2":
                                split_t(name, hT, name[2], 1)
                            else:
                                split_t(name, fT[c % 2], *name[2:])
                    else:
                        if c:
                            dve.wait_ge(v_empty, v0 + done(MIX_V[("g", c - 1, NT - 1)]))
                        else:
                            dve.wait_ge(bias_added, L * 2 * NT + (2 * NT + 1))
                        for t in range(NT):
                            if c < FC - 1:
                                onto_residual(("g", c, t), t)
                                continue
                            final_residual(("g", c, t), t, LN_MIX + 2)
                            if t == 5:
                                normalise_half(residual, nat1, normed, 0, L * 4, LN_MIX + 2)

            with dve.Fori(0, LAYERS) as L:
                mix_layer(L)

            nc.vector.memset(zeros[:], 0.0).then_inc(zeros_ready, 1)
            dve.wait_ge(iota_in, 16)
            dve.wait_ge(bounds_ready, 1)
            dve.sem_inc(hot_ready, 2 * EG)
            dve.sem_inc(hot_used, 2 * EG + 2)

            def take_p(t, i, base, p_base):
                dve.wait_ge(v_full, base + (i + 1))
                hold(dve)
                nc.vector.tensor_copy(Pr[0][:, t, :], psV[:, i % BANKS, :]).then_inc(p_high, 1)
                dve.wait_ge(p_high, p_base)
                nc.vector.tensor_tensor(Pr[1][:, t, :], psV[:, i % BANKS, :], Pr[0][:, t, :].bitcast(f32),
                                        ALU.subtract).then_inc(v_empty, 1)

            def one_hots(b):
                first, end, base = group_bounds(dve, b)
                with dve.Fori(first, end) as c:
                    for u in range(2):
                        dve.wait_ge(hot_used, (c + base) * 2 + (u + 1))
                        for chunk in (2 * u, 2 * u + 1):
                            edge = c * GC + chunk
                            nc.vector.tensor_scalar(hot_dst[:, chunk, :], iota[:, bass.ts(b, P)],
                                                    ends_f[:, 1, bass.ds(edge, 1)], None, ALU.is_equal)
                            last = nc.vector.tensor_scalar(hot_src[:, chunk, :], iota[:],
                                                           ends_f[:, 0, bass.ds(edge, 1)], None, ALU.is_equal)
                        last.then_inc(hot_ready, 1)

            one_hots(0)
            for b in range(1, NT):
                one_hots(b)
                take_p(b - 1, GV + b - 1, 0, b)
            take_p(NT - 1, GV + NT - 1, 0, NT)
            dve.wait_ge(adj_copied, NT + 1)
            nc.vector.tensor_reduce(most_p[:], most_b[:].rearrange("p a b -> p (a b)"), axis=AX.X,
                                    op=ALU.max).then_inc(most_ready, 1)
            dve.wait_ge(most_all, 1)
            nc.vector.tensor_copy(most_i[:], most[:]).then_inc(most_loaded, 1)
            with dve.Fori(0, LAYERS) as L:
                def split_stage(stage_):
                    for h in range(H):
                        dve.wait_ge(a_full, L * 16 + (GA + 8 * stage_ + KT * (h + 1)))
                        for m in range(KT):
                            n = 8 * stage_ + KT * h + m
                            split_block(SP_G + n, L * 16, hT[0][:, m, half(h)], hT[1][:, m, half(h)],
                                        after=L * 16 + done(GA + n))

                split_stage(0)
                with dve.If(L < LAYERS - 1):
                    split_stage(1)
                    for t in range(NT):
                        take_p(t, GV + NT + t, L * NT, L * NT + (NT + t + 1))

            def split_experts_input(h):
                for k in range(KT):
                    n = h * KT + k
                    split_block(SP_M + n, 0, hT[0][:, k, half(h)], hT[1][:, k, half(h)], after=done(MA_T[h] + k))

            dve.wait_ge(w_split, N_SLOTS * PIECES)
            dve.wait_ge(lin_row_in, 16)
            for n, w in enumerate((Whi, Wlo)):
                last = nc.vector.tensor_copy(router_r[:, :, n * EXP:(n + 1) * EXP],
                                             w[:, GNN_SLOTS - 1, 2, 0:KT * EXP].rearrange("p (k n) -> p k n", k=KT).bitcast(f32))
            last.then_inc(router_ready, 1)
            nc.vector.memset(hot[:], 0.0)
            for t in range(NT):
                i = GV_X + t
                dve.wait_ge(v_full, i + 1)
                nc.vector.tensor_tensor(lin_sum[:, t % 2, :], psV[:, i % BANKS, :], lin_row[:], ALU.add).then_inc(v_empty, 1)
                dve.wait_ge(v_empty, done(i))
                nc.vector.scalar_tensor_tensor(out=Xm[:, t, :], in0=lin_sum[:, t % 2, :], scalar=0.0, in1=Xm[:, t, :],
                                               op0=ALU.max, op1=ALU.add).then_inc(relu_done, 1)
                dve.wait_ge(relu_done, t + 1)
                statistics(residual, [t])
                if t % 4 == 3:
                    aggregate(half_tiles(t // 4), LN_M + t // 4 + 1)
                if t == 4:
                    normalise_half(residual, Xf, normed, 0, 0, LN_M)
                if t == NT - 3:
                    split_experts_input(0)
            normalise_half(residual, Xf, normed, 1, 0, LN_M)
            split_experts_input(1)

            def expert_job(*name):
                i = MV + EXPERT_V[name if len(name) > 1 else name[0]]
                dve.wait_ge(v_full, i + 1)
                return psV[:, i % BANKS, :]


            ps = expert_job("logits")
            nc.vector.tensor_copy(logit2[:], ps[:, 0:NT * 2 * EXP].rearrange("p (t e) -> p t e", e=2 * EXP)).then_inc(v_empty, 1)
            expert_done(dve, "logits")
            then(nc.vector.tensor_tensor(logit[:], logit2[:, :, 0:EXP], logit2[:, :, EXP:], ALU.add))
            for t in range(NT):
                last = nc.vector.max(best[:, t, :], logit[:, t, :])
            then(last)
            nc.vector.tensor_tensor(gate[:, 0, :], best[:, :, 1], best[:, :, 0], ALU.subtract).then_inc(gate_in, 1)
            for t in range(NT):
                last = nc.vector.max_index(besti[:, t, :], best[:, t, :], logit[:, t, :])
            then(last)
            then(nc.vector.tensor_copy(bestf[:], besti[:]))
            for q in range(2):
                nc.vector.tensor_tensor(hot[:, :, SET * q:SET * q + 2 * EXP],
                                        iota8[:].unsqueeze(1).to_broadcast([P, NT, 2 * EXP]),
                                        bestf[:, :, q:q + 1].to_broadcast([P, NT, 2 * EXP]), ALU.is_equal)
            dve.wait_ge(gate_exp, 1)
            then(nc.vector.tensor_scalar(gate[:, 2, :], gate[:, 1, :], 1.0, None, ALU.add))
            then(nc.vector.reciprocal(gate[:, 2, :], gate[:, 2, :]))
            then(nc.vector.tensor_tensor(gate[:, 3, :], gate[:, 1, :], gate[:, 2, :], ALU.mult))
            for q in range(2):
                last = nc.vector.tensor_tensor(gated[:, q, :, :], hot[:, :, SET * q:SET * q + EXP],
                                               gate[:, 2 + q, :].unsqueeze(2).to_broadcast([P, NT, EXP]), ALU.mult)
            then(last)
            then(nc.vector.tensor_tensor(gated[:, 0, :, :], gated[:, 0, :, :], gated[:, 1, :, :], ALU.add))
            then(nc.vector.tensor_copy(gated_hi[:], gated[:, 0, :, :]))
            for n in range(2):
                nc.vector.tensor_copy(hot[:, :, 2 * SET + n * EXP:2 * SET + (n + 1) * EXP], gated_hi[:].bitcast(f32))
            nc.vector.tensor_tensor(hot[:, :, 2 * SET + 2 * EXP:2 * SET + 3 * EXP], gated[:, 0, :, :],
                                    gated_hi[:].bitcast(f32), ALU.subtract).then_inc(hots_ready, 1)
            for h in range(H):
                ps = expert_job("hot", h)
                nc.vector.tensor_copy(hotT[:, half(h)], ps[0:3 * SET, :]).then_inc(v_empty, 1)
            for h in range(H):
                dve.wait_ge(a_empty, done(MA_H[h] + 1))
                for q in range(2):
                    for m in range(2):
                        ps = expert_job("mask", q, m, h)
                        nc.vector.tensor_tensor(hm[q][:, m, half(h)], ps, h1[:, m, half(h)], ALU.mult).then_inc(v_empty, 1)
            for what, *which in expert_order():
                t = which[-1]
                if what == "gamma" and t % 4 == 0 and which[0] == 0:
                    h = t // 4
                    dve.wait_ge(rstd_ready, LN_Y + h + 1)
                    columns = slice(NT * h, NT * (h + 1))
                    then(nc.vector.tensor_tensor(gscale[:, columns].rearrange("p (t q) -> p t q", q=2),
                                                 rstd[:, columns].rearrange("p (t q) -> p t q", q=2),
                                                 gate[:, 2:4, 4 * h:4 * h + 4].rearrange("p q t -> p t q"), ALU.mult))
                    nc.vector.scalar_tensor_tensor(out=gshift[:, columns], in0=mv[:, columns, 0], scalar=-1.0,
                                                   in1=gscale[:, columns], op0=ALU.mult,
                                                   op1=ALU.mult).then_inc(scale_ready, 1)
                ps = expert_job(what, *which)
                if what == "z":
                    q = which[0]
                    nc.vector.tensor_tensor(zz[q][:, t, :], ps, Xf[:, t, :], ALU.add).then_inc(v_empty, 1)
                    if q == 1:
                        expert_done(dve, "z", 1, t)
                        statistics(lambda c: zz[c % 2][:, t, :], range(2 * t, 2 * t + 2), NT)
                        if t % 4 == 3:
                            columns = range(NT * (t // 4), NT * (t // 4 + 1))
                            aggregate(columns, LN_Y + t // 4 + 1)
                elif what == "gamma":
                    q = which[0]
                    dve.wait_ge(shifted, 2 * t + q + 1)
                    if t >= 2 and q == 0:
                        dve.wait_ge(summed, t - 1)
                    nc.vector.tensor_tensor(weighted[t % 2][:, q, :], ps, ut[t % 2][:, q, :], ALU.mult).then_inc(v_empty, 1)
                else:
                    nc.vector.tensor_tensor(Xm[:, t, :], ps, Xm[:, t, :], ALU.add).then_inc(v_empty, 1)


def kernel(**inputs):
    import numpy as np
    import concourse.bacc as bacc
    from concourse.bass_utils import run_bass_kernel_spmd

    a = {k: np.asarray(v) for k, v in inputs.items()}
    g = lambda k: a["L0_gnn_" + k]
    m = lambda k: a["L0_mix_" + k]
    e = lambda k: a["L0_ffn_" + k]

    def slot(w):
        return w.reshape(PIECES, 2, P, 512).transpose(0, 2, 1, 3).reshape(PIECES, P, 1024)

    def columns(v):
        return v.reshape(-1, P).T

    slots = []
    for l in range(LAYERS):
        slots += [slot(m(n)[l]) for n in ("Wq", "Wv", "Wk", "Wo")]
        for kind, c in FFN_ORDER:
            piece = slice(512 * c, 512 * (c + 1))
            slots.append(slot(m("W1")[l][:, piece] if kind == "f" else m("W2")[l][piece, :]))
    w1 = e("w1").transpose(1, 0, 2).reshape(KT, P, EXP * EF).transpose(1, 0, 2).reshape(P, 1024)
    router = np.zeros((P, 1024), np.float32)
    router[:, :KT * EXP] = e("router_w").reshape(KT, P, EXP).transpose(1, 0, 2).reshape(P, KT * EXP)
    experts = np.stack([w1, router])
    for l in "12":
        slots += [slot(g(n + l).T) for n in ("W_rel", "W_root", "W_lin")] + [experts]
    hidden = np.arange(2 * P)
    small = np.zeros((3, SET // EXP, EXP, 2, D), np.float32)
    small[:2, :2] = np.stack([e("b2"), e("gamma")], axis=1)
    small[2, :3, :, 0] = e("beta")
    small = small.reshape(3 * SET, 2, D)
    data = {
        "x": a["x"],
        "ends_c": np.stack([a[n].reshape(EC, P).T for n in ("src", "dst")], axis=1),
        "wstream": np.stack(slots),
        "cols": np.stack([np.concatenate([columns(m(n)[l]) for n in ("ln1_s", "ln1_b", "bq", "bk", "ln2_s", "ln2_b", "b1")],
                                         axis=1) for l in range(LAYERS)]),
        "rows": np.stack([np.stack([m(n)[l] for n in ("bv", "b2", "bo")]) for l in range(LAYERS)]),
        "projt": np.stack([np.concatenate([m("proj")[l].T] * 2) for l in range(LAYERS)]),
        "gcols": np.concatenate([columns(g(n)) for n in ("b_rel1", "b_lin1", "b_rel2", "b_lin2")], axis=1),
        "b1col": columns(e("b1").reshape(-1)),
        "small": small,
        "lin_row_c": g("b_lin2"),
        "high_c": np.tile(np.repeat([[1, 0], [0, 1], [1, 0], [1, 0]], EXP, axis=0), (3, 1)).astype(np.float32),
        "w2": e("w2").reshape(2, P, D).transpose(1, 0, 2),
        "ident_c": np.eye(P, dtype=np.float32),
        "headmask_c": (2 * np.arange(KT)[:, None] + np.arange(P)[:, None, None] // DH == np.arange(NH)).astype(np.float32),
        "repl_c": (hidden // EF == np.arange(2 * SET)[:, None] % SET).astype(np.float32),
        "iota_c": np.arange(N, dtype=np.float16),
        "group_c": np.stack([np.arange(EC) // GC + 1, EG - np.arange(EC) // GC]).astype(np.float32),
        "iota8_c": np.tile(np.arange(EXP, dtype=np.float32), (P, 2)),
    }
    nc = bacc.Bacc("TRN2", target_bir_lowering=False, num_devices=1)
    data = {n: np.ascontiguousarray(v) for n, v in data.items()}
    aps = {n: nc.dram_tensor(n, v.shape, mybir.dt.from_np(v.dtype), kind="ExternalInput").ap() for n, v in data.items()}
    out = nc.dram_tensor("out", (N, D), f32, kind="ExternalOutput").ap()
    xt_d = nc.dram_tensor("xt_d", (2, P, KT, N), f32, kind="Internal").ap()
    build(nc, xt_d=xt_d, out=out, **aps)
    r = run_bass_kernel_spmd(nc, [data], core_ids=[0])
    return r.results[0]["out"]
```
